# Optimizing a Trainium2 kernel written in Bass

```python
import numpy as np
import jax
import jax.numpy as jnp

def _softmax(x, axis=-1):
    return jax.nn.softmax(x, axis=axis)

def _gelu(x):
    return jax.nn.gelu(x, approximate=True)

def _silu(x):
    return jax.nn.silu(x)

def _sigmoid(x):
    return jax.nn.sigmoid(x)

def _layernorm(x, axis=-1, eps=1e-05):
    m = jnp.mean(x, axis=axis, keepdims=True)
    v = jnp.var(x, axis=axis, keepdims=True)
    return (x - m) / jnp.sqrt(v + eps)

def _scatter_add(tgt, idx, src, axis=0):
    return tgt.at[idx].add(src)

def _segment_sum(src, seg, n):
    return jax.ops.segment_sum(src, seg, n)
kernel_name = 'mk_gnn_resnorm_d4_gnn_r32_33bad8'

def setup_inputs(seed: int=0):
    np.random.seed(seed)
    _w = jnp.asarray

    def _rec_inputs():
        import jax
        import jax.numpy as jnp
        _gk = jax.random.key(seed)
        x = -0.0003713 + 1 * jax.random.normal(jax.random.fold_in(_gk, 1), (3125, 256), jnp.float32)
        _s = jax.random.randint(jax.random.fold_in(_gk, 2), (25000,), 0, 3125, jnp.int32)
        _d = jax.random.randint(jax.random.fold_in(_gk, 3), (25000,), 0, 3125, jnp.int32)
        _loop = jnp.arange(3125, dtype=jnp.int32)
        src = jnp.concatenate([_s, _d, _loop])
        dst = jnp.concatenate([_d, _s, _loop])
        _o = jnp.argsort(dst, stable=True)
        src = src[_o]
        dst = dst[_o]
        edge_attr_16 = -0.000153872 + 1.00011 * jax.random.normal(jax.random.fold_in(_gk, 12), (53125, 16), jnp.float32)
        edge_attr_4 = 0.0007022 + 0.999661 * jax.random.normal(jax.random.fold_in(_gk, 13), (53125, 4), jnp.float32)
        edge_attr_64 = -5.3897e-05 + 0.999841 * jax.random.normal(jax.random.fold_in(_gk, 14), (53125, 64), jnp.float32)
        return (x, src, dst, edge_attr_16, edge_attr_4, edge_attr_64)
    x, src, dst, edge_attr_16, edge_attr_4, edge_attr_64 = _rec_inputs()

    def _L0_gnn_setup():
        import jax, jax.numpy as jnp
        import numpy as np
        N_NODES = 50000
        N_EDGES = 12500
        D_NODE = 256
        D_EDGE = 64
        LN_EPS = 1e-06

        def _layer_norm(x, scale, bias):
            mu = jnp.mean(x, axis=-1, keepdims=True)
            var = jnp.mean(jnp.square(x - mu), axis=-1, keepdims=True)
            return (x - mu) * jax.lax.rsqrt(var + LN_EPS) * scale + bias

        def _glorot(key, shape):
            fan_in, fan_out = shape
            std = jnp.sqrt(2.0 / (fan_in + fan_out))
            return std * jax.random.normal(key, shape, dtype=jnp.float32)

        def _relu_mlp_skip(x, Ws, bs):
            n = len(Ws)
            for i, (W, b) in enumerate(zip(Ws, bs)):
                y = x @ W + b
                if i < n - 1:
                    y = jax.nn.relu(y)
                x = x + y if y.shape[-1] == x.shape[-1] else y
            return x
        key = jax.random.key(seed)
        ks = jax.random.split(key, 10)
        inp = {'nodes': jax.random.normal(ks[0], (N_NODES, D_NODE), dtype=jnp.float32), 'edges': jax.random.normal(ks[1], (N_EDGES, D_EDGE), dtype=jnp.float32), 'senders': jax.random.randint(ks[2], (N_EDGES,), 0, N_NODES, dtype=jnp.int32), 'receivers': jax.random.randint(ks[3], (N_EDGES,), 0, N_NODES, dtype=jnp.int32), 'W_message': _glorot(ks[4], (D_NODE + D_EDGE, D_NODE)), 'mlp_W0': _glorot(ks[5], (D_NODE, D_NODE)), 'mlp_b0': jnp.zeros((D_NODE,), jnp.float32), 'mlp_W1': _glorot(ks[6], (D_NODE, D_NODE)), 'mlp_b1': jnp.zeros((D_NODE,), jnp.float32), 'mlp_W2': _glorot(ks[7], (D_NODE, D_NODE)), 'mlp_b2': jnp.zeros((D_NODE,), jnp.float32), 'ln_aggr_scale': jnp.ones((D_NODE,), jnp.float32), 'ln_aggr_bias': jnp.zeros((D_NODE,), jnp.float32), 'ln_out_scale': jnp.ones((D_NODE,), jnp.float32), 'ln_out_bias': jnp.zeros((D_NODE,), jnp.float32)}
        return inp
    _L0_gnn_all = _L0_gnn_setup()
    _L0_gnn_in = {k: v for k, v in _L0_gnn_all.items() if k in ('W_message', 'mlp_W0', 'mlp_b0', 'mlp_W1', 'mlp_b1', 'mlp_W2', 'mlp_b2', 'ln_aggr_scale', 'ln_aggr_bias', 'ln_out_scale', 'ln_out_bias')}
    del _L0_gnn_all

    def _L1_gnn_setup():
        import jax, jax.numpy as jnp
        import numpy as np
        N = 50000
        E = 12500
        IN = 256
        HID = 128
        HEADS = 4
        OUT = 256
        NEG = 0.2

        def _glorot(key, shape, fan_in):
            return jax.random.normal(key, shape, jnp.float32) * (1.0 / np.sqrt(fan_in))

        def gatv2_conv(x, src, dst, Wl, Wr, att, bias, heads, ch, concat):
            n = x.shape[0]
            xl = (x @ Wl).reshape(n, heads, ch)
            xr = (x @ Wr).reshape(n, heads, ch)
            g = xl[src] + xr[dst]
            e = jnp.einsum('ehc,hc->eh', jax.nn.leaky_relu(g, NEG), att)
            e_max = jax.ops.segment_max(e, dst, num_segments=n)
            p = jnp.exp(e - e_max[dst])
            denom = jax.ops.segment_sum(p, dst, num_segments=n)
            alpha = p / denom[dst]
            out = jax.ops.segment_sum(alpha[:, :, None] * xl[src], dst, num_segments=n)
            out = out.reshape(n, heads * ch) if concat else out.mean(axis=1)
            return out + bias
        key = jax.random.key(seed)
        ks = jax.random.split(key, 8)
        x = jax.random.normal(ks[0], (N, IN), jnp.float32)
        edge_index = jax.random.randint(ks[1], (2, E), 0, N, dtype=jnp.int64)
        W1l = _glorot(ks[2], (IN, HEADS * HID), IN)
        W1r = _glorot(ks[3], (IN, HEADS * HID), IN)
        a1 = _glorot(ks[4], (HEADS, HID), HID)
        b1 = jnp.zeros((HEADS * HID,), jnp.float32)
        W2l = _glorot(ks[5], (HEADS * HID, OUT), HEADS * HID)
        W2r = _glorot(ks[6], (HEADS * HID, OUT), HEADS * HID)
        a2 = _glorot(ks[7], (1, OUT), OUT)
        b2 = jnp.zeros((OUT,), jnp.float32)
        return dict(x=x, edge_index=edge_index, W1l=W1l, W1r=W1r, a1=a1, b1=b1, W2l=W2l, W2r=W2r, a2=a2, b2=b2)
    _L1_gnn_all = _L1_gnn_setup()
    _L1_gnn_in = {k: v for k, v in _L1_gnn_all.items() if k in ('W1l', 'W1r', 'a1', 'b1', 'W2l', 'W2r', 'a2', 'b2')}
    del _L1_gnn_all

    def _L2_gnn_setup():
        import jax, jax.numpy as jnp
        import numpy as np
        N = 50000
        E = 25000
        HIDDEN = 256
        HEADS = 8
        HEAD_DIM = HIDDEN // HEADS

        def _linear_params(key, fan_in, fan_out):
            k1, k2 = jax.random.split(key)
            s = 1.0 / np.sqrt(fan_in)
            W = jax.random.uniform(k1, (fan_in, fan_out), jnp.float32, -s, s)
            b = jax.random.uniform(k2, (fan_out,), jnp.float32, -s, s)
            return (W, b)
        key = jax.random.key(seed)
        ks = jax.random.split(key, 7)
        h = jax.random.normal(ks[0], (N, HIDDEN), jnp.float32)
        row = jnp.sort(jax.random.randint(ks[1], (E,), 0, N))
        col = jax.random.randint(ks[2], (E,), 0, N)
        Wq, bq = _linear_params(ks[3], HIDDEN, HIDDEN)
        Wk, bk = _linear_params(ks[4], HIDDEN, HIDDEN)
        Wv, bv = _linear_params(ks[5], HIDDEN, HIDDEN)
        Wo, bo = _linear_params(ks[6], HIDDEN, HIDDEN)
        return dict(h=h, row=row, col=col, Wq=Wq, bq=bq, Wk=Wk, bk=bk, Wv=Wv, bv=bv, Wo=Wo, bo=bo)
    _L2_gnn_all = _L2_gnn_setup()
    _L2_gnn_in = {k: v for k, v in _L2_gnn_all.items() if k in ('Wq', 'bq', 'Wk', 'bk', 'Wv', 'bv', 'Wo', 'bo')}
    del _L2_gnn_all

    def _L3_gnn_setup():
        import jax, jax.numpy as jnp
        import numpy as np
        N, E, C, R, HID = (50000, 15625, 64, 16, 64)
        key = jax.random.key(seed)
        ks = jax.random.split(key, 24)
        g = lambda k, shape, s=1.0: jax.random.normal(k, shape, dtype=jnp.float32) * s
        cs = C ** (-0.5)
        inp = {'h': g(ks[0], (N, 4 * C)), 'edge_index': jax.random.randint(ks[1], (2, E), 0, N), 'edge_sh': g(ks[2], (E, 4)), 'edge_rbf': g(ks[3], (E, R)), 'W_up0': g(ks[4], (C, C), cs), 'W_up1': g(ks[5], (C, C), cs), 'M1': g(ks[6], (R, HID), R ** (-0.5)), 'M2': g(ks[7], (HID, HID), HID ** (-0.5)), 'M3': g(ks[8], (HID, HID), HID ** (-0.5)), 'M4': g(ks[9], (HID, 4 * C), HID ** (-0.5)), 'W_lin0': g(ks[10], (C, C), cs), 'W_lin1': g(ks[11], (C, C), cs), 'Wsc0': g(ks[12], (C, C), cs), 'Wsc1': g(ks[13], (C, C), cs), 'Wc0': g(ks[14], (C, 5)), 'Wc1': g(ks[15], (C, 4)), 'WB0': g(ks[16], (C, C), cs), 'WB1': g(ks[17], (C, C), cs), 'gamma0': jnp.ones((C,), jnp.float32), 'beta0': jnp.zeros((C,), jnp.float32), 'gamma1': jnp.ones((C,), jnp.float32)}
        return inp
    _L3_gnn_all = _L3_gnn_setup()
    _L3_gnn_in = {k: v for k, v in _L3_gnn_all.items() if k in ('W_up0', 'W_up1', 'M1', 'M2', 'M3', 'M4', 'W_lin0', 'W_lin1', 'Wsc0', 'Wsc1', 'Wc0', 'Wc1', 'WB0', 'WB1', 'gamma0', 'beta0', 'gamma1')}
    del _L3_gnn_all
    return {'x': x, 'src': src, 'dst': dst, 'edge_attr_16': edge_attr_16, 'edge_attr_4': edge_attr_4, 'edge_attr_64': edge_attr_64, 'L0_gnn_W_message': _L0_gnn_in['W_message'], 'L0_gnn_mlp_W0': _L0_gnn_in['mlp_W0'], 'L0_gnn_mlp_b0': _L0_gnn_in['mlp_b0'], 'L0_gnn_mlp_W1': _L0_gnn_in['mlp_W1'], 'L0_gnn_mlp_b1': _L0_gnn_in['mlp_b1'], 'L0_gnn_mlp_W2': _L0_gnn_in['mlp_W2'], 'L0_gnn_mlp_b2': _L0_gnn_in['mlp_b2'], 'L0_gnn_ln_aggr_scale': _L0_gnn_in['ln_aggr_scale'], 'L0_gnn_ln_aggr_bias': _L0_gnn_in['ln_aggr_bias'], 'L0_gnn_ln_out_scale': _L0_gnn_in['ln_out_scale'], 'L0_gnn_ln_out_bias': _L0_gnn_in['ln_out_bias'], 'L1_gnn_W1l': _L1_gnn_in['W1l'], 'L1_gnn_W1r': _L1_gnn_in['W1r'], 'L1_gnn_a1': _L1_gnn_in['a1'], 'L1_gnn_b1': _L1_gnn_in['b1'], 'L1_gnn_W2l': _L1_gnn_in['W2l'], 'L1_gnn_W2r': _L1_gnn_in['W2r'], 'L1_gnn_a2': _L1_gnn_in['a2'], 'L1_gnn_b2': _L1_gnn_in['b2'], 'L2_gnn_Wq': _L2_gnn_in['Wq'], 'L2_gnn_bq': _L2_gnn_in['bq'], 'L2_gnn_Wk': _L2_gnn_in['Wk'], 'L2_gnn_bk': _L2_gnn_in['bk'], 'L2_gnn_Wv': _L2_gnn_in['Wv'], 'L2_gnn_bv': _L2_gnn_in['bv'], 'L2_gnn_Wo': _L2_gnn_in['Wo'], 'L2_gnn_bo': _L2_gnn_in['bo'], 'L3_gnn_W_up0': _L3_gnn_in['W_up0'], 'L3_gnn_W_up1': _L3_gnn_in['W_up1'], 'L3_gnn_M1': _L3_gnn_in['M1'], 'L3_gnn_M2': _L3_gnn_in['M2'], 'L3_gnn_M3': _L3_gnn_in['M3'], 'L3_gnn_M4': _L3_gnn_in['M4'], 'L3_gnn_W_lin0': _L3_gnn_in['W_lin0'], 'L3_gnn_W_lin1': _L3_gnn_in['W_lin1'], 'L3_gnn_Wsc0': _L3_gnn_in['Wsc0'], 'L3_gnn_Wsc1': _L3_gnn_in['Wsc1'], 'L3_gnn_Wc0': _L3_gnn_in['Wc0'], 'L3_gnn_Wc1': _L3_gnn_in['Wc1'], 'L3_gnn_WB0': _L3_gnn_in['WB0'], 'L3_gnn_WB1': _L3_gnn_in['WB1'], 'L3_gnn_gamma0': _L3_gnn_in['gamma0'], 'L3_gnn_beta0': _L3_gnn_in['beta0'], 'L3_gnn_gamma1': _L3_gnn_in['gamma1']}

def reference(x, src, dst, edge_attr_16, edge_attr_4, edge_attr_64, L0_gnn_W_message, L0_gnn_mlp_W0, L0_gnn_mlp_b0, L0_gnn_mlp_W1, L0_gnn_mlp_b1, L0_gnn_mlp_W2, L0_gnn_mlp_b2, L0_gnn_ln_aggr_scale, L0_gnn_ln_aggr_bias, L0_gnn_ln_out_scale, L0_gnn_ln_out_bias, L1_gnn_W1l, L1_gnn_W1r, L1_gnn_a1, L1_gnn_b1, L1_gnn_W2l, L1_gnn_W2r, L1_gnn_a2, L1_gnn_b2, L2_gnn_Wq, L2_gnn_bq, L2_gnn_Wk, L2_gnn_bk, L2_gnn_Wv, L2_gnn_bv, L2_gnn_Wo, L2_gnn_bo, L3_gnn_W_up0, L3_gnn_W_up1, L3_gnn_M1, L3_gnn_M2, L3_gnn_M3, L3_gnn_M4, L3_gnn_W_lin0, L3_gnn_W_lin1, L3_gnn_Wsc0, L3_gnn_Wsc1, L3_gnn_Wc0, L3_gnn_Wc1, L3_gnn_WB0, L3_gnn_WB1, L3_gnn_gamma0, L3_gnn_beta0, L3_gnn_gamma1):
    import jax
    import jax.numpy as jnp

    def _L0_gnn_ref(nodes, edges, senders, receivers, W_message, mlp_W0, mlp_b0, mlp_W1, mlp_b1, mlp_W2, mlp_b2, ln_aggr_scale, ln_aggr_bias, ln_out_scale, ln_out_bias):
        import jax, jax.numpy as jnp
        import numpy as np
        N_NODES = 50000
        N_EDGES = 12500
        D_NODE = 256
        D_EDGE = 64
        LN_EPS = 1e-06

        def _layer_norm(x, scale, bias):
            mu = jnp.mean(x, axis=-1, keepdims=True)
            var = jnp.mean(jnp.square(x - mu), axis=-1, keepdims=True)
            return (x - mu) * jax.lax.rsqrt(var + LN_EPS) * scale + bias

        def _glorot(key, shape):
            fan_in, fan_out = shape
            std = jnp.sqrt(2.0 / (fan_in + fan_out))
            return std * jax.random.normal(key, shape, dtype=jnp.float32)

        def _relu_mlp_skip(x, Ws, bs):
            n = len(Ws)
            for i, (W, b) in enumerate(zip(Ws, bs)):
                y = x @ W + b
                if i < n - 1:
                    y = jax.nn.relu(y)
                x = x + y if y.shape[-1] == x.shape[-1] else y
            return x
        total_nodes = nodes.shape[0]
        sender_features = nodes[senders]
        msg_in = jnp.concatenate([sender_features, edges], axis=-1)
        messages = msg_in @ W_message
        agg = jax.ops.segment_sum(messages, receivers, num_segments=total_nodes)
        h = _layer_norm(jax.nn.relu(agg) + nodes, ln_aggr_scale, ln_aggr_bias)
        nodes_out = _relu_mlp_skip(h, [mlp_W0, mlp_W1, mlp_W2], [mlp_b0, mlp_b1, mlp_b2])
        nodes_new = _layer_norm(nodes + nodes_out, ln_out_scale, ln_out_bias)
        return nodes_new

    def _L1_gnn_ref(x, edge_index, W1l, W1r, a1, b1, W2l, W2r, a2, b2):
        import jax, jax.numpy as jnp
        import numpy as np
        N = 50000
        E = 12500
        IN = 256
        HID = 128
        HEADS = 4
        OUT = 256
        NEG = 0.2

        def _glorot(key, shape, fan_in):
            return jax.random.normal(key, shape, jnp.float32) * (1.0 / np.sqrt(fan_in))

        def gatv2_conv(x, src, dst, Wl, Wr, att, bias, heads, ch, concat):
            n = x.shape[0]
            xl = (x @ Wl).reshape(n, heads, ch)
            xr = (x @ Wr).reshape(n, heads, ch)
            g = xl[src] + xr[dst]
            e = jnp.einsum('ehc,hc->eh', jax.nn.leaky_relu(g, NEG), att)
            e_max = jax.ops.segment_max(e, dst, num_segments=n)
            p = jnp.exp(e - e_max[dst])
            denom = jax.ops.segment_sum(p, dst, num_segments=n)
            alpha = p / denom[dst]
            out = jax.ops.segment_sum(alpha[:, :, None] * xl[src], dst, num_segments=n)
            out = out.reshape(n, heads * ch) if concat else out.mean(axis=1)
            return out + bias
        loop = jnp.arange(x.shape[0], dtype=edge_index.dtype)
        src = jnp.concatenate([edge_index[0], loop])
        dst = jnp.concatenate([edge_index[1], loop])
        h = jax.nn.relu(gatv2_conv(x, src, dst, W1l, W1r, a1, b1, HEADS, HID, True))
        return gatv2_conv(h, src, dst, W2l, W2r, a2, b2, 1, OUT, False)

    def _L2_gnn_ref(h, row, col, Wq, bq, Wk, bk, Wv, bv, Wo, bo):
        import jax, jax.numpy as jnp
        import numpy as np
        N = 50000
        E = 25000
        HIDDEN = 256
        HEADS = 8
        HEAD_DIM = HIDDEN // HEADS

        def _linear_params(key, fan_in, fan_out):
            k1, k2 = jax.random.split(key)
            s = 1.0 / np.sqrt(fan_in)
            W = jax.random.uniform(k1, (fan_in, fan_out), jnp.float32, -s, s)
            b = jax.random.uniform(k2, (fan_out,), jnp.float32, -s, s)
            return (W, b)
        n = h.shape[0]
        scaling = HEAD_DIM ** (-0.5)
        q = (h @ Wq + bq).reshape(n, HEADS, HEAD_DIM) * scaling
        k = (h @ Wk + bk).reshape(n, HEADS, HEAD_DIM)
        v = (h @ Wv + bv).reshape(n, HEADS, HEAD_DIM)
        s = jnp.einsum('ehd,ehd->eh', q[row], k[col])
        m = jax.ops.segment_max(s, row, num_segments=n)
        p = jnp.exp(s - m[row])
        denom = jax.ops.segment_sum(p, row, num_segments=n)
        attn = p / denom[row]
        out = jax.ops.segment_sum(attn[:, :, None] * v[col], row, num_segments=n)
        return out.reshape(n, HIDDEN) @ Wo + bo

    def _L3_gnn_ref(h, edge_index, edge_sh, edge_rbf, W_up0, W_up1, M1, M2, M3, M4, W_lin0, W_lin1, Wsc0, Wsc1, Wc0, Wc1, WB0, WB1, gamma0, beta0, gamma1):
        import jax, jax.numpy as jnp
        import numpy as np
        N, E, C, R, HID = (50000, 15625, 64, 16, 64)
        n = h.shape[0]
        h0 = h[:, :C]
        h1 = h[:, C:].reshape(n, C, 3)
        up0 = h0 @ W_up0
        up1 = jnp.einsum('ncx,cd->ndx', h1, W_up1)
        r = jax.nn.silu(edge_rbf @ M1)
        r = jax.nn.silu(r @ M2)
        r = jax.nn.silu(r @ M3)
        tpw = (r @ M4).reshape(-1, 4, C)
        snd, rcv = (edge_index[0], edge_index[1])
        x0 = up0[snd]
        x1 = up1[snd]
        sh0 = edge_sh[:, 0]
        sh1 = edge_sh[:, 1:]
        inv3 = 1.0 / jnp.sqrt(jnp.float32(3.0))
        m0e = tpw[:, 0] * x0 * sh0[:, None] + tpw[:, 3] * jnp.einsum('ecx,ex->ec', x1, sh1) * inv3
        m1e = tpw[:, 1][:, :, None] * x0[:, :, None] * sh1[:, None, :] + tpw[:, 2][:, :, None] * x1 * sh0[:, None, None]
        msg0 = jax.ops.segment_sum(m0e, rcv, num_segments=n)
        msg1 = jax.ops.segment_sum(m1e, rcv, num_segments=n)
        A0 = msg0 @ W_lin0
        A1 = jnp.einsum('ncx,cd->ndx', msg1, W_lin1)
        sc0 = h0 @ Wsc0
        sc1 = jnp.einsum('ncx,cd->ndx', h1, Wsc1)
        vv = jnp.sum(A1 * A1, -1)
        B0 = Wc0[:, 0] * A0 + Wc0[:, 1] * A0 * A0 + Wc0[:, 2] * vv + Wc0[:, 3] * A0 ** 3 + Wc0[:, 4] * A0 * vv
        B1 = (Wc1[:, 0] + Wc1[:, 1] * A0 + Wc1[:, 2] * A0 * A0 + Wc1[:, 3] * vv)[..., None] * A1
        o0 = B0 @ WB0 + sc0
        o1 = jnp.einsum('ncx,cd->ndx', B1, WB1) + sc1
        eps = jnp.float32(1e-05)
        mu = jnp.mean(o0, 0)
        xc = o0 - mu
        var = jnp.mean(xc * xc, 0)
        n0 = xc * jax.lax.rsqrt(var + eps) * gamma0 + beta0
        nrm1 = jnp.mean(jnp.sum(o1 * o1, -1) / 3.0, 0)
        n1 = o1 * (jax.lax.rsqrt(nrm1 + eps) * gamma1)[None, :, None]
        return jnp.concatenate([n0, n1.reshape(n, 3 * C)], -1)
    edge_index = jnp.stack([src, dst])
    x = _layernorm(x + _L0_gnn_ref(x, edge_attr_64, src, dst, L0_gnn_W_message, L0_gnn_mlp_W0, L0_gnn_mlp_b0, L0_gnn_mlp_W1, L0_gnn_mlp_b1, L0_gnn_mlp_W2, L0_gnn_mlp_b2, L0_gnn_ln_aggr_scale, L0_gnn_ln_aggr_bias, L0_gnn_ln_out_scale, L0_gnn_ln_out_bias), axis=-1)
    x = _layernorm(x + _L1_gnn_ref(x, edge_index, L1_gnn_W1l, L1_gnn_W1r, L1_gnn_a1, L1_gnn_b1, L1_gnn_W2l, L1_gnn_W2r, L1_gnn_a2, L1_gnn_b2), axis=-1)
    x = _layernorm(x + _L2_gnn_ref(x, src, dst, L2_gnn_Wq, L2_gnn_bq, L2_gnn_Wk, L2_gnn_bk, L2_gnn_Wv, L2_gnn_bv, L2_gnn_Wo, L2_gnn_bo), axis=-1)
    x = _layernorm(x + _L3_gnn_ref(x, edge_index, edge_attr_4, edge_attr_16, L3_gnn_W_up0, L3_gnn_W_up1, L3_gnn_M1, L3_gnn_M2, L3_gnn_M3, L3_gnn_M4, L3_gnn_W_lin0, L3_gnn_W_lin1, L3_gnn_Wsc0, L3_gnn_Wsc1, L3_gnn_Wc0, L3_gnn_Wc1, L3_gnn_WB0, L3_gnn_WB1, L3_gnn_gamma0, L3_gnn_beta0, L3_gnn_gamma1), axis=-1)
    return x

_drawn_inputs = setup_inputs


def setup_inputs(seed=0):
    import zlib

    import numpy as np

    out = dict(_drawn_inputs(seed))
    spreads = {'L0_gnn_mlp_b0': (0.0, 0.1),
     'L0_gnn_mlp_b1': (0.0, 0.29),
     'L0_gnn_mlp_b2': (0.0, 0.292),
     'L0_gnn_ln_aggr_scale': (1.0, 0.2),
     'L0_gnn_ln_aggr_bias': (0.0, 0.1),
     'L0_gnn_ln_out_scale': (1.0, 0.2),
     'L0_gnn_ln_out_bias': (0.0, 0.1),
     'L1_gnn_b1': (0.0, 0.1),
     'L1_gnn_b2': (0.0, 0.1),
     'L3_gnn_gamma0': (1.0, 0.2),
     'L3_gnn_beta0': (0.0, 0.1),
     'L3_gnn_gamma1': (1.0, 0.2)}
    factors = {'L1_gnn_W1r': 4.231,
     'L1_gnn_W2r': 8.0,
     'L1_gnn_a2': 8.0,
     'L2_gnn_bq': 31.84,
     'L2_gnn_bk': 64.0}
    for name, (base, spread) in spreads.items():
        noise = np.random.default_rng([zlib.crc32(name.encode()), seed]).standard_normal(out[name].shape)
        drawn = base * np.exp(spread * noise) if base else spread * noise
        out[name] = jnp.asarray(drawn.astype(out[name].dtype))
    for name, factor in factors.items():
        out[name] = (out[name] * factor).astype(out[name].dtype)
    return out
```

```python
from contextlib import ExitStack

import numpy as np

import concourse.bass as bass
from concourse import mybir

ALU = mybir.AluOpType
ACT = mybir.ActivationFunctionType
AX = mybir.AxisListType
F32 = mybir.dt.float32
I32 = mybir.dt.int32

P = 128
N_NODES = 3125
N_EDGES = 53125
D = 256
D_EA64, D_EA16 = 64, 16
WN = -(-N_NODES // P)
CW = 5
CHUNKS = WN // CW
NP = WN * P
WX = WN + 1
J = 4
GE = P * J
NG = -(-N_EDGES // GE)
EP = NG * GE
KC = -(-(NG * WX + 3) // P)
KMAX = KC * P
BIG = 1e30
SLOPE = 0.2
C3 = 64
assert WN % CW == 0


class Model:

    def __init__(self, inputs):
        self.inputs = inputs


class Order:

    def __init__(self, dram, name, key, other):
        self.key, self.other = key, other
        self.key_f = dram(name + "_key_f", (EP,))
        self.gk_d, self.wk_d = dram(name + "_group", (KMAX,), I32), dram(name + "_window", (KMAX,), I32)


class State:

    def __init__(self, total, weight, top):
        self.total, self.weight, self.top = total, weight, top


class Stages:

    def __init__(self, sem, names):
        self.sem, self.names = sem, list(names)
        self.n = len(self.names)
        self.start = 2 * self.n

    def at(self, name, step):
        return (step + 2) * self.n + self.names.index(name) + 1


def settle(eng):
    eng.nop(nofuse=True)


def column(v):
    return v.rearrange("(p a) -> p a", a=1)


def row_everywhere(v):
    return v.rearrange("(a n) -> a n", a=1).broadcast_to([P, v.shape[-1]])


def build_steps(nc, m, o, tag):
    with ExitStack() as ctx:
        sb = lambda n, s, d=F32: ctx.enter_context(nc.sbuf_tensor(tag + n, s, d))
        sem = lambda n: ctx.enter_context(nc.semaphore(tag + n))
        dst_rows = sb("st_dst_rows", [NG, GE], I32)
        dst_i = sb("st_dst_i", [P, EP // P], I32)
        dst_f = sb("st_dst_f", [P, EP // P])
        lim_f = sb("st_lim_f", [NG, 2])
        lim_i = sb("st_lim_i", [NG, 2], I32)
        win_i = sb("st_win_i", [NG, 2], I32)
        win = sb("st_win", [NG, 2])
        count = sb("st_count", [NG, 1])
        count_b = sb("st_count_b", [NG, P])
        wmin_b = sb("st_wmin_b", [NG, P])
        below = sb("st_below", [NG, NG + 1])
        start = sb("st_start", [P, NG + 1])
        delta = sb("st_delta", [P, NG])
        delta_step = sb("st_delta_step", [P, NG])
        k_i = sb("st_k_i", [P, KC], I32)
        k_f = sb("st_k_f", [P, KC])
        le = sb("st_le", [P, KC, NG])
        gk = sb("st_gk", [P, KC])
        wk = sb("st_wk", [P, KC])
        gk_i = sb("st_gk_i", [P, KC], I32)
        wk_i = sb("st_wk_i", [P, KC], I32)
        half_f = sb("st_half_f", [1, 1])
        half_i = sb("st_half_i", [1, 1], I32)
        ps = ctx.enter_context(nc.psum_tensor(tag + "st_ps", [P, 512], F32))
        loaded, stored, listed = sem("st_loaded"), sem("st_stored"), sem("st_listed")
        pool_done, dve_done, pe_done = sem("st_pool"), sem("st_dve"), sem("st_pe")
        block = ctx.enter_context(nc.Block())

        @block.sync
        def _(sp):
            sp.dma_start(dst_rows[:, :], o.key.rearrange("(g e) -> g e", e=GE)).then_inc(loaded, 16)
            sp.dma_start(dst_i[:, :], o.key.rearrange("(p c) -> p c", p=P)).then_inc(loaded, 16)
            sp.wait_ge(dve_done, 1)
            sp.dma_start(o.key_f.rearrange("(p c) -> p c", p=P), dst_f[:, :]).then_inc(stored, 16)
            sp.wait_ge(dve_done, 26)
            sp.dma_start(o.gk_d.rearrange("(p c) -> p c", p=P), gk_i[:, :]).then_inc(stored, 16)
            sp.dma_start(o.wk_d.rearrange("(p c) -> p c", p=P), wk_i[:, :]).then_inc(stored, 16)
            sp.wait_ge(stored, 48)
            sp.dma_start(o.gk[:, :], o.gk_d.rearrange("(a k) -> a k", a=1)).then_inc(listed, 16)
            sp.dma_start(o.wk[:, :], o.wk_d.rearrange("(a k) -> a k", a=1)).then_inc(listed, 16)
            sp.wait_ge(listed, 32)

        @block.gpsimd
        def _(pool):
            nc.gpsimd.iota(m.iota[:, :], [[1, P]], base=0, channel_multiplier=0,
                           allow_small_or_imprecise_dtypes=True).then_inc(pool_done, 1)
            nc.gpsimd.iota(m.node[:, :], [[P, WX]], base=0, channel_multiplier=1,
                           allow_small_or_imprecise_dtypes=True).then_inc(pool_done, 1)
            nc.gpsimd.iota(m.base[:, :], [[P, WX]], base=0, channel_multiplier=0,
                           allow_small_or_imprecise_dtypes=True).then_inc(pool_done, 1)
            nc.gpsimd.iota(k_i[:, :], [[1, KC]], base=0, channel_multiplier=KC).then_inc(pool_done, 1)

        @block.tensor
        def _(pe):
            pe.wait_ge(dve_done, 12)
            nc.tensor.matmul(ps[:, 0:NG + 1], count_b[:, :], below[:, :], start=True, stop=True)
            nc.tensor.matmul(ps[:, 256:256 + NG], wmin_b[:, :], m.ident[0:NG, 0:NG],
                             start=True, stop=True).then_inc(pe_done, 1)

        @block.vector
        def _(dve):
            n = [0]

            def link(ins):
                n[0] += 1
                ins.then_inc(dve_done, 1)
                dve.wait_ge(dve_done, n[0])

            dve.wait_ge(loaded, 32)
            dve.wait_ge(pool_done, 4)
            link(nc.vector.tensor_copy(dst_f[:, :], dst_i[:, :]))
            link(nc.vector.tensor_scalar(m.ident[:, :], m.iota[:, :], m.node[:, 0:1], None, ALU.is_equal))
            link(nc.vector.tensor_reduce(lim_f[:, 0:1], dst_rows[:, :], AX.X, ALU.min))
            link(nc.vector.tensor_reduce(lim_f[:, 1:2], dst_rows[:, :], AX.X, ALU.max))
            link(nc.vector.tensor_copy(lim_i[:, :], lim_f[:, :]))
            link(nc.vector.tensor_scalar(win_i[:, :], lim_i[:, :], 7, None, ALU.arith_shift_right))
            link(nc.vector.tensor_copy(win[:, :], win_i[:, :]))
            link(nc.vector.scalar_tensor_tensor(count[:, :], win[:, 1:2], 1.0, win[:, 0:1], ALU.add, ALU.subtract))
            link(nc.vector.tensor_copy(count_b[:, :], count[:, 0:1].broadcast_to([NG, P])))
            link(nc.vector.tensor_copy(wmin_b[:, :], win[:, 0:1].broadcast_to([NG, P])))
            link(nc.vector.tensor_scalar(below[:, :], m.iota[0:NG, 0:NG + 1], m.node[0:NG, 0:1], None, ALU.is_gt))
            link(nc.vector.tensor_copy(k_f[:, :], k_i[:, :]))
            dve.wait_ge(pe_done, 1)
            link(nc.vector.tensor_copy(start[:, :], ps[:, 0:NG + 1]))
            link(nc.vector.tensor_tensor(delta[:, :], ps[:, 256:256 + NG], start[:, 0:NG], ALU.subtract))
            link(nc.vector.tensor_tensor(delta_step[:, 1:NG], delta[:, 1:NG], delta[:, 0:NG - 1], ALU.subtract))
            link(nc.vector.tensor_copy(delta_step[:, 0:1], delta[:, 0:1]))
            start_b = start[:, 0:NG].unsqueeze(1).broadcast_to([P, KC, NG])
            k_b = k_f[:, :].unsqueeze(2).broadcast_to([P, KC, NG])
            link(nc.vector.tensor_tensor(le[:, :, :], start_b, k_b, ALU.is_le))
            link(nc.vector.tensor_reduce(gk[:, :], le[:, :, :], AX.X, ALU.add))
            link(nc.vector.tensor_scalar(gk[:, :], gk[:, :], -1.0, None, ALU.add))
            link(nc.vector.tensor_copy(gk_i[:, :], gk[:, :]))
            d_b = delta_step[:, :].unsqueeze(1).broadcast_to([P, KC, NG])
            link(nc.vector.tensor_tensor(le[:, :, :], le[:, :, :], d_b, ALU.mult))
            link(nc.vector.tensor_reduce(wk[:, :], le[:, :, :], AX.X, ALU.add))
            link(nc.vector.tensor_tensor(wk[:, :], wk[:, :], k_f[:, :], ALU.add))
            link(nc.vector.tensor_scalar(wk[:, :], wk[:, :], float(WX - 1), None, ALU.min))
            link(nc.vector.tensor_copy(wk_i[:, :], wk[:, :]))
            link(nc.vector.tensor_scalar(half_f[:, :], start[0:1, NG:NG + 1], 1.0, None, ALU.add))
            link(nc.vector.tensor_copy(half_i[:, :], half_f[:, :]))
            link(nc.vector.tensor_scalar(o.pairs[:, :], half_i[:, :], 1, None, ALU.arith_shift_right))


def drive(eng, o, front, back=None):
    pairs = eng.value_load(o.pairs[0:1, 0:1], min_val=1, max_val=KMAX // 2 - 1)
    if front:
        front(0, 0, 0)
    with eng.Fori(0, pairs) as i:
        if front:
            front(2 * i + 1, i, 1)
        if back:
            back(2 * i, i, 0)
        if front:
            front(2 * i + 2, i + 1, 0)
        if back:
            back(2 * i + 1, i, 1)


def window_of(eng, o, k):
    return eng.value_load(o.wk[0:1, bass.ds(k, 1)], min_val=0, max_val=WX - 1)


def group_of(eng, o, k):
    return eng.value_load(o.gk[0:1, bass.ds(k, 1)], min_val=0, max_val=NG - 1)


def edge_sums(nc, m, o, agg):
    with ExitStack() as ctx:
        sb = lambda n, s, d=F32: [ctx.enter_context(nc.sbuf_tensor(f"{n}{b}", s, d)) for b in range(2)]
        sem = lambda n: ctx.enter_context(nc.semaphore(n))
        W = D + D_EA64
        idx, dst_c = sb("e0_idx", [P, J], I32), sb("e0_dst_c", [P, J])
        attr = sb("e0_attr", [P, J, D_EA64])
        rel, hot, xg = sb("e0_rel", [P, J]), sb("e0_hot", [P, J, P]), sb("e0_xg", [P, J, D])
        total = [ctx.enter_context(nc.psum_tensor(f"e0_total{b}", [P, 512], F32)) for b in range(2)]
        loaded = [sem(f"e0_loaded{b}") for b in range(2)]
        gathered = [sem(f"e0_gathered{b}") for b in range(2)]
        hots = Stages(sem("e0_hots"), ["rel", "hot"])
        sums = Stages(sem("e0_sums"), ["sum"])
        merges = Stages(sem("e0_merges"), ["merged"])
        zeroed = sem("e0_zeroed")
        block = ctx.enter_context(nc.Block())

        @block.sync
        def _(sp):
            def front(k, i, b):
                g = group_of(sp, o, k)
                sp.wait_ge(sums.sem, sums.at("sum", k - 2))
                sp.dma_start(idx[b][:, :], o.other[bass.ds(g * GE, GE)].rearrange("(p j) -> p j", j=J)).then_inc(loaded[b], 16)
                sp.dma_start(dst_c[b][:, :], o.key_f[bass.ds(g * GE, GE)].rearrange("(p j) -> p j", j=J)).then_inc(loaded[b], 16)
                sp.dma_start(attr[b][:, :, :], m.inputs["ea64"][bass.ds(g * GE, GE), :].rearrange("(p j) c -> p j c", j=J)).then_inc(loaded[b], 16)
            drive(sp, o, front)

        @block.gpsimd
        def _(pool):
            nc.gpsimd.memset(agg[:, :, :], 0.0).then_inc(zeroed, 1)

            def front(k, i, b):
                pool.wait_ge(loaded[b], 48 * (i + 1))
                settle(pool)
                for j in range(J):
                    pool.indirect_dma_start(
                        out=xg[b][:, j, :], out_offset=None, in_=m.inputs["x"],
                        in_offset=bass.IndirectOffsetOnAxis(ap=idx[b][:, j:j + 1], axis=0)).then_inc(gathered[b], 16)
            drive(pool, o, front)

        @block.tensor
        def _(pe):
            pe.sem_inc(sums.sem, sums.start)

            def back(k, i, b):
                pe.wait_ge(hots.sem, hots.at("hot", k))
                pe.wait_ge(merges.sem, merges.at("merged", k - 2))
                pe.wait_ge(gathered[b], 16 * J * (i + 1))
                for j in range(J):
                    nc.tensor.matmul(total[b][:, 0:D], hot[b][:, j, :], xg[b][:, j, :], start=(j == 0), stop=(j == J - 1))
                pe.wait_ge(loaded[b], 48 * (i + 1))
                for j in range(J):
                    mm = nc.tensor.matmul(total[b][:, D:W], hot[b][:, j, :], attr[b][:, j, :], start=(j == 0), stop=(j == J - 1))
                mm.then_inc(sums.sem, 1)
            drive(pe, o, None, back)

        @block.vector
        def _(dve):
            dve.sem_inc(hots.sem, hots.start)
            dve.sem_inc(merges.sem, merges.start)
            dve.wait_ge(zeroed, 1)

            def front(k, i, b):
                w = window_of(dve, o, k)
                dve.wait_ge(loaded[b], 48 * (i + 1))
                nc.vector.tensor_scalar(rel[b][:, :], dst_c[b][:, :], m.base[:, bass.ds(w, 1)], None, ALU.subtract).then_inc(hots.sem, 1)
                dve.wait_ge(hots.sem, hots.at("rel", k))
                dve.wait_ge(sums.sem, sums.at("sum", k - 2))
                for j in range(J):
                    ins = nc.vector.tensor_scalar(hot[b][:, j, :], m.iota[:, :], rel[b][:, j:j + 1], None, ALU.is_equal)
                ins.then_inc(hots.sem, 1)

            def back(k, i, b):
                w = window_of(dve, o, k)
                dve.wait_ge(sums.sem, sums.at("sum", k))
                dve.wait_ge(merges.sem, merges.at("merged", k - 1))
                a = agg[:, bass.ds(w, 1), :].rearrange("p a c -> p (a c)")
                nc.vector.tensor_tensor(a, a, total[b][:, 0:W], ALU.add).then_inc(merges.sem, 1)
            drive(dve, o, front, back)


def sort_edges(nc, m):
    with ExitStack() as ctx:
        one = lambda n, s, d=F32: ctx.enter_context(nc.sbuf_tensor(f"so_{n}", s, d))
        two = lambda n, s, d=F32: [one(f"{n}{b}", s, d) for b in range(2)]
        bank = lambda n: ctx.enter_context(nc.psum_tensor(f"so_{n}", [P, 512], F32))
        sem = lambda n: ctx.enter_context(nc.semaphore(f"so_{n}"))
        run = one("run", [P, J + 1, WX])
        lower = one("lower", [P, P])

        C, CB = EP // P, 16
        with ExitStack() as first:
            tmp = lambda n, s, d=F32: first.enter_context(nc.sbuf_tensor(f"so_{n}", s, d))
            pair_all = tmp("pair_all", [P, C, 2], I32)
            lo_i, hi_i = tmp("lo_i", [P, C], I32), tmp("hi_i", [P, C], I32)
            row_i = tmp("row_i", [P, C], I32)
            cols = tmp("cols", [P, C, 3])
            flat = [tmp(f"flat{i}", [P, C]) for i in range(2)]
            hot, high = tmp("hot_all", [P, CB, P]), tmp("high_all", [P, CB, WX])
            zero, ones = tmp("zero", [P, P]), tmp("ones", [P, P])
            below = tmp("below", [P, P])
            per_window, before_window = tmp("per_window", [P, WX]), tmp("before_window", [P, WX])
            counts = tmp("counts", [P, WX])
            count_ps, pre_ps = bank("count"), bank("pre")
            loaded, stored, made, counted, dve_done, pe_done = (sem(n) for n in ("a_loaded", "a_stored", "a_made", "a_counted", "a_dve", "a_pe"))
            block = first.enter_context(nc.Block())

            @block.sync
            def _(sp):
                sp.dma_start(pair_all[:, :, :], m.inputs["pair"].rearrange("(p c) t -> p c t", p=P)).then_inc(loaded, 16)
                sp.wait_ge(dve_done, 8)
                sp.dma_start(m.row_cols.rearrange("(p c) t -> p c t", p=P), cols[:, :, :]).then_inc(stored, 16)
                sp.dma_start(m.row_f.rearrange("(p c) -> p c", p=P), flat[0][:, :]).then_inc(stored, 16)
                sp.dma_start(m.row_lo.rearrange("(p c) -> p c", p=P), flat[1][:, :]).then_inc(stored, 16)
                sp.wait_ge(stored, 48)

            @block.gpsimd
            def _(pool):
                nc.gpsimd.memset(zero[:, :], 0.0).then_inc(loaded, 1)
                nc.gpsimd.memset(ones[:, :], 1.0).then_inc(loaded, 1)

            @block.tensor
            def _(pe):
                pe.wait_ge(loaded, 18)
                nc.tensor.matmul(count_ps[:, 0:WX], zero[:, :], zero[:, 0:WX], start=True, stop=True)
                with pe.Fori(0, C // CB) as i:
                    pe.wait_ge(made, i + 1)
                    for t in range(CB):
                        mm = nc.tensor.matmul(count_ps[:, 0:WX], hot[:, t, :], high[:, t, :], start=False, stop=True, skip_group_check=True)
                    mm.then_inc(counted, 1)
                pe.wait_ge(dve_done, 11)
                nc.tensor.matmul(pre_ps[:, 0:WX], below[:, :], counts[:, :], start=True, stop=True)
                nc.tensor.matmul(pre_ps[:, 64:64 + WX], ones[:, :], counts[:, :], start=True, stop=True).then_inc(pe_done, 1)

            @block.vector
            def _(dve):
                n = [0]

                def link(ins):
                    n[0] += 1
                    ins.then_inc(dve_done, 1)
                    dve.wait_ge(dve_done, n[0])

                dve.wait_ge(loaded, 18)
                link(nc.vector.tensor_copy(row_i[:, :], pair_all[:, :, 0:1].rearrange("p c a -> p (c a)")))
                link(nc.vector.tensor_scalar(lo_i[:, :], row_i[:, :], P - 1, None, ALU.bitwise_and))
                link(nc.vector.tensor_scalar(hi_i[:, :], row_i[:, :], 7, None, ALU.arith_shift_right))
                link(nc.vector.tensor_copy(cols[:, :, 0:1].rearrange("p c a -> p (c a)"), row_i[:, :]))
                link(nc.vector.tensor_copy(cols[:, :, 1:2].rearrange("p c a -> p (c a)"), lo_i[:, :]))
                link(nc.vector.tensor_copy(cols[:, :, 2:3].rearrange("p c a -> p (c a)"), hi_i[:, :]))
                link(nc.vector.tensor_copy(flat[0][:, :], row_i[:, :]))
                link(nc.vector.tensor_copy(flat[1][:, :], lo_i[:, :]))
                dve.sem_inc(counted, 1)
                with dve.Fori(0, C // CB) as i:
                    dve.wait_ge(counted, i + 1)
                    lo = cols[:, bass.ds(i * CB, CB), 1:2].broadcast_to([P, CB, P])
                    hi = cols[:, bass.ds(i * CB, CB), 2:3].broadcast_to([P, CB, WX])
                    nc.vector.tensor_tensor(hot[:, :, :], m.iota[:, :].unsqueeze(1).broadcast_to([P, CB, P]), lo, ALU.is_equal)
                    nc.vector.tensor_tensor(high[:, :, :], m.iota[:, 0:WX].unsqueeze(1).broadcast_to([P, CB, WX]), hi, ALU.is_equal).then_inc(made, 1)
                dve.wait_ge(counted, C // CB + 1)
                link(nc.vector.tensor_copy(counts[:, :], count_ps[:, 0:WX]))
                link(nc.vector.tensor_scalar(below[:, :], m.iota[:, :], m.node[:, 0:1], None, ALU.is_gt))
                link(nc.vector.tensor_scalar(lower[:, :], m.iota[:, :], m.node[:, 0:1], None, ALU.is_lt))
                dve.wait_ge(pe_done, 1)
                link(nc.vector.tensor_copy(per_window[:, :], pre_ps[:, 64:64 + WX]))
                link(nc.vector.tensor_tensor_scan(before_window[:, :], ones[:, 0:WX], per_window[:, :], 0.0, ALU.mult, ALU.add))
                link(nc.vector.tensor_tensor(before_window[:, :], before_window[:, :], per_window[:, :], ALU.subtract))
                link(nc.vector.tensor_tensor(run[:, 0, :], pre_ps[:, 0:WX], before_window[:, :], ALU.add))

        with ExitStack() as second:
            tmp = lambda n, s, d=F32: second.enter_context(nc.sbuf_tensor(f"so_{n}", s, d))
            two = lambda n, s, d=F32: [tmp(f"{n}{b}", s, d) for b in range(2)]
            pair, col = two("pair", [P, J, 2], I32), two("col", [P, J, 3])
            row_r, lo_r = two("row_r", [P, GE]), two("lo_r", [P, GE])
            hot, hot_t, high = two("hot", [P, J, P]), two("hot_t", [P, J, P]), two("high", [P, J, WX])
            tied = tmp("tied", [P, J, P])
            tie, place = two("tie", [P, J]), tmp("place", [P, J])
            at_sel = tmp("at_sel", [P, J, WX])
            place_i = two("place_i", [P, J], I32)
            hist, at = [second.enter_context(nc.psum_tensor(f"so_hist{b}", [P, 512], F32)) for b in range(2)], \
                [second.enter_context(nc.psum_tensor(f"so_at{b}", [P, 512], F32)) for b in range(2)]
            loaded = [sem(f"b_loaded{b}") for b in range(2)]
            scattered = [sem(f"b_scattered{b}") for b in range(2)]
            dve_s = Stages(sem("b_dve"), ["hot_t", "hots", "tie"] + [f"run{j}" for j in range(1, J + 1)] + ["run0", "picked", "place", "ranked", "placed"])
            pe_s = Stages(sem("b_pe"), ["hist", "at"])
            pool_s = Stages(sem("b_pool"), ["scattered"])
            block = second.enter_context(nc.Block())

            @block.sync
            def _(sp):
                with sp.Fori(0, NG // 2) as i:
                    for b in range(2):
                        k = 2 * i + b
                        part = bass.ds(k * GE, GE)
                        sp.wait_ge(dve_s.sem, dve_s.at("tie", k - 2))
                        sp.dma_start(col[b][:, :, :], m.row_cols[part, :].rearrange("(p j) t -> p j t", j=J)).then_inc(loaded[b], 16)
                        sp.dma_start(row_r[b][:, :], row_everywhere(m.row_f[part])).then_inc(loaded[b], 16)
                        sp.dma_start(lo_r[b][:, :], row_everywhere(m.row_lo[part])).then_inc(loaded[b], 16)
                        sp.wait_ge(pool_s.sem, pool_s.at("scattered", k - 2))
                        sp.dma_start(pair[b][:, :, :], m.inputs["pair"][part, :].rearrange("(p j) t -> p j t", j=J)).then_inc(loaded[b], 16)

            @block.gpsimd
            def _(pool):
                pool.sem_inc(pool_s.sem, pool_s.start)
                with pool.Fori(0, NG // 2) as i:
                    for b in range(2):
                        pool.wait_ge(loaded[b], 64 * (i + 1))
                        pool.wait_ge(dve_s.sem, dve_s.at("placed", 2 * i + b))
                        settle(pool)
                        for j in range(J):
                            pool.indirect_dma_start(
                                out=m.sorted, out_offset=bass.IndirectOffsetOnAxis(ap=place_i[b][:, j:j + 1], axis=0),
                                in_=pair[b][:, j, :], in_offset=None).then_inc(scattered[b], 16)
                        pool.wait_ge(scattered[b], 16 * J * (i + 1))
                        pool.sem_inc(pool_s.sem, 1)

            @block.tensor
            def _(pe):
                pe.sem_inc(pe_s.sem, pe_s.start)
                with pe.Fori(0, NG // 2) as i:
                    for b in range(2):
                        k = 2 * i + b
                        pe.wait_ge(dve_s.sem, dve_s.at("hots", k))
                        for j in range(J):
                            mm = nc.tensor.matmul(hist[b][:, j * WX:(j + 1) * WX], hot[b][:, j, :], high[b][:, j, :], start=True, stop=True)
                        mm.then_inc(pe_s.sem, 1)
                        pe.wait_ge(dve_s.sem, dve_s.at(f"run{J}", k))
                        for j in range(J):
                            mm = nc.tensor.matmul(at[b][:, j * WX:(j + 1) * WX], hot_t[b][:, j, :], run[:, j, :], start=True, stop=True)
                        mm.then_inc(pe_s.sem, 1)

            @block.vector
            def _(dve):
                dve.sem_inc(dve_s.sem, dve_s.start)
                with dve.Fori(0, NG // 2) as i:
                    for b in range(2):
                        k = 2 * i + b

                        def link(name, ins):
                            ins.then_inc(dve_s.sem, 1)
                            dve.wait_ge(dve_s.sem, dve_s.at(name, k))

                        dve.wait_ge(loaded[b], 64 * (i + 1))
                        dve.wait_ge(pe_s.sem, pe_s.at("at", k - 2))
                        nc.vector.tensor_scalar(hot_t[b][:, :, :], lo_r[b][:, :].rearrange("p (e j) -> p j e", j=J),
                                                m.node[:, 0:1], None, ALU.is_equal).then_inc(dve_s.sem, 1)
                        for j in range(J):
                            nc.vector.tensor_scalar(hot[b][:, j, :], m.iota[:, :], col[b][:, j, 1:2], None, ALU.is_equal)
                        nc.vector.tensor_tensor(high[b][:, :, :], m.iota[:, 0:WX].unsqueeze(1).broadcast_to([P, J, WX]),
                                                col[b][:, :, 2:3].broadcast_to([P, J, WX]), ALU.is_equal).then_inc(dve_s.sem, 1)
                        for j in range(J):
                            ins = nc.vector.scalar_tensor_tensor(tied[:, j, :], row_r[b][:, :].rearrange("p (e j) -> p j e", j=J)[:, j, :],
                                                                 col[b][:, j, 0:1], lower[:, :], ALU.is_equal, ALU.mult, accum_out=tie[b][:, j:j + 1])
                        link("tie", ins)
                        dve.wait_ge(pe_s.sem, pe_s.at("hist", k))
                        for j in range(J):
                            link(f"run{j + 1}", nc.vector.tensor_tensor(run[:, j + 1, :], run[:, j, :], hist[b][:, j * WX:(j + 1) * WX], ALU.add))
                        dve.wait_ge(pe_s.sem, pe_s.at("at", k))
                        link("run0", nc.vector.tensor_copy(run[:, 0, :], run[:, J, :]))
                        link("picked", nc.vector.tensor_tensor(at_sel[:, :, :], at[b][:, 0:J * WX].rearrange("p (j w) -> p j w", j=J), high[b][:, :, :], ALU.mult))
                        link("place", nc.vector.tensor_reduce(place[:, :], at_sel[:, :, :], AX.X, ALU.add))
                        link("ranked", nc.vector.tensor_tensor(place[:, :], place[:, :], tie[b][:, :], ALU.add))
                        dve.wait_ge(pool_s.sem, pool_s.at("scattered", k - 2))
                        link("placed", nc.vector.tensor_copy(place_i[b][:, :], place[:, :]))

        with ExitStack() as third:
            tmp = lambda n, s, d=F32: third.enter_context(nc.sbuf_tensor(f"so_{n}", s, d))
            pair_all, row, col = tmp("pairs", [P, C, 2], I32), tmp("row", [P, C], I32), tmp("col_s", [P, C], I32)
            loaded, split, stored = sem("c_loaded"), sem("c_split"), sem("c_stored")
            block = third.enter_context(nc.Block())

            @block.sync
            def _(sp):
                sp.dma_start(pair_all[:, :, :], m.sorted.rearrange("(p c) t -> p c t", p=P)).then_inc(loaded, 16)
                sp.wait_ge(split, 2)
                sp.dma_start(m.row_sorted.rearrange("(p c) -> p c", p=P), row[:, :]).then_inc(stored, 16)
                sp.dma_start(m.col_sorted.rearrange("(p c) -> p c", p=P), col[:, :]).then_inc(stored, 16)
                sp.wait_ge(stored, 32)

            @block.vector
            def _(dve):
                dve.wait_ge(loaded, 16)
                nc.vector.tensor_copy(row[:, :], pair_all[:, :, 0:1].rearrange("p c a -> p (c a)")).then_inc(split, 1)
                nc.vector.tensor_copy(col[:, :], pair_all[:, :, 1:2].rearrange("p c a -> p (c a)")).then_inc(split, 1)


def attention(nc, m, o, tag, H, C, table, own, own_lin, state, dot):
    W, JH = H * C, J * H
    TW = 2 * W if dot else W + H
    banks = J if dot else 3
    before = lambda j, k: (j - banks, k) if j >= banks else (max(t for t in range(J) if t % banks == j), k - 1)
    with ExitStack() as ctx:
        one = lambda n, s, d=F32: ctx.enter_context(nc.sbuf_tensor(f"{tag}_{n}", s, d))
        two = lambda n, s, d=F32: [one(f"{n}{b}", s, d) for b in range(2)]
        bank = lambda n: ctx.enter_context(nc.psum_tensor(f"{tag}_{n}", [P, 512], F32))
        sem = lambda n: ctx.enter_context(nc.semaphore(f"{tag}_{n}"))
        idx, dst_c, dst_r = two("idx", [P, J], I32), two("dst_c", [P, J]), two("dst_r", [P, GE])
        rel, hot, hot_t, mask = two("rel", [P, J]), two("hot", [P, J, P]), two("hot_t", [P, J, P]), two("mask", [P, J, P])
        rows = two("rows", [P, J, TW])
        score = two("score", [P, JH])
        mixed = one("mixed", [P, J, W])
        score_t = one("score_t", [JH, P])
        top_old, top, gap, shrink = (one(n, [P, H]) for n in ("top_old", "top", "gap", "shrink"))
        arg, prob = one("arg", [P, JH]), one("prob", [P, JH])
        weighed = one("weighed", [P, J, W] if dot else [P, JH, P])
        own_at_edge = [bank(f"own{j}") for j in range(banks)] * 2
        lin = None if dot else bank("lin")
        spread = [bank(f"spread{b}") for b in range(2)]
        sums, small = bank("sums"), bank("small")
        loaded = [sem(f"loaded{b}") for b in range(2)]
        gathered = [sem(f"gathered{b}") for b in range(2)]
        zeroed, self_loaded = sem("zeroed"), sem("self_loaded")
        pair, self_score = mixed[:, 0, :], one("self_score", [P, H])
        selfs = Stages(sem("selfs"), ["pair", "relu", "dot", "lin", "top"])
        hots = Stages(sem("hots"), ["rel", "hot_t", "mask", "hot"])
        owns = Stages(sem("owns"), [f"own{j}" for j in range(J)] + ([] if dot else ["lin"]))
        relus = Stages(sem("relus"), [f"relu{j}" for j in range(J)])
        scores = Stages(sem("scores"), [f"product{j}" for j in range(J)] + ["score"] if dot else ["relu_part", "score"])
        pe_b = Stages(sem("pe"), ["turned"] + [f"spread{h}" for h in range(H)] + ["top_at_edge", "summed"])
        act_b = Stages(sem("act"), ["turned", "shrink", "prob"])
        dve_b = Stages(sem("dve"), ["old"] + [f"top{h}" for h in range(H)] + ["kept", "gap", "arg", "clamped", "weighed"]
                       + (["shrunk"] if dot else []) + ["weight_shrunk", "merged_weight", "merged"])
        block = ctx.enter_context(nc.Block())

        @block.sync
        def _(sp):
            def front(k, i, b):
                g = group_of(sp, o, k)
                sp.wait_ge(pe_b.sem, pe_b.at("summed", k - 2))
                part = bass.ds(g * GE, GE)
                sp.dma_start(idx[b][:, :], o.other[part].rearrange("(p j) -> p j", j=J)).then_inc(loaded[b], 16)
                sp.dma_start(dst_c[b][:, :], o.key_f[part].rearrange("(p j) -> p j", j=J)).then_inc(loaded[b], 16)
                sp.dma_start(dst_r[b][:, :], row_everywhere(o.key_f[part])).then_inc(loaded[b], 16)
            if not dot:
                sp.dma_start(state.total[:, 0:WN, :], table[:, 0:W].rearrange("(w p) c -> p w c", p=P)).then_inc(self_loaded, 16)
                with nc.allow_non_contiguous_dma(reason="H numbers per node, once"):
                    sp.dma_start(state.top[:, 0:WN, :], table[:, W:W + H].rearrange("(w p) c -> p w c", p=P)).then_inc(self_loaded, 16)
            drive(sp, o, front)

        @block.gpsimd
        def _(pool):
            first = 0 if dot else WN
            nc.gpsimd.memset(state.total[:, first:WX, :], 0.0).then_inc(zeroed, 1)
            nc.gpsimd.memset(state.weight[:, :, :], 0.0 if dot else 1.0).then_inc(zeroed, 1)
            nc.gpsimd.memset(state.top[:, first:WX, :], -BIG).then_inc(zeroed, 1)
            nc.gpsimd.memset(own[:, WX - 1, :], 0.0).then_inc(zeroed, 1)
            nc.gpsimd.memset(own_lin[:, WX - 1, :], 0.0).then_inc(zeroed, 1)

            def front(k, i, b):
                pool.wait_ge(loaded[b], 48 * (i + 1))
                settle(pool)
                for j in range(J):
                    pool.indirect_dma_start(
                        out=rows[b][:, j, :], out_offset=None, in_=table,
                        in_offset=bass.IndirectOffsetOnAxis(ap=idx[b][:, j:j + 1], axis=0)).then_inc(gathered[b], 16)
            drive(pool, o, front)

        @block.tensor
        def _(pe):
            pe.sem_inc(owns.sem, owns.start)
            pe.sem_inc(pe_b.sem, pe_b.start)
            pe.wait_ge(zeroed, 5)

            def front(k, i, b):
                w = window_of(pe, o, k)
                pe.wait_ge(hots.sem, hots.at("hot_t", k))
                if not dot:
                    pe.wait_ge(gathered[b], 16 * J * (i + 1))
                for j in range(J):
                    t, at = before(j, k)
                    if dot:
                        pe.wait_ge(scores.sem, scores.at(f"product{t}", at))
                    else:
                        pe.wait_ge(relus.sem, relus.at(f"relu{t}", at))
                        nc.tensor.matmul(own_at_edge[j][:, 0:W], m.ident[:, :], rows[b][:, j, 0:W], start=True, stop=False)
                    nc.tensor.matmul(own_at_edge[j][:, 0:W], hot_t[b][:, j, :], own[:, bass.ds(w, 1), :].rearrange("p a c -> p (a c)"),
                                     start=dot, stop=True).then_inc(owns.sem, 1)
                if not dot:
                    pe.wait_ge(scores.sem, scores.at("score", k - 1))
                    for j in range(J):
                        nc.tensor.matmul(lin[:, j * H:(j + 1) * H], m.ident[:, :], rows[b][:, j, W:W + H], start=True, stop=False)
                        mm = nc.tensor.matmul(lin[:, j * H:(j + 1) * H], hot_t[b][:, j, :],
                                              own_lin[:, bass.ds(w, 1), :].rearrange("p a c -> p (a c)"), start=False, stop=True)
                    mm.then_inc(owns.sem, 1)

            def back(k, i, b):
                pe.wait_ge(scores.sem, scores.at("score", k))
                pe.wait_ge(dve_b.sem, dve_b.at("merged_weight", k - 1))
                nc.tensor.transpose(small[0:JH, 0:P], score[b][:, :], m.ident[:, :]).then_inc(pe_b.sem, 1)
                pe.wait_ge(act_b.sem, act_b.at("turned", k))
                for h in range(H):
                    pe.wait_ge(dve_b.sem, dve_b.at(f"top{h - 2}", k) if h >= 2 else
                               dve_b.at(f"top{H - 1 if H == 1 else H - 2 + h}", k - 1))
                    for j in range(J):
                        r = j * H + h
                        mm = nc.tensor.matmul(spread[h % 2][:, j * P:(j + 1) * P], m.ident[0:JH, r:r + 1].broadcast_to([JH, P]),
                                              score_t[:, :], start=True, stop=True)
                    mm.then_inc(pe_b.sem, 1)
                pe.wait_ge(dve_b.sem, dve_b.at(f"top{H - 1}", k))
                for j in range(J):
                    mm = nc.tensor.matmul(small[:, j * H:(j + 1) * H], hot_t[b][:, j, :], top[:, :], start=True, stop=True)
                mm.then_inc(pe_b.sem, 1)
                pe.wait_ge(dve_b.sem, dve_b.at("merged", k - 1))
                pe.wait_ge(dve_b.sem, dve_b.at("weighed", k))
                if dot:
                    for j in range(J):
                        nc.tensor.matmul(sums[:, 0:W], hot[b][:, j, :], weighed[:, j, :], start=(j == 0), stop=(j == J - 1))
                else:
                    for h in range(H):
                        for j in range(J):
                            nc.tensor.matmul(sums[:, h * C:(h + 1) * C], weighed[:, j * H + h, :], rows[b][:, j, h * C:(h + 1) * C],
                                             start=(j == 0), stop=(j == J - 1))
                for j in range(J):
                    mm = nc.tensor.matmul(small[:, 0:H], hot[b][:, j, :], prob[:, j * H:(j + 1) * H], start=(j == 0), stop=(j == J - 1))
                mm.then_inc(pe_b.sem, 1)
            drive(pe, o, front, back)

        @block.scalar
        def _(act):
            act.sem_inc(relus.sem, relus.start)
            act.sem_inc(act_b.sem, act_b.start)
            if not dot:
                act.wait_ge(selfs.sem, selfs.at("dot", WN - 1))

            def front(k, i, b):
                act.wait_ge(scores.sem, scores.at("relu_part", k - 1))
                for j in range(J):
                    act.wait_ge(owns.sem, owns.at(f"own{j}", k))
                    nc.scalar.activation(mixed[:, j, :], own_at_edge[j][:, 0:W], ACT.Relu).then_inc(relus.sem, 1)

            def back(k, i, b):
                act.wait_ge(pe_b.sem, pe_b.at("turned", k))
                nc.scalar.copy(score_t[:, :], small[0:JH, 0:P]).then_inc(act_b.sem, 1)
                act.wait_ge(dve_b.sem, dve_b.at("gap", k))
                act.wait_ge(dve_b.sem, dve_b.at("merged", k - 1))
                nc.scalar.activation(shrink[:, :], gap[:, :], ACT.Exp).then_inc(act_b.sem, 1)
                act.wait_ge(dve_b.sem, dve_b.at("clamped", k))
                nc.scalar.activation(prob[:, :], arg[:, :], ACT.Exp).then_inc(act_b.sem, 1)
            drive(act, o, None if dot else front, back)

        @block.vector
        def _(dve):
            for s in (hots, scores, dve_b, selfs):
                dve.sem_inc(s.sem, s.start)
            dve.wait_ge(zeroed, 5)
            if not dot:
                dve.wait_ge(self_loaded, 32)
                with dve.Fori(0, WN) as w:
                    def link(name, ins):
                        ins.then_inc(selfs.sem, 1)
                        dve.wait_ge(selfs.sem, selfs.at(name, w))

                    at = lambda t: t[:, bass.ds(w, 1), :].rearrange("p a c -> p (a c)")
                    link("pair", nc.vector.tensor_tensor(pair, at(state.total), at(own), ALU.add))
                    link("relu", nc.vector.tensor_scalar(pair, pair, 0.0, None, ALU.max))
                    settle(dve)
                    for h in range(H):
                        part = pair[:, h * C:(h + 1) * C]
                        ins = nc.vector.tensor_tensor_reduce(part, part, m.att[tag][:, h * C:(h + 1) * C], 1.0 - SLOPE, 0.0,
                                                             ALU.mult, ALU.add, self_score[:, h:h + 1])
                    link("dot", ins)
                    link("lin", nc.vector.tensor_tensor(self_score[:, :], self_score[:, :], at(own_lin), ALU.add))
                    link("top", nc.vector.tensor_tensor(at(state.top), at(state.top), self_score[:, :], ALU.add))

            def front(k, i, b):
                w = window_of(dve, o, k)
                dve.wait_ge(loaded[b], 48 * (i + 1))
                dve.wait_ge(pe_b.sem, pe_b.at("summed", k - 2))
                nc.vector.tensor_scalar(rel[b][:, :], dst_c[b][:, :], m.base[:, bass.ds(w, 1)], None, ALU.subtract).then_inc(hots.sem, 1)
                nc.vector.tensor_scalar(hot_t[b][:, :, :], dst_r[b][:, :].rearrange("p (e j) -> p j e", j=J),
                                        m.node[:, bass.ds(w, 1)], None, ALU.is_equal).then_inc(hots.sem, 1)
                dve.wait_ge(hots.sem, hots.at("hot_t", k))
                nc.vector.tensor_scalar(mask[b][:, :, :], hot_t[b][:, :, :], -1.0, BIG, ALU.add, ALU.mult).then_inc(hots.sem, 1)
                for j in range(J):
                    ins = nc.vector.tensor_scalar(hot[b][:, j, :], m.iota[:, :], rel[b][:, j:j + 1], None, ALU.is_equal)
                ins.then_inc(hots.sem, 1)
                if dot:
                    dve.wait_ge(gathered[b], 16 * J * (i + 1))
                    dve.wait_ge(scores.sem, scores.at("score", k - 1))
                    for j in range(J):
                        dve.wait_ge(owns.sem, owns.at(f"own{j}", k))
                        nc.vector.tensor_tensor(mixed[:, j, :], own_at_edge[j][:, 0:W], rows[b][:, j, 0:W], ALU.mult).then_inc(scores.sem, 1)
                    dve.wait_ge(scores.sem, scores.at(f"product{J - 1}", k))
                    nc.vector.tensor_reduce(score[b][:, :], mixed[:, :, :].rearrange("p j (h c) -> p (j h) c", h=H), AX.X, ALU.add).then_inc(scores.sem, 1)
                else:
                    for j in range(J):
                        dve.wait_ge(relus.sem, relus.at(f"relu{j}", k))
                        settle(dve)
                        for h in range(H):
                            part = mixed[:, j, h * C:(h + 1) * C]
                            r = j * H + h
                            ins = nc.vector.tensor_tensor_reduce(part, part, m.att[tag][:, h * C:(h + 1) * C], 1.0 - SLOPE, 0.0,
                                                                 ALU.mult, ALU.add, score[b][:, r:r + 1])
                    ins.then_inc(scores.sem, 1)
                    dve.wait_ge(owns.sem, owns.at("lin", k))
                    dve.wait_ge(scores.sem, scores.at("relu_part", k))
                    nc.vector.tensor_tensor(score[b][:, :], score[b][:, :], lin[:, 0:JH], ALU.add).then_inc(scores.sem, 1)

            def back(k, i, b):
                w = window_of(dve, o, k)
                dve.wait_ge(dve_b.sem, dve_b.at("merged", k - 1))
                settle(dve)
                nc.vector.tensor_copy(top_old[:, :], state.top[:, bass.ds(w, 1), :].rearrange("p a h -> p (a h)")).then_inc(dve_b.sem, 1)
                dve.wait_ge(dve_b.sem, dve_b.at("old", k))
                for h in range(H):
                    dve.wait_ge(pe_b.sem, pe_b.at(f"spread{h}", k))
                    settle(dve)
                    nc.vector.tensor_tensor_reduce(spread[h % 2][:, :], spread[h % 2][:, :], mask[b][:, :, :].rearrange("p j e -> p (j e)"),
                                                   1.0, top_old[:, h:h + 1], ALU.add, ALU.max, top[:, h:h + 1]).then_inc(dve_b.sem, 1)
                dve.wait_ge(dve_b.sem, dve_b.at(f"top{H - 1}", k))
                settle(dve)
                nc.vector.tensor_copy(state.top[:, bass.ds(w, 1), :].rearrange("p a h -> p (a h)"), top[:, :]).then_inc(dve_b.sem, 1)
                dve.wait_ge(act_b.sem, act_b.at("shrink", k - 1))
                nc.vector.tensor_tensor(gap[:, :], top_old[:, :], top[:, :], ALU.subtract).then_inc(dve_b.sem, 1)
                dve.wait_ge(pe_b.sem, pe_b.at("top_at_edge", k))
                nc.vector.tensor_tensor(arg[:, :], score[b][:, :], small[:, 0:JH], ALU.subtract).then_inc(dve_b.sem, 1)
                dve.wait_ge(dve_b.sem, dve_b.at("arg", k))
                nc.vector.tensor_scalar(arg[:, :], arg[:, :], 0.0, None, ALU.min).then_inc(dve_b.sem, 1)
                dve.wait_ge(act_b.sem, act_b.at("prob", k))
                if dot:
                    for j in range(J):
                        ins = nc.vector.tensor_tensor(
                            weighed[:, j, :].rearrange("p (h c) -> p h c", h=H), rows[b][:, j, W:2 * W].rearrange("p (h c) -> p h c", h=H),
                            prob[:, j * H:(j + 1) * H].unsqueeze(2).broadcast_to([P, H, C]), ALU.mult)
                else:
                    for r in range(JH):
                        ins = nc.vector.tensor_scalar(weighed[:, r, :], hot[b][:, r // H, :], prob[:, r:r + 1], None, ALU.mult)
                ins.then_inc(dve_b.sem, 1)
                dve.wait_ge(act_b.sem, act_b.at("shrink", k))
                total = state.total[:, bass.ds(w, 1), :].rearrange("p a c -> p (a c)")
                weight = state.weight[:, bass.ds(w, 1), :].rearrange("p a h -> p (a h)")
                if dot:
                    by_head = total.rearrange("p (h c) -> p h c", h=H)
                    nc.vector.tensor_tensor(by_head, by_head, shrink[:, :].unsqueeze(2).broadcast_to([P, H, C]), ALU.mult).then_inc(dve_b.sem, 1)
                nc.vector.tensor_tensor(weight, weight, shrink[:, :], ALU.mult).then_inc(dve_b.sem, 1)
                dve.wait_ge(dve_b.sem, dve_b.at("weight_shrunk", k))
                dve.wait_ge(pe_b.sem, pe_b.at("summed", k))
                nc.vector.tensor_tensor(weight, weight, small[:, 0:H], ALU.add).then_inc(dve_b.sem, 1)
                if dot:
                    ins = nc.vector.tensor_tensor(total, total, sums[:, 0:W], ALU.add)
                else:
                    for h in range(H):
                        part = state.total[:, bass.ds(w, 1), h * C:(h + 1) * C].rearrange("p a c -> p (a c)")
                        ins = nc.vector.scalar_tensor_tensor(part, part, shrink[:, h:h + 1], sums[:, h * C:(h + 1) * C], ALU.mult, ALU.add)
                ins.then_inc(dve_b.sem, 1)
            drive(dve, o, front, back)


def norm_stages(t):
    return [f"{t}_stats", f"{t}_moments", f"{t}_eps", f"{t}_rstd", f"{t}_normed"]


def layer_norm(dve, link, act_s, c, t, src, dst, nb, eps):
    for w in range(CW):
        ins = nc_of(dve).vector.bn_stats(nb.stats[:, w, :], src[:, w, :])
    link(f"{t}_stats", ins)
    settle(dve)
    for w in range(CW):
        ins = nc_of(dve).vector.bn_aggr(nb.moments[:, w, :], nb.stats[:, w, :])
    link(f"{t}_moments", ins)
    link(f"{t}_eps", nc_of(dve).vector.tensor_scalar(nb.var[:, :], nb.moments[:, :, 1:2].rearrange("p w a -> p (w a)"), eps, None, ALU.add))
    dve.wait_ge(act_s.sem, act_s.at(f"{t}_std", c))
    link(f"{t}_rstd", nc_of(dve).vector.reciprocal(nb.rstd[:, :], nb.std[:, :]))
    for w in range(CW):
        ins = nc_of(dve).vector.tensor_scalar(dst[:, w, :], src[:, w, :], nb.moments[:, w, 0:1], nb.rstd[:, w:w + 1], ALU.subtract, ALU.mult)
    link(f"{t}_normed", ins)


def nc_of(eng):
    return eng.bass


def standard_deviation(act, dve_s, act_s, c, t, nb):
    act.wait_ge(dve_s.sem, dve_s.at(f"{t}_eps", c))
    nc_of(act).scalar.activation(nb.std[:, :], nb.var[:, :], ACT.Sqrt).then_inc(act_s.sem, 1)


class NormBuffers:
    def __init__(self, one):
        self.stats, self.moments = one("stats", [P, CW, 6]), one("moments", [P, CW, 2])
        self.var, self.std, self.rstd = one("var", [P, CW]), one("std", [P, CW]), one("rstd", [P, CW])


class LinearWeights:
    def __init__(self, one, k, H, C):
        self.sums, self.products = one("w_lin", [P, k, 2 * H]), one("w_lin_products", [P, C])


def over_windows(row, n=CW):
    return row.unsqueeze(1).broadcast_to([P, n, row.shape[-1]])


def project_stages(outs):
    return [f"proj{w}_{o}" for w in range(CW) for o in range(outs)]


def project(pe, pe_s, act_s, c, lhs, weights, bias, ring, ones_row):
    n = 0
    for w in range(CW):
        for o, wt in enumerate(weights):
            width = wt[0].shape[-1]
            to = ring[:, n % 3, 0:width]
            if n >= 3:
                pe.wait_ge(act_s.sem, act_s.at(f"proj{(n - 3) // len(weights)}_{(n - 3) % len(weights)}", c))
            for kc, piece in enumerate(wt):
                mm = nc_of(pe).tensor.matmul(to, lhs(kc, w), piece, start=(kc == 0), stop=(kc == len(wt) - 1 and not bias))
            if bias:
                mm = nc_of(pe).tensor.matmul(to, ones_row, bias[o], start=False, stop=True)
            mm.then_inc(pe_s.sem, 1)
            n += 1


def linear_weights(dve, w_lin, weights, att, H, C, ready):
    for o, wt in enumerate(weights):
        for kc in range(wt.shape[1]):
            for h in range(H):
                n = (o * wt.shape[1] + kc) * H + h
                if n:
                    dve.wait_ge(ready, n)
                nc_of(dve).vector.tensor_tensor_reduce(w_lin.products[:, :], wt[:, kc, h * C:(h + 1) * C], att[:, h * C:(h + 1) * C], SLOPE, 0.0,
                                                       ALU.mult, ALU.add, w_lin.sums[:, kc, o * H + h:o * H + h + 1]).then_inc(ready, 1)


def pieces(weight, k, lo, hi):
    return [weight[:, kc, lo:hi] for kc in range(k)]


def project_linear(pe, pe_s, lhs, w_lin, k, H, turn):
    for w in range(CW):
        for kc in range(k):
            mm = nc_of(pe).tensor.matmul(turn[:, 0, w * 2 * H:(w + 1) * 2 * H], lhs(kc, w), w_lin.sums[:, kc, :], start=(kc == 0), stop=(kc == k - 1))
    mm.then_inc(pe_s.sem, 1)


def keep_linear(act, pe_s, act_s, c, turn, stage, own_lin, W, H):
    act.wait_ge(pe_s.sem, pe_s.at("lin", c))
    both = turn[:, 0, 0:CW * 2 * H].rearrange("p (w t h) -> p w t h", w=CW, t=2)
    nc_of(act).scalar.copy(stage[:, :, W:W + H], both[:, :, 0, :])
    nc_of(act).scalar.copy(own_lin[:, bass.ds(c * CW, CW), :], both[:, :, 1, :]).then_inc(act_s.sem, 1)


def nodes_0(nc, m, agg, table, own, own_lin, H, C):
    with ExitStack() as ctx:
        one = lambda n, s, d=F32: ctx.enter_context(nc.sbuf_tensor(f"n0_{n}", s, d))
        sem = lambda n: ctx.enter_context(nc.semaphore(f"n0_{n}"))
        sums = one("sums", [P, CW, D + D_EA64])
        sums_t = one("sums_t", [P, 3 * CW, P])
        h = one("h", [P, CW, D])
        h_t, y = one("h_t", [P, 2, CW * P]), one("y", [P, 2, CW * P])
        x_t = one("x_t", [P, 2 * CW, P])
        stage = one("stage", [P, CW, 512 + H])
        w_lin = LinearWeights(one, 2, H, C)
        nb = NormBuffers(one)
        w_msg, w_edge = one("w_msg", [P, 2, D]), one("w_edge", [D_EA64, D])
        w_mlp = [one(f"w_mlp{l}", [P, 2, D]) for l in range(3)]
        b_mlp = [one(f"b_mlp{l}", [P, 2]) for l in range(3)]
        rows = {n: one(n, [P, D]) for n in ("ln_aggr_scale", "ln_aggr_bias", "ln_out_scale", "ln_out_bias")}
        w_l, w_r = one("w_l", [P, 2, 512]), one("w_r", [P, 2, 512])
        turn = ctx.enter_context(nc.psum_tensor("n0_turn", [P, 16, P], F32))
        mlp_ps = turn[:, :, :].rearrange("p (b t) c -> p b (t c)", b=4)[:, :, 0:CW * P // 2]
        ring = ctx.enter_context(nc.psum_tensor("n0_ring", [P, 3, 512], F32))
        flat = ring[:, :, :].rearrange("p b c -> p (b c)")[:, 0:CW * D].rearrange("p (w c) -> p w c", w=CW)
        weights_in, taken, stored, lin_ready = sem("weights"), sem("taken"), sem("stored"), sem("lin_ready")
        pe_s = Stages(sem("pe"), ["sums_t", "msg", "h_t", "mlp0", "mlp1", "mlp2", "out", "x_t", "lin"] + project_stages(2))
        act_s = Stages(sem("act"), ["sums_t", "a_std", "h_t", "mlp0", "mlp1", "mlp2", "b_std", "c_std", "x_t", "lin"] + project_stages(2))
        dve_s = Stages(sem("dve"), ["h"] + norm_stages("a") + ["a_scale", "a_bias", "skip0", "skip1", "skip2", "r"] + norm_stages("b")
                       + ["b_scale", "b_bias", "xr"] + norm_stages("c") + ["kept"])
        n_weights = 2 + 3 + 6 + 4 + 2
        block = ctx.enter_context(nc.Block())

        @block.sync
        def _(sp):
            load = lambda to, of: sp.dma_start(to, of).then_inc(weights_in, 16)
            load(w_msg[:, :, :], m.inputs["L0_W_message"][0:D, :].rearrange("(k p) n -> p k n", p=P))
            load(w_edge[:, :], m.inputs["L0_W_message"][D:D + D_EA64, :])
            for l in range(3):
                w, bias = [(m.inputs["L0_mlp_W0"], m.inputs["L0_mlp_b0"]), (m.inputs["L0_mlp_W1"], m.inputs["L0_mlp_b1"]), (m.inputs["L0_mlp_W2"], m.inputs["L0_mlp_b2"])][l]
                load(w_mlp[l][:, :, :], w.rearrange("(k p) n -> p k n", p=P))
                for f in range(2):
                    load(b_mlp[l][:, f:f + 1], column(bias[f * P:(f + 1) * P]))
            for name, of in (("ln_aggr_scale", m.inputs["L0_ln_aggr_scale"]), ("ln_aggr_bias", m.inputs["L0_ln_aggr_bias"]),
                             ("ln_out_scale", m.inputs["L0_ln_out_scale"]), ("ln_out_bias", m.inputs["L0_ln_out_bias"])):
                load(rows[name][:, :], row_everywhere(of))
            load(w_l[:, :, :], m.inputs["L1_W1l"].rearrange("(k p) n -> p k n", p=P))
            load(w_r[:, :, :], m.inputs["L1_W1r"].rearrange("(k p) n -> p k n", p=P))
            with sp.Fori(0, CHUNKS) as c:
                sp.wait_ge(pe_s.sem, pe_s.at("sums_t", c - 1))
                sp.dma_start(sums[:, :, :], agg[:, bass.ds(c * CW, CW), :]).then_inc(taken, 16)
                sp.wait_ge(act_s.sem, act_s.at(f"proj{CW - 1}_1", c))
                sp.dma_start(table[bass.ds(c * CW * P, CW * P), :].rearrange("(w p) n -> p w n", p=P), stage[:, :, :]).then_inc(stored, 16)
            sp.wait_ge(stored, 16 * (CHUNKS + 1))

        @block.tensor
        def _(pe):
            pe.sem_inc(pe_s.sem, pe_s.start)
            pe.wait_ge(weights_in, 16 * n_weights)
            pe.wait_ge(lin_ready, 4 * H)
            with pe.Fori(0, CHUNKS) as c:
                pe.wait_ge(taken, 16 * (c + 1))
                pe.wait_ge(act_s.sem, act_s.at("lin", c - 1))
                for w in range(CW):
                    for kc in range(2):
                        nc.tensor.transpose(turn[:, kc * CW + w, :], sums[:, w, kc * P:(kc + 1) * P], m.ident[:, :])
                    mm = nc.tensor.transpose(turn[0:D_EA64, 2 * CW + w, :], sums[:, w, D:D + D_EA64], m.ident[:, :])
                mm.then_inc(pe_s.sem, 1)
                pe.wait_ge(act_s.sem, act_s.at("sums_t", c))
                pe.wait_ge(act_s.sem, act_s.at(f"proj{CW - 1}_1", c - 1))
                for w in range(CW):
                    nc.tensor.matmul(flat[:, w, :], sums_t[:, w, :], w_msg[:, 0, :], start=True, stop=False)
                    nc.tensor.matmul(flat[:, w, :], sums_t[:, CW + w, :], w_msg[:, 1, :], start=False, stop=False)
                    mm = nc.tensor.matmul(flat[:, w, :], sums_t[0:D_EA64, 2 * CW + w, :], w_edge[:, :], start=False, stop=True)
                mm.then_inc(pe_s.sem, 1)
                pe.wait_ge(dve_s.sem, dve_s.at("a_bias", c))
                for w in range(CW):
                    for kc in range(2):
                        mm = nc.tensor.transpose(turn[:, kc * CW + w, :], h[:, w, kc * P:(kc + 1) * P], m.ident[:, :])
                mm.then_inc(pe_s.sem, 1)
                for l in range(3):
                    pe.wait_ge(act_s.sem, act_s.at("h_t" if l == 0 else f"mlp{l - 1}", c))
                    if l:
                        pe.wait_ge(dve_s.sem, dve_s.at(f"skip{l - 1}", c))
                    for f in range(2):
                        for half in range(2):
                            for kc in range(2):
                                mm = nc.tensor.matmul(mlp_ps[:, 2 * f + half, :], w_mlp[l][:, kc, f * P:(f + 1) * P],
                                                      h_t[:, kc, half * CW * P // 2:(half + 1) * CW * P // 2], start=(kc == 0), stop=(kc == 1))
                    mm.then_inc(pe_s.sem, 1)
                pe.wait_ge(dve_s.sem, dve_s.at("skip2", c))
                for w in range(CW):
                    for kc in range(2):
                        mm = nc.tensor.transpose(flat[:, w, kc * P:(kc + 1) * P], h_t[:, kc, w * P:(w + 1) * P], m.ident[:, :])
                mm.then_inc(pe_s.sem, 1)
                pe.wait_ge(dve_s.sem, dve_s.at("c_normed", c))
                for w in range(CW):
                    for kc in range(2):
                        mm = nc.tensor.transpose(turn[:, kc * CW + w, :], h[:, w, kc * P:(kc + 1) * P], m.ident[:, :])
                mm.then_inc(pe_s.sem, 1)
                pe.wait_ge(act_s.sem, act_s.at("x_t", c))
                project_linear(pe, pe_s, lambda kc, w: x_t[:, kc * CW + w, :], w_lin, 2, H, turn)
                project(pe, pe_s, act_s, c, lambda kc, w: x_t[:, kc * CW + w, :], [pieces(w_l, 2, 0, 512), pieces(w_r, 2, 0, 512)], None, ring, None)

        @block.scalar
        def _(act):
            act.sem_inc(act_s.sem, act_s.start)
            act.sem_inc(stored, 16)
            act.wait_ge(weights_in, 16 * n_weights)
            with act.Fori(0, CHUNKS) as c:
                act.wait_ge(pe_s.sem, pe_s.at("sums_t", c))
                nc.scalar.copy(sums_t[:, 0:2 * CW, :], turn[:, 0:2 * CW, :])
                nc.scalar.copy(sums_t[0:D_EA64, 2 * CW:3 * CW, :], turn[0:D_EA64, 2 * CW:3 * CW, :]).then_inc(act_s.sem, 1)
                standard_deviation(act, dve_s, act_s, c, "a", nb)
                act.wait_ge(pe_s.sem, pe_s.at("h_t", c))
                nc.scalar.copy(h_t[:, :, :].rearrange("p k (w e) -> p (k w) e", e=P), turn[:, 0:2 * CW, :]).then_inc(act_s.sem, 1)
                for l in range(3):
                    act.wait_ge(pe_s.sem, pe_s.at(f"mlp{l}", c))
                    if l:
                        act.wait_ge(dve_s.sem, dve_s.at(f"skip{l - 1}", c))
                    for f in range(2):
                        ins = nc.scalar.activation(y[:, f, :].rearrange("p (b e) -> p b e", b=2), mlp_ps[:, 2 * f:2 * f + 2, :],
                                                   ACT.Relu if l < 2 else ACT.Identity, bias=b_mlp[l][:, f:f + 1])
                    ins.then_inc(act_s.sem, 1)
                standard_deviation(act, dve_s, act_s, c, "b", nb)
                standard_deviation(act, dve_s, act_s, c, "c", nb)
                act.wait_ge(pe_s.sem, pe_s.at("x_t", c))
                nc.scalar.copy(x_t[:, :, :], turn[:, 0:2 * CW, :]).then_inc(act_s.sem, 1)
                act.wait_ge(stored, 16 * (c + 1))
                keep_linear(act, pe_s, act_s, c, turn, stage, own_lin, 512, H)
                for w in range(CW):
                    act.wait_ge(pe_s.sem, pe_s.at(f"proj{w}_0", c))
                    nc.scalar.copy(stage[:, w, 0:512], ring[:, (2 * w) % 3, :]).then_inc(act_s.sem, 1)
                    act.wait_ge(pe_s.sem, pe_s.at(f"proj{w}_1", c))
                    nc.scalar.copy(own[:, bass.ds(c * CW + w, 1), :].rearrange("p a n -> p (a n)"), ring[:, (2 * w + 1) % 3, :]).then_inc(act_s.sem, 1)

        @block.vector
        def _(dve):
            dve.sem_inc(dve_s.sem, dve_s.start)
            dve.wait_ge(weights_in, 16 * n_weights)
            linear_weights(dve, w_lin, (w_l, w_r), m.att["a1"], H, C, lin_ready)
            with dve.Fori(0, CHUNKS) as c:
                def link(name, ins):
                    ins.then_inc(dve_s.sem, 1)
                    dve.wait_ge(dve_s.sem, dve_s.at(name, c))

                x = m.xs[:, bass.ds(c * CW, CW), :]
                dve.wait_ge(pe_s.sem, pe_s.at("x_t", c - 1))
                dve.wait_ge(pe_s.sem, pe_s.at("msg", c))
                link("h", nc.vector.scalar_tensor_tensor(h[:, :, :], flat, 0.0, x, ALU.max, ALU.add))
                layer_norm(dve, link, act_s, c, "a", h, h, nb, 1e-6)
                link("a_scale", nc.vector.tensor_tensor(h[:, :, :], h[:, :, :], over_windows(rows["ln_aggr_scale"][:, :]), ALU.mult))
                link("a_bias", nc.vector.tensor_tensor(h[:, :, :], h[:, :, :], over_windows(rows["ln_aggr_bias"][:, :]), ALU.add))
                for l in range(3):
                    dve.wait_ge(act_s.sem, act_s.at(f"mlp{l}", c))
                    link(f"skip{l}", nc.vector.tensor_tensor(h_t[:, :, :], h_t[:, :, :], y[:, :, :], ALU.add))
                dve.wait_ge(pe_s.sem, pe_s.at("out", c))
                link("r", nc.vector.tensor_tensor(h[:, :, :], flat, x, ALU.add))
                layer_norm(dve, link, act_s, c, "b", h, h, nb, 1e-6)
                link("b_scale", nc.vector.tensor_tensor(h[:, :, :], h[:, :, :], over_windows(rows["ln_out_scale"][:, :]), ALU.mult))
                link("b_bias", nc.vector.tensor_tensor(h[:, :, :], h[:, :, :], over_windows(rows["ln_out_bias"][:, :]), ALU.add))
                link("xr", nc.vector.tensor_tensor(h[:, :, :], h[:, :, :], x, ALU.add))
                layer_norm(dve, link, act_s, c, "c", h, h, nb, 1e-5)
                settle(dve)
                link("kept", nc.vector.tensor_copy(x, h[:, :, :]))


def nodes_att(nc, m, tag, state, H, C, table, own, bias, w_out=None, w_in=None, b_in=None, own_scale=1.0, residual=True,
              next_att=None):
    LH = next_att[1] if next_att else 0
    W = H * C
    KI = W // P
    KX = KI if w_in else 4
    PX = P if w_in else C3
    widths = [v.shape[-1] for v in w_in] if w_in else [D, D]
    with ExitStack() as ctx:
        one = lambda n, s, d=F32: ctx.enter_context(nc.sbuf_tensor(f"{tag}_{n}", s, d))
        sem = lambda n: ctx.enter_context(nc.semaphore(f"{tag}_{n}"))
        y = one("y", [P, CW, W])
        inverse = one("inverse", [P, CW, H])
        x_t = one("x_t", [P, KX * CW, P])
        stage = one("stage", [P, CW, widths[0] + LH])
        if next_att:
            w_lin = LinearWeights(one, KI, LH, next_att[2])
        bias_row = one("bias", [P, bias.shape[-1]])
        ones_row = one("ones", [1, P])
        w_sb = [one(f"w{o}", [P, KI, n]) for o, n in enumerate(widths)] if w_in else [one("w3", [C3, 4, 2, C3])]
        b_sb = [one(f"b{o}", [1, n]) for o, n in enumerate(widths)] if b_in else []
        nb = NormBuffers(one)
        if w_out is not None:
            w_o, y_t = one("w_o", [P, KI, D]), one("y_t", [P, KI * CW, P])
        turn = ctx.enter_context(nc.psum_tensor(f"{tag}_turn", [P, 20, P], F32))
        ring = ctx.enter_context(nc.psum_tensor(f"{tag}_ring", [P, 3, 512], F32))
        flat = ring[:, :, :].rearrange("p b c -> p (b c)")[:, 0:CW * D].rearrange("p (w c) -> p w c", w=CW)
        weights_in, stored, ready, lin_ready = sem("weights"), sem("stored"), sem("ready"), sem("lin_ready")
        outs = 2 if w_in else 1
        first = ["y_t", "out"] if w_out is not None else []
        pe_s = Stages(sem("pe"), first + ["x_t"] + (["lin"] if next_att else []) + project_stages(outs))
        act_s = Stages(sem("act"), first[:1] + (["c_std"] if residual else []) + ["x_t"] + (["lin"] if next_att else []) + project_stages(outs))
        dve_s = Stages(sem("dve"), ["floor", "inverse", "mean", "biased"]
                       + (["xr"] + norm_stages("c") + ["kept"] if residual else ["relu"]))
        block = ctx.enter_context(nc.Block())
        n_in = 1 + (2 if w_in else 8) + len(b_sb) + (w_out is not None)

        @block.sync
        def _(sp):
            load = lambda to, of: sp.dma_start(to, of).then_inc(weights_in, 16)
            load(bias_row[:, :], row_everywhere(bias))
            if w_in:
                for o in range(2):
                    load(w_sb[o][:, :, :], w_in[o].rearrange("(k p) n -> p k n", p=P))
            else:
                for i in range(4):
                    load(w_sb[0][:, i, 0, :], m.inputs["L3_W_up1"] if i else m.inputs["L3_W_up0"])
                    load(w_sb[0][:, i, 1, :], m.inputs["L3_Wsc1"] if i else m.inputs["L3_Wsc0"])
            for o, t in enumerate(b_sb):
                load(t[:, :], b_in[o].rearrange("(a n) -> a n", a=1))
            if w_out is not None:
                load(w_o[:, :, :], w_out.rearrange("(k p) n -> p k n", p=P))
            with sp.Fori(0, CHUNKS) as c:
                sp.wait_ge(act_s.sem, act_s.at(f"proj{CW - 1}_{outs - 1}", c))
                sp.dma_start(table[bass.ds(c * CW * P, CW * P), :].rearrange("(w p) n -> p w n", p=P), stage[:, :, :]).then_inc(stored, 16)
            sp.wait_ge(stored, 16 * (CHUNKS + 1))

        @block.gpsimd
        def _(pool):
            nc.gpsimd.memset(ones_row[:, :], 1.0).then_inc(ready, 1)

        @block.tensor
        def _(pe):
            pe.sem_inc(pe_s.sem, pe_s.start)
            pe.wait_ge(weights_in, 16 * n_in)
            pe.wait_ge(ready, 1)
            if next_att:
                pe.wait_ge(lin_ready, 2 * KI * LH)
            with pe.Fori(0, CHUNKS) as c:
                if w_out is not None:
                    pe.wait_ge(dve_s.sem, dve_s.at("mean", c))
                    pe.wait_ge(act_s.sem, act_s.at("x_t", c - 1))
                    for w in range(CW):
                        for kc in range(KI):
                            mm = nc.tensor.transpose(turn[:, kc * CW + w, :], y[:, w, kc * P:(kc + 1) * P], m.ident[:, :])
                    mm.then_inc(pe_s.sem, 1)
                    pe.wait_ge(act_s.sem, act_s.at("y_t", c))
                    pe.wait_ge(act_s.sem, act_s.at(f"proj{CW - 1}_{outs - 1}", c - 1))
                    for w in range(CW):
                        for kc in range(KI):
                            mm = nc.tensor.matmul(flat[:, w, :], y_t[:, kc * CW + w, :], w_o[:, kc, :], start=(kc == 0), stop=(kc == KI - 1))
                    mm.then_inc(pe_s.sem, 1)
                pe.wait_ge(dve_s.sem, dve_s.at("c_normed" if residual else "relu", c))
                pe.wait_ge(act_s.sem, act_s.at("lin" if next_att else "x_t", c - 1))
                settle(pe)
                for w in range(CW):
                    for kc in range(KX):
                        if w_in:
                            piece = y[:, w, kc * P:(kc + 1) * P]
                        else:
                            piece = y[:, w, 0:C3] if kc == 0 else y[:, w, C3 + kc - 1:D:3]
                        mm = nc.tensor.transpose(turn[0:PX, kc * CW + w, :], piece, m.ident[:, :])
                mm.then_inc(pe_s.sem, 1)
                pe.wait_ge(act_s.sem, act_s.at("x_t", c))
                pe.wait_ge(act_s.sem, act_s.at(f"proj{CW - 1}_{outs - 1}", c - 1))
                if next_att:
                    project_linear(pe, pe_s, lambda kc, w: x_t[:, kc * CW + w, :], w_lin, KI, LH, turn)
                if w_in:
                    project(pe, pe_s, act_s, c, lambda kc, w: x_t[:, kc * CW + w, :],
                            [pieces(w_sb[o], KI, 0, widths[o]) for o in range(2)], [b[:, :] for b in b_sb], ring, ones_row[:, :])
                else:
                    for w in range(CW):
                        if w >= 3:
                            pe.wait_ge(act_s.sem, act_s.at(f"proj{w - 3}_0", c))
                        for i in range(4):
                            mm = nc.tensor.matmul(ring[:, w % 3, i * P:(i + 1) * P], x_t[0:C3, i * CW + w, :],
                                                  w_sb[0][:, i, :, :].rearrange("p t c -> p (t c)"), start=True, stop=True)
                        mm.then_inc(pe_s.sem, 1)

        @block.scalar
        def _(act):
            act.sem_inc(act_s.sem, act_s.start)
            act.sem_inc(stored, 16)
            with act.Fori(0, CHUNKS) as c:
                if w_out is not None:
                    act.wait_ge(pe_s.sem, pe_s.at("y_t", c))
                    nc.scalar.copy(y_t[:, :, :], turn[:, 0:KI * CW, :]).then_inc(act_s.sem, 1)
                if residual:
                    standard_deviation(act, dve_s, act_s, c, "c", nb)
                act.wait_ge(pe_s.sem, pe_s.at("x_t", c))
                nc.scalar.copy(x_t[0:PX, :, :], turn[0:PX, 0:KX * CW, :]).then_inc(act_s.sem, 1)
                act.wait_ge(stored, 16 * (c + 1))
                if next_att:
                    keep_linear(act, pe_s, act_s, c, turn, stage, next_att[3], widths[0], LH)
                for w in range(CW):
                    to_own = own[:, bass.ds(c * CW + w, 1), :].rearrange("p a n -> p (a n)")
                    act.wait_ge(pe_s.sem, pe_s.at(f"proj{w}_0", c))
                    if w_in:
                        nc.scalar.copy(stage[:, w, 0:widths[0]], ring[:, (2 * w) % 3, 0:widths[0]]).then_inc(act_s.sem, 1)
                        act.wait_ge(pe_s.sem, pe_s.at(f"proj{w}_1", c))
                        nc.scalar.mul(to_own, ring[:, (2 * w + 1) % 3, 0:widths[1]], own_scale).then_inc(act_s.sem, 1)
                    else:
                        both = ring[:, w % 3, :].rearrange("p (i t c) -> p i t c", i=4, t=2)
                        nc.scalar.copy(stage[:, w, :].rearrange("p (i c) -> p i c", i=4), both[:, :, 0, :])
                        nc.scalar.copy(to_own.rearrange("p (i c) -> p i c", i=4), both[:, :, 1, :]).then_inc(act_s.sem, 1)

        @block.vector
        def _(dve):
            dve.sem_inc(dve_s.sem, dve_s.start)
            dve.wait_ge(weights_in, 16 * n_in)
            if next_att:
                linear_weights(dve, w_lin, w_sb, *next_att[:3], lin_ready)
            with dve.Fori(0, CHUNKS) as c:
                def link(name, ins):
                    ins.then_inc(dve_s.sem, 1)
                    dve.wait_ge(dve_s.sem, dve_s.at(name, c))

                dve.wait_ge(pe_s.sem, pe_s.at("x_t", c - 1))
                weight = state.weight[:, bass.ds(c * CW, CW), :]
                link("floor", nc.vector.tensor_scalar(inverse[:, :, :], weight, 1e-30, None, ALU.max))
                link("inverse", nc.vector.reciprocal(inverse[:, :, :], inverse[:, :, :]))
                for w in range(CW):
                    ins = nc.vector.tensor_tensor(
                        y[:, w, :].rearrange("p (h n) -> p h n", h=H),
                        state.total[:, bass.ds(c * CW + w, 1), :].rearrange("p a (h n) -> p (a h) n", h=H),
                        inverse[:, w, :].unsqueeze(2).broadcast_to([P, H, C]), ALU.mult)
                link("mean", ins)
                if w_out is not None:
                    dve.wait_ge(pe_s.sem, pe_s.at("out", c))
                    link("biased", nc.vector.tensor_tensor(y[:, :, :], flat, over_windows(bias_row[:, :]), ALU.add))
                else:
                    link("biased", nc.vector.tensor_tensor(y[:, :, :], y[:, :, :], over_windows(bias_row[:, :]), ALU.add))
                if residual:
                    x = m.xs[:, bass.ds(c * CW, CW), :]
                    link("xr", nc.vector.tensor_tensor(y[:, :, :], y[:, :, :], x, ALU.add))
                    layer_norm(dve, link, act_s, c, "c", y, y, nb, 1e-5)
                    settle(dve)
                    link("kept", nc.vector.tensor_copy(x, y[:, :, :]))
                else:
                    link("relu", nc.vector.tensor_scalar(y[:, :, :], y[:, :, :], 0.0, None, ALU.max))


def reload_steps(nc, o):
    with ExitStack() as ctx:
        listed = ctx.enter_context(nc.semaphore("relisted"))
        block = ctx.enter_context(nc.Block())

        @block.sync
        def _(sp):
            sp.dma_start(o.gk[:, :], o.gk_d.rearrange("(a k) -> a k", a=1)).then_inc(listed, 16)
            sp.dma_start(o.wk[:, :], o.wk_d.rearrange("(a k) -> a k", a=1)).then_inc(listed, 16)
            sp.wait_ge(listed, 32)


def edge_messages(nc, m, o, table, total):
    with ExitStack() as ctx:
        one = lambda n, s, d=F32: ctx.enter_context(nc.sbuf_tensor(f"e3_{n}", s, d))
        two = lambda n, s, d=F32: [one(f"{n}{b}", s, d) for b in range(2)]
        bank = lambda n, w=512: ctx.enter_context(nc.psum_tensor(f"e3_{n}", [P, w], F32))
        sem = lambda n: ctx.enter_context(nc.semaphore(f"e3_{n}"))
        idx, dst_c = two("idx", [P, J], I32), two("dst_c", [P, J])
        sh, rbf = two("sh", [P, J, 4]), two("rbf", [D_EA16, GE])
        rel, hot = two("rel", [P, J]), two("hot", [P, J, P])
        rows = two("rows", [P, J, D])
        by_sh = two("by_sh", [P, J, 3, C3])
        dot = two("dot", [P, J, C3])
        by_sh0 = two("by_sh0", [P, J, 4, C3])
        scalar_part, x0_part = one("scalar_part", [P, J, C3]), one("x0_part", [P, J, C3])
        vector_part = one("vector_part", [P, J, 3, C3])
        message = two("message", [P, J, 4, C3])
        m1, m2, m3, m4 = one("m1", [D_EA16, C3]), one("m2", [C3, C3]), one("m3", [C3, C3]), one("m4", [C3, D])
        r = [one(f"r{l}", [C3, GE]) for l in range(3)]
        z = [bank(f"z{l}") for l in range(2)]
        tp = [bank(f"tp{b}", J * D) for b in range(2)]
        sums = [bank(f"sums{b}") for b in range(2)]
        weights_in, zeroed = sem("weights"), sem("zeroed")
        loaded = [sem(f"loaded{b}") for b in range(2)]
        gathered = [sem(f"gathered{b}") for b in range(2)]
        pe_f, act_f = Stages(sem("mlp"), ["z0", "z1", "z2", "tp"]), Stages(sem("silu"), ["r0", "r1", "r2"])
        pe_b = Stages(sem("sums"), ["sum"])
        dve_f = Stages(sem("dve_front"), ["rel", "hot", "by_sh0", "by_sh", "dot2", "dot"])
        dve_b = Stages(sem("dve_back"), ["tp0", "tp3", "m0", "x0_part", "tp2", "tp1", "m1", "merged"])
        block = ctx.enter_context(nc.Block())

        @block.sync
        def _(sp):
            for to, of in ((m1, m.inputs["L3_M1"]), (m2, m.inputs["L3_M2"]), (m3, m.inputs["L3_M3"]), (m4, m.inputs["L3_M4"])):
                sp.dma_start(to[:, :], of).then_inc(weights_in, 16)

            def front(k, i, b):
                g = group_of(sp, o, k)
                part = bass.ds(g * GE, GE)
                sp.wait_ge(dve_b.sem, dve_b.at("m1", k - 2))
                settle(sp)
                sp.wait_ge(pe_f.sem, pe_f.at("z0", k - 2))
                settle(sp)
                sp.dma_start(idx[b][:, :], o.other[part].rearrange("(p j) -> p j", j=J)).then_inc(loaded[b], 16)
                sp.dma_start(dst_c[b][:, :], o.key_f[part].rearrange("(p j) -> p j", j=J)).then_inc(loaded[b], 16)
                sp.dma_start(sh[b][:, :, :], m.inputs["ea4"][part, :].rearrange("(p j) c -> p j c", j=J)).then_inc(loaded[b], 16)
                sp.dma_start(rbf[b][:, :], m.inputs["rbf_t"][bass.ds(g * D_EA16, D_EA16), :]).then_inc(loaded[b], 16)
            drive(sp, o, front)

        @block.gpsimd
        def _(pool):
            nc.gpsimd.memset(total[:, :, :], 0.0).then_inc(zeroed, 1)

            def front(k, i, b):
                pool.wait_ge(loaded[b], 64 * (i + 1))
                settle(pool)
                for j in range(J):
                    pool.indirect_dma_start(
                        out=rows[b][:, j, :], out_offset=None, in_=table,
                        in_offset=bass.IndirectOffsetOnAxis(ap=idx[b][:, j:j + 1], axis=0)).then_inc(gathered[b], 16)
            drive(pool, o, front)

        @block.tensor
        def _(pe):
            for s in (pe_f, pe_b):
                pe.sem_inc(s.sem, s.start)
            pe.wait_ge(weights_in, 64)

            def front(k, i, b):
                pe.wait_ge(loaded[b], 64 * (i + 1))
                pe.wait_ge(act_f.sem, act_f.at("r2", k - 1))
                nc.tensor.matmul(z[0][0:C3, :], m1[:, :], rbf[b][:, :], start=True, stop=True).then_inc(pe_f.sem, 1)
                pe.wait_ge(act_f.sem, act_f.at("r0", k))
                settle(pe)
                nc.tensor.matmul(z[1][0:C3, :], m2[:, :], r[0][:, :], start=True, stop=True).then_inc(pe_f.sem, 1)
                pe.wait_ge(act_f.sem, act_f.at("r1", k))
                settle(pe)
                nc.tensor.matmul(z[0][0:C3, :], m3[:, :], r[1][:, :], start=True, stop=True).then_inc(pe_f.sem, 1)
                pe.wait_ge(act_f.sem, act_f.at("r2", k))
                pe.wait_ge(dve_b.sem, dve_b.at("tp1", k - 2))
                for j in range(J):
                    mm = nc.tensor.matmul(tp[b][:, j * D:(j + 1) * D], r[2][:, j * P:(j + 1) * P], m4[:, :], start=True, stop=True)
                mm.then_inc(pe_f.sem, 1)

            def back(k, i, b):
                pe.wait_ge(dve_b.sem, dve_b.at("merged", k - 2))
                pe.wait_ge(dve_b.sem, dve_b.at("m1", k))
                for j in range(J):
                    mm = nc.tensor.matmul(sums[b][:, 0:D], hot[b][:, j, :], message[b][:, j, :, :].rearrange("p t c -> p (t c)"),
                                          start=(j == 0), stop=(j == J - 1))
                mm.then_inc(pe_b.sem, 1)
            drive(pe, o, front, back)

        @block.scalar
        def _(act):
            act.sem_inc(act_f.sem, act_f.start)

            def front(k, i, b):
                for l in range(3):
                    if l == 0:
                        act.wait_ge(pe_f.sem, pe_f.at("tp", k - 1))
                    act.wait_ge(pe_f.sem, pe_f.at(f"z{l}", k))
                    nc.scalar.activation(r[l][:, :], z[l % 2][0:C3, :], ACT.Silu).then_inc(act_f.sem, 1)
            drive(act, o, front, None)

        @block.vector
        def _(dve):
            for s in (dve_f, dve_b):
                dve.sem_inc(s.sem, s.start)
            dve.wait_ge(zeroed, 1)

            def front(k, i, b):
                def link(name, ins):
                    ins.then_inc(dve_f.sem, 1)
                    dve.wait_ge(dve_f.sem, dve_f.at(name, k))

                w = window_of(dve, o, k)
                dve.wait_ge(loaded[b], 64 * (i + 1))
                link("rel", nc.vector.tensor_scalar(rel[b][:, :], dst_c[b][:, :], m.base[:, bass.ds(w, 1)], None, ALU.subtract))
                dve.wait_ge(pe_b.sem, pe_b.at("sum", k - 2))
                for j in range(J):
                    ins = nc.vector.tensor_scalar(hot[b][:, j, :], m.iota[:, :], rel[b][:, j:j + 1], None, ALU.is_equal)
                ins.then_inc(dve_f.sem, 1)
                dve.wait_ge(gathered[b], 16 * J * (i + 1))
                x = rows[b][:, :, :].rearrange("p j (t c) -> p j t c", t=4)
                nc.vector.tensor_tensor(by_sh0[b][:, :, :, :].rearrange("p j t c -> p j (t c)"), rows[b][:, :, :],
                                        sh[b][:, :, 0:1].broadcast_to([P, J, D]), ALU.mult).then_inc(dve_f.sem, 1)
                link("by_sh", nc.vector.tensor_tensor(by_sh[b][:, :, :, :], x[:, :, 1:4, :], sh[b][:, :, 1:4].unsqueeze(3).broadcast_to([P, J, 3, C3]), ALU.mult))
                link("dot2", nc.vector.tensor_tensor(dot[b][:, :, :], by_sh[b][:, :, 0, :], by_sh[b][:, :, 1, :], ALU.add))
                nc.vector.tensor_tensor(dot[b][:, :, :], dot[b][:, :, :], by_sh[b][:, :, 2, :], ALU.add).then_inc(dve_f.sem, 1)

            def back(k, i, b):
                def link(name, ins):
                    ins.then_inc(dve_b.sem, 1)
                    dve.wait_ge(dve_b.sem, dve_b.at(name, k))

                w = window_of(dve, o, k)
                x = rows[b][:, :, :].rearrange("p j (t c) -> p j t c", t=4)
                t = tp[b][:, :].rearrange("p (j t c) -> p j t c", j=J, t=4)
                dve.wait_ge(dve_f.sem, dve_f.at("dot", k))
                dve.wait_ge(pe_f.sem, pe_f.at("tp", k))
                dve.wait_ge(pe_b.sem, pe_b.at("sum", k - 2))
                nc.vector.tensor_tensor(message[b][:, :, 0, :], t[:, :, 0, :], by_sh0[b][:, :, 0, :], ALU.mult).then_inc(dve_b.sem, 1)
                link("tp3", nc.vector.scalar_tensor_tensor(scalar_part[:, :, :], t[:, :, 3, :], float(3 ** -0.5), dot[b][:, :, :], ALU.mult, ALU.mult))
                nc.vector.tensor_tensor(message[b][:, :, 0, :], message[b][:, :, 0, :], scalar_part[:, :, :], ALU.add).then_inc(dve_b.sem, 1)
                link("x0_part", nc.vector.tensor_tensor(x0_part[:, :, :], t[:, :, 1, :], x[:, :, 0, :], ALU.mult))
                nc.vector.tensor_tensor(message[b][:, :, 1:4, :], by_sh0[b][:, :, 1:4, :],
                                        t[:, :, 2:3, :].broadcast_to([P, J, 3, C3]), ALU.mult).then_inc(dve_b.sem, 1)
                link("tp1", nc.vector.tensor_tensor(vector_part[:, :, :, :], x0_part[:, :, :].unsqueeze(2).broadcast_to([P, J, 3, C3]),
                                                    sh[b][:, :, 1:4].unsqueeze(3).broadcast_to([P, J, 3, C3]), ALU.mult))
                nc.vector.tensor_tensor(message[b][:, :, 1:4, :], message[b][:, :, 1:4, :], vector_part[:, :, :, :], ALU.add).then_inc(dve_b.sem, 1)
                dve.wait_ge(pe_b.sem, pe_b.at("sum", k))
                dve.wait_ge(dve_b.sem, dve_b.at("merged", k - 1))
                a = total[:, bass.ds(w, 1), :].rearrange("p a c -> p (a c)")
                nc.vector.tensor_tensor(a, a, sums[b][:, 0:D], ALU.add).then_inc(dve_b.sem, 1)
            drive(dve, o, front, back)


def nodes_3(nc, m, total, own, out):
    with ExitStack() as ctx:
        one = lambda n, s, d=F32: ctx.enter_context(nc.sbuf_tensor(f"n4_{n}", s, d))
        sem = lambda n: ctx.enter_context(nc.semaphore(f"n4_{n}"))
        rows = {n: one(n, [P, C3]) for n in ("gamma0", "beta0", "gamma1")}
        coef = one("coef", [P, 9, C3])
        w_lin, w_b = one("w_lin", [C3, 4, C3]), one("w_b", [C3, 4, C3])
        weights_in = sem("weights")

        with ExitStack() as first:
            tmp = lambda n, s: first.enter_context(nc.sbuf_tensor(f"n4_{n}", s, F32))
            turned = tmp("turned", [C3, 4 * CW, P])
            a, b = tmp("a", [P, CW, 4, C3]), tmp("b", [P, CW, 4, C3])
            squares = tmp("squares", [P, CW, 3, C3])
            vv, aa, part, poly0, poly1 = (tmp(n, [P, CW, C3]) for n in ("vv", "aa", "part", "poly0", "poly1"))
            turn = first.enter_context(nc.psum_tensor("n4_turn", [P, 20, P], F32))
            ring = first.enter_context(nc.psum_tensor("n4_ring", [P, 1536], F32))
            flat = ring[:, 0:CW * D].rearrange("p (w i c) -> p w i c", w=CW, i=4)
            pe_s = Stages(sem("pe"), ["msg_t", "a", "b_t", "o"])
            act_s = Stages(sem("act"), ["msg", "msg_t", "a", "b_t"])
            steps = ["aa", "sq", "vv2", "vv", "w1", "w0", "w3", "+w3", "w4", "+w4", "poly0", "w2", "b0",
                     "w6", "w5", "w7", "+w7", "w8", "+w8", "b1", "o"]
            dve_s = Stages(sem("dve"), steps)
            block = first.enter_context(nc.Block())

            @block.sync
            def _(sp):
                load = lambda to, of: sp.dma_start(to, of).then_inc(weights_in, 16)
                for n, of in (("gamma0", m.inputs["L3_gamma0"]), ("beta0", m.inputs["L3_beta0"]), ("gamma1", m.inputs["L3_gamma1"])):
                    load(rows[n][:, :], row_everywhere(of))
                load(coef[:, :, :].rearrange("p t c -> p (t c)"), row_everywhere(m.inputs["L3_Wc"]))
                for i in range(4):
                    load(w_lin[:, i, :], m.inputs["L3_W_lin1"] if i else m.inputs["L3_W_lin0"])
                    load(w_b[:, i, :], m.inputs["L3_WB1"] if i else m.inputs["L3_WB0"])
                sp.wait_ge(weights_in, 12 * 16)

            @block.tensor
            def _(pe):
                pe.sem_inc(pe_s.sem, pe_s.start)
                pe.wait_ge(weights_in, 12 * 16)
                with pe.Fori(0, CHUNKS) as c:
                    for phase in range(2):
                        if phase:
                            pe.wait_ge(dve_s.sem, dve_s.at("b1", c))
                        else:
                            pe.wait_ge(act_s.sem, act_s.at("msg", c))
                        settle(pe)
                        for i in range(4):
                            for w in range(CW):
                                mm = nc.tensor.transpose(turn[0:C3, i * CW + w, :], (b if phase else a)[:, w, i, :], m.ident[:, :])
                        mm.then_inc(pe_s.sem, 1)
                        pe.wait_ge(act_s.sem, act_s.at("b_t" if phase else "msg_t", c))
                        if phase == 0:
                            pe.wait_ge(dve_s.sem, dve_s.at("o", c - 1))
                        for w in range(CW):
                            for i in range(4):
                                mm = nc.tensor.matmul(flat[:, w, i, :], turned[:, i * CW + w, :], (w_b if phase else w_lin)[:, i, :], start=True, stop=True)
                        mm.then_inc(pe_s.sem, 1)

            @block.scalar
            def _(act):
                act.sem_inc(act_s.sem, act_s.start)
                with act.Fori(0, CHUNKS) as c:
                    act.wait_ge(dve_s.sem, dve_s.at("b1", c - 1))
                    nc.scalar.copy(a[:, :, :, :].rearrange("p w i c -> p w (i c)"), total[:, bass.ds(c * CW, CW), :]).then_inc(act_s.sem, 1)
                    act.wait_ge(pe_s.sem, pe_s.at("msg_t", c))
                    nc.scalar.copy(turned[:, :, :], turn[0:C3, :, :]).then_inc(act_s.sem, 1)
                    act.wait_ge(pe_s.sem, pe_s.at("a", c))
                    nc.scalar.copy(a[:, :, :, :], flat).then_inc(act_s.sem, 1)
                    act.wait_ge(pe_s.sem, pe_s.at("b_t", c))
                    nc.scalar.copy(turned[:, :, :], turn[0:C3, :, :]).then_inc(act_s.sem, 1)

            @block.vector
            def _(dve):
                dve.sem_inc(dve_s.sem, dve_s.start)
                dve.wait_ge(weights_in, 12 * 16)
                with dve.Fori(0, CHUNKS) as c:
                    def link(name, ins):
                        ins.then_inc(dve_s.sem, 1)
                        dve.wait_ge(dve_s.sem, dve_s.at(name, c))

                    tt = nc.vector.tensor_tensor
                    row = lambda t: over_windows(coef[:, t, :])
                    a0 = a[:, :, 0, :]
                    dve.wait_ge(act_s.sem, act_s.at("a", c))
                    link("aa", tt(aa[:, :, :], a0, a0, ALU.mult))
                    link("sq", tt(squares[:, :, :, :], a[:, :, 1:4, :], a[:, :, 1:4, :], ALU.mult))
                    link("vv2", tt(vv[:, :, :], squares[:, :, 0, :], squares[:, :, 1, :], ALU.add))
                    link("vv", tt(vv[:, :, :], vv[:, :, :], squares[:, :, 2, :], ALU.add))
                    link("w1", tt(poly0[:, :, :], a0, row(1), ALU.mult))
                    link("w0", tt(poly0[:, :, :], poly0[:, :, :], row(0), ALU.add))
                    for name, t, factor in (("w3", 3, aa), ("w4", 4, vv)):
                        link(name, tt(part[:, :, :], factor[:, :, :], row(t), ALU.mult))
                        link("+" + name, tt(poly0[:, :, :], poly0[:, :, :], part[:, :, :], ALU.add))
                    link("poly0", tt(poly0[:, :, :], poly0[:, :, :], a0, ALU.mult))
                    link("w2", tt(part[:, :, :], vv[:, :, :], row(2), ALU.mult))
                    link("b0", tt(b[:, :, 0, :], poly0[:, :, :], part[:, :, :], ALU.add))
                    link("w6", tt(poly1[:, :, :], a0, row(6), ALU.mult))
                    link("w5", tt(poly1[:, :, :], poly1[:, :, :], row(5), ALU.add))
                    for name, t, factor in (("w7", 7, aa), ("w8", 8, vv)):
                        link(name, tt(part[:, :, :], factor[:, :, :], row(t), ALU.mult))
                        link("+" + name, tt(poly1[:, :, :], poly1[:, :, :], part[:, :, :], ALU.add))
                    link("b1", tt(b[:, :, 1:4, :], a[:, :, 1:4, :], poly1[:, :, :].unsqueeze(2).broadcast_to([P, CW, 3, C3]), ALU.mult))
                    dve.wait_ge(pe_s.sem, pe_s.at("o", c))
                    chunk = bass.ds(c * CW, CW)
                    tt(total[:, chunk, :].rearrange("p w (i n) -> p w i n", i=4), flat, own[:, chunk, :].rearrange("p w (i n) -> p w i n", i=4),
                       ALU.add).then_inc(dve_s.sem, 1)

        with ExitStack() as second:
            tmp = lambda n, s: second.enter_context(nc.sbuf_tensor(f"n4_{n}", s, F32))
            ones, real = tmp("ones", [P, P]), tmp("real", [P, P])
            mean, moment = tmp("mean", [P, C3]), tmp("moment", [P, 2, C3])
            root, scale = tmp("root", [P, 2, C3]), tmp("scale", [P, 2, C3])
            squares = tmp("squares_o", [P, CW, D])
            y = [tmp(f"y{i}", [P, CW, D]) for i in range(2)]
            nb = NormBuffers(tmp)
            mean_ps = second.enter_context(nc.psum_tensor("n4_mean_ps", [P, 512], F32))
            square_ps = second.enter_context(nc.psum_tensor("n4_square_ps", [P, 512], F32))
            ready, stat, pe_done, act_done = sem("ready"), sem("stat"), sem("stat_pe"), sem("stat_act")
            squared, used = Stages(sem("squared"), ["centred", "square"]), sem("used")
            stored = sem("stored")
            act_s = Stages(sem("norm_act"), ["c_std"])
            dve_s = Stages(sem("norm_dve"), ["scaled0", "scaled1", "shifted", "xr"] + norm_stages("c"))
            block = second.enter_context(nc.Block())

            @block.sync
            def _(sp):
                def store(c, i):
                    sp.wait_ge(dve_s.sem, dve_s.at("c_normed", c))
                    settle(sp)
                    sp.dma_start(out[bass.ds(c * CW * P, CW * P), :].rearrange("(w p) d -> p w d", p=P), y[i][:, :, :]).then_inc(stored, 16)

                with sp.Fori(0, CHUNKS // 2) as h:
                    for i in range(2):
                        store(2 * h + i, i)
                store(CHUNKS - 1, 0)
                sp.wait_ge(stored, 16 * (CHUNKS + 1))

            @block.gpsimd
            def _(pool):
                nc.gpsimd.memset(ones[:, :], 1.0).then_inc(ready, 1)

            @block.tensor
            def _(pe):
                pe.wait_ge(stat, 1)
                nc.tensor.matmul(mean_ps[:, 0:C3], real[:, :], total[:, WN - 1, 0:C3], start=True, stop=True)
                with pe.Fori(0, WN - 2) as w:
                    nc.tensor.matmul(mean_ps[:, 0:C3], ones[:, :], total[:, bass.ds(w, 1), 0:C3].rearrange("p a c -> p (a c)"),
                                     start=False, stop=True, skip_group_check=True)
                nc.tensor.matmul(mean_ps[:, 0:C3], ones[:, :], total[:, WN - 2, 0:C3], start=False, stop=True, skip_group_check=True).then_inc(pe_done, 1)

                def squares_of(c, first=False, last=False):
                    pe.wait_ge(squared.sem, squared.at("square", c))
                    for w in range(CW):
                        mm = nc.tensor.matmul(square_ps[:, 0:D], (real if last and w == CW - 1 else ones)[:, :], squares[:, w, :],
                                              start=first and w == 0, stop=True, skip_group_check=True)
                    mm.then_inc(used, 1)

                squares_of(0, first=True)
                with pe.Fori(1, CHUNKS - 1) as c:
                    squares_of(c)
                squares_of(CHUNKS - 1, last=True)

            @block.scalar
            def _(act):
                act.sem_inc(act_s.sem, act_s.start)
                act.wait_ge(stat, 5)
                nc.scalar.activation(root[:, :, :], moment[:, :, :], ACT.Sqrt).then_inc(act_done, 1)
                with act.Fori(0, CHUNKS) as c:
                    standard_deviation(act, dve_s, act_s, c, "c", nb)

            @block.vector
            def _(dve):
                n = [0]

                def stage(ins):
                    n[0] += 1
                    ins.then_inc(stat, 1)
                    dve.wait_ge(stat, n[0])

                dve.sem_inc(squared.sem, squared.start)
                dve.sem_inc(dve_s.sem, dve_s.start)
                dve.sem_inc(used, 1)
                dve.sem_inc(stored, 16)
                dve.wait_ge(ready, 1)
                stage(nc.vector.tensor_scalar(real[:, :], m.node[:, 0:1].broadcast_to([P, P]), float(N_NODES - (WN - 1) * P), None, ALU.is_lt))
                dve.wait_ge(pe_done, 1)
                stage(nc.vector.tensor_scalar(mean[:, :], mean_ps[:, 0:C3], 1.0 / N_NODES, None, ALU.mult))
                with dve.Fori(0, CHUNKS) as c:
                    centred = total[:, bass.ds(c * CW, CW), 0:C3]
                    nc.vector.tensor_tensor(centred, centred, over_windows(mean[:, :]), ALU.subtract).then_inc(squared.sem, 1)
                    dve.wait_ge(squared.sem, squared.at("centred", c))
                    dve.wait_ge(used, c + 1)
                    chunk = total[:, bass.ds(c * CW, CW), :]
                    nc.vector.tensor_tensor(squares[:, :, :], chunk, chunk, ALU.mult).then_inc(squared.sem, 1)
                dve.wait_ge(used, CHUNKS + 1)
                eps = 1e-5
                stage(nc.vector.tensor_scalar(moment[:, 0, :], square_ps[:, 0:C3], 1.0 / N_NODES, eps, ALU.mult, ALU.add))
                stage(nc.vector.tensor_reduce(moment[:, 1, :], square_ps[:, C3:D].rearrange("p (x c) -> p c x", x=3), AX.X, ALU.add))
                stage(nc.vector.tensor_scalar(moment[:, 1, :], moment[:, 1, :], 1.0 / (3.0 * N_NODES), eps, ALU.mult, ALU.add))
                dve.wait_ge(act_done, 1)
                stage(nc.vector.reciprocal(scale[:, :, :], root[:, :, :]))
                stage(nc.vector.tensor_tensor(scale[:, 0, :], scale[:, 0, :], rows["gamma0"][:, :], ALU.mult))
                stage(nc.vector.tensor_tensor(scale[:, 1, :], scale[:, 1, :], rows["gamma1"][:, :], ALU.mult))

                def finish(c, i, before):
                    def link(name, ins):
                        ins.then_inc(dve_s.sem, 1)
                        dve.wait_ge(dve_s.sem, dve_s.at(name, c))

                    chunk = bass.ds(c * CW, CW)
                    dve.wait_ge(stored, before)
                    nc.vector.tensor_tensor(y[i][:, :, 0:C3], total[:, chunk, 0:C3], over_windows(scale[:, 0, :]), ALU.mult).then_inc(dve_s.sem, 1)
                    link("scaled1", nc.vector.tensor_tensor(y[i][:, :, C3:D].rearrange("p w (c x) -> p w x c", x=3),
                                                            total[:, chunk, C3:D].rearrange("p w (x c) -> p w x c", x=3),
                                                            scale[:, 1:2, :].unsqueeze(1).broadcast_to([P, CW, 3, C3]), ALU.mult))
                    link("shifted", nc.vector.tensor_tensor(y[i][:, :, 0:C3], y[i][:, :, 0:C3], over_windows(rows["beta0"][:, :]), ALU.add))
                    link("xr", nc.vector.tensor_tensor(y[i][:, :, :], y[i][:, :, :], m.xs[:, chunk, :], ALU.add))
                    layer_norm(dve, link, act_s, c, "c", y[i], y[i], nb, 1e-5)

                with dve.Fori(0, CHUNKS // 2) as h:
                    for i in range(2):
                        finish(2 * h + i, i, 16 * 2 * h + 16)
                finish(CHUNKS - 1, 0, 16 * CHUNKS)
def build(nc, a, out):
    m = Model(a)
    dram = lambda n, s, d=F32: nc.dram_tensor(n, s, d, kind="Internal").ap()
    m.row_cols, m.row_f, m.row_lo = dram("row_cols", (EP, 3)), dram("row_f", (EP,)), dram("row_lo", (EP,))
    m.sorted, m.row_sorted, m.col_sorted = dram("sorted", (EP, 2), I32), dram("row_sorted", (EP,), I32), dram("col_sorted", (EP,), I32)
    by_dst, by_row = Order(dram, "by_dst", m.inputs["dst"], m.inputs["src"]), Order(dram, "by_row", m.row_sorted, m.col_sorted)
    table_1, table_2 = dram("table_1", (NP, 512 + 4)), dram("table_2", (NP, 256 + 1))
    table_kv, table_up = dram("table_kv", (NP, 512)), dram("table_up", (NP, 256))
    with ExitStack() as ctx:
        sb = lambda n, s, d=F32: ctx.enter_context(nc.sbuf_tensor(n, s, d))
        m.ident, m.iota = sb("ident", [P, P]), sb("iota", [P, P])
        m.node, m.base = sb("node", [P, WX]), sb("base", [P, WX])
        for o in (by_dst, by_row):
            o.gk = sb("gk", [1, KMAX], I32) if o is by_dst else by_dst.gk
            o.wk = sb("wk", [1, KMAX], I32) if o is by_dst else by_dst.wk
            o.pairs = sb("pairs_by_dst" if o is by_dst else "pairs_by_row", [1, 1], I32)
        m.att = {"a1": sb("att1", [P, 512]), "a2": sb("att2", [P, 256])}
        build_steps(nc, m, by_dst, "d_")
        m.xs = sb("xs", [P, WN, D])
        load_nodes(nc, m)
        own = sb("own", [P, WX * 512])
        own_lin_all = sb("own_lin", [P, WX * 4])
        own_lin = lambda h: own_lin_all[:, 0:WX * h].rearrange("p (w h) -> p w h", h=h)
        own_of = lambda w: own[:, 0:WX * w].rearrange("p (w c) -> p w c", c=w)
        with ExitStack() as life:
            agg = life.enter_context(nc.sbuf_tensor("agg", [P, WX, D + D_EA64], F32))
            edge_sums(nc, m, by_dst, agg)
            nodes_0(nc, m, agg, table_1, own_of(512), own_lin(4), 4, 128)
        view = lambda t, w: t[:, 0:WX * w].rearrange("p (w c) -> p w c", c=w)
        with ExitStack() as life:
            of = lambda n, s, d=F32: life.enter_context(nc.sbuf_tensor(n, s, d))
            total = of("total", [P, WX * 512])
            weight, top = of("weight", [P, WX * 8]), of("top", [P, WX * 8])
            state = lambda w, h: State(view(total, w), view(weight, h), view(top, h))
            s = state(512, 4)
            attention(nc, m, by_dst, "a1", 4, 128, table_1, own_of(512), own_lin(4), s, dot=False)
            nodes_att(nc, m, "n1", s, 4, 128, table_2, own_of(256), m.inputs["L1_b1"], w_in=(m.inputs["L1_W2l"], m.inputs["L1_W2r"]), residual=False,
                      next_att=(m.att["a2"], 1, 256, own_lin(1)))
            s = state(256, 1)
            attention(nc, m, by_dst, "a2", 1, 256, table_2, own_of(256), own_lin(1), s, dot=False)
            nodes_att(nc, m, "n2", s, 1, 256, table_kv, own_of(256), m.inputs["L1_b2"], w_in=(m.inputs["L2_Wkv"], m.inputs["L2_Wq"]), b_in=(m.inputs["L2_bkv"], m.inputs["L2_bq"]),
                      own_scale=float(32 ** -0.5))
            s = state(256, 8)
            sort_edges(nc, m)
            build_steps(nc, m, by_row, "r_")
            attention(nc, m, by_row, "a3", 8, 32, table_kv, own_of(256), own_lin(1), s, dot=True)
            nodes_att(nc, m, "n3", s, 8, 32, table_up, own_of(256), m.inputs["L2_bo"], w_out=m.inputs["L2_Wo"])
        summed = sb("summed", [P, WX, D])
        reload_steps(nc, by_dst)
        edge_messages(nc, m, by_dst, table_up, summed)
        nodes_3(nc, m, summed, own_of(256), out)


def load_nodes(nc, m):
    with ExitStack() as ctx:
        loaded = ctx.enter_context(nc.semaphore("x_loaded"))
        block = ctx.enter_context(nc.Block())

        @block.sync
        def _(sp):
            sp.dma_start(m.xs[:, :, :], m.inputs["x"].rearrange("(w p) d -> p w d", p=P)).then_inc(loaded, 16)
            sp.dma_start(m.att["a1"][:, :], row_everywhere(m.inputs["L1_a1"])).then_inc(loaded, 16)
            sp.dma_start(m.att["a2"][:, :], row_everywhere(m.inputs["L1_a2"])).then_inc(loaded, 16)
            sp.wait_ge(loaded, 48)


def kernel(**inputs):
    import numpy as _np
    import concourse.bacc as _bacc
    from concourse.bass_utils import run_bass_kernel_spmd as _run

    raw = {k: _np.asarray(v) for k, v in inputs.items()}
    edges = EP - N_EDGES
    rbf = _np.pad(raw["edge_attr_16"], ((0, edges), (0, 0)))
    arrays = {
        "x": _np.pad(raw["x"], ((0, NP - N_NODES), (0, 0))),
        "src": _np.pad(raw["src"], (0, edges)),
        "dst": _np.pad(raw["dst"], (0, edges), constant_values=NP),
        "pair": _np.stack([_np.pad(raw["src"], (0, edges), constant_values=NP), _np.pad(raw["dst"], (0, edges))], axis=1),
        "ea64": _np.pad(raw["edge_attr_64"], ((0, edges), (0, 0))),
        "ea4": _np.pad(raw["edge_attr_4"], ((0, edges), (0, 0))),
        "rbf_t": _np.ascontiguousarray(rbf.reshape(NG, P, J, D_EA16).transpose(0, 3, 2, 1)).reshape(NG * D_EA16, GE),
        "L1_a1": raw["L1_gnn_a1"].reshape(-1), "L1_a2": raw["L1_gnn_a2"].reshape(-1),
        "L2_Wkv": _np.concatenate([raw["L2_gnn_Wk"], raw["L2_gnn_Wv"]], axis=1),
        "L2_bkv": _np.concatenate([raw["L2_gnn_bk"], raw["L2_gnn_bv"]]),
        "L3_Wc": _np.ascontiguousarray(_np.concatenate([raw["L3_gnn_Wc0"], raw["L3_gnn_Wc1"]], axis=1).T).reshape(-1),
    }
    taken = {"L1_gnn_a1", "L1_gnn_a2", "L2_gnn_Wk", "L2_gnn_Wv", "L2_gnn_bk", "L2_gnn_bv", "L3_gnn_Wc0", "L3_gnn_Wc1"}
    arrays.update({k.replace("_gnn", ""): _np.ascontiguousarray(v) for k, v in raw.items() if "_gnn_" in k and k not in taken})
    nc = _bacc.Bacc("TRN2", target_bir_lowering=False, num_devices=1)
    args = {n: nc.dram_tensor(f"in_{n}", v.shape, mybir.dt.from_np(v.dtype), kind="ExternalInput").ap() for n, v in arrays.items()}
    out = nc.dram_tensor("out_0", (NP, D), F32, kind="ExternalOutput").ap()
    build(nc, args, out)
    r = _run(nc, [{f"in_{n}": v for n, v in arrays.items()}], core_ids=[0])
    return r.results[0]["out_0"][:N_NODES]
```

```python
from contextlib import ExitStack

import numpy as np

import concourse.bass as bass
from concourse import mybir

ALU = mybir.AluOpType
ACT = mybir.ActivationFunctionType
AX = mybir.AxisListType
F32 = mybir.dt.float32
I32 = mybir.dt.int32

P = 128
N_NODES = 3125
N_EDGES = 53125
D = 256
D_EA64, D_EA16 = 64, 16
WN = -(-N_NODES // P)
CW = 5
CHUNKS = WN // CW
NP = WN * P
WX = WN + 1
J = 4
GE = P * J
NG = -(-N_EDGES // GE)
EP = NG * GE
ES = N_EDGES + N_NODES
NGS = -(-ES // GE)
EPS = NGS * GE
KC = -(-(max(NG, NGS) * WX + 3) // P)
KMAX = KC * P
BIG = 1e30
SLOPE = 0.2
C3 = 64
assert WN % CW == 0 and NG % 2 == 0 and NGS % 2 == 0


class Model:

    def __init__(self, inputs):
        self.inputs = inputs


class Order:

    def __init__(self, dram, name, groups, key, other):
        self.groups, self.edges = groups, groups * GE
        self.key, self.other = key, other
        self.key_around = dram(name + "_key_f", (self.edges + 2,))
        self.key_f = self.key_around[1:self.edges + 1]
        self.gk_d, self.wk_d = dram(name + "_group", (KMAX,), I32), dram(name + "_window", (KMAX,), I32)


class Sorted(Order):

    def __init__(self, dram, name, groups, pairs):
        dr = lambda n, s, d=F32: dram(f"{name}_{n}", s, d)
        edges = groups * GE
        Order.__init__(self, dram, name, groups, dr("key", (edges,), I32), dr("other", (edges,), I32))
        self.unsorted, self.sorted = pairs, dr("sorted", (edges, 2), I32)
        self.cols, self.key_in_f, self.key_in_lo = dr("cols", (edges, 3)), dr("key_in", (edges,)), dr("key_in_lo", (edges,))


class Stages:

    def __init__(self, sem, names):
        self.sem, self.names = sem, list(names)
        self.n = len(self.names)
        self.start = 2 * self.n

    def at(self, name, step):
        return (step + 2) * self.n + self.names.index(name) + 1


class Chain:

    def __init__(self, sem, names):
        self.sem, self.names = sem, list(names)

    def at(self, name):
        return self.names.index(name) + 1


def settle(eng):
    eng.nop(nofuse=True)


def column(v):
    return v.rearrange("(p a) -> p a", a=1)


def row_everywhere(v):
    return v.rearrange("(a n) -> a n", a=1).broadcast_to([P, v.shape[-1]])


def build_steps(nc, m, o, tag):
    NG, EP = o.groups, o.edges
    with ExitStack() as ctx:
        sb = lambda n, s, d=F32: ctx.enter_context(nc.sbuf_tensor(tag + n, s, d))
        sem = lambda n: ctx.enter_context(nc.semaphore(tag + n))
        dst_rows = sb("st_dst_rows", [NG, GE], I32)
        dst_i = sb("st_dst_i", [P, EP // P], I32)
        dst_f = sb("st_dst_f", [P, EP // P])
        lim_f = sb("st_lim_f", [NG, 2])
        lim_i = sb("st_lim_i", [NG, 2], I32)
        win_i = sb("st_win_i", [NG, 2], I32)
        win = sb("st_win", [NG, 2])
        count = sb("st_count", [NG, 1])
        count_b = sb("st_count_b", [NG, P])
        wmin_b = sb("st_wmin_b", [NG, P])
        below = sb("st_below", [NG, NG + 1])
        start = sb("st_start", [P, NG + 1])
        delta = sb("st_delta", [P, NG])
        delta_step = sb("st_delta_step", [P, NG])
        k_i = sb("st_k_i", [P, KC], I32)
        k_f = sb("st_k_f", [P, KC])
        le = sb("st_le", [P, KC, NG])
        gk = sb("st_gk", [P, KC])
        wk = sb("st_wk", [P, KC])
        gk_i = sb("st_gk_i", [P, KC], I32)
        wk_i = sb("st_wk_i", [P, KC], I32)
        half_f = sb("st_half_f", [1, 1])
        half_i = sb("st_half_i", [1, 1], I32)
        ps = ctx.enter_context(nc.psum_tensor(tag + "st_ps", [P, 512], F32))
        loaded, stored, listed = sem("st_loaded"), sem("st_stored"), sem("st_listed")
        pool_done, dve_done, pe_done = sem("st_pool"), sem("st_dve"), sem("st_pe")
        block = ctx.enter_context(nc.Block())

        @block.sync
        def _(sp):
            sp.dma_start(dst_rows[:, :], o.key.rearrange("(g e) -> g e", e=GE)).then_inc(loaded, 16)
            sp.dma_start(dst_i[:, :], o.key.rearrange("(p c) -> p c", p=P)).then_inc(loaded, 16)
            sp.wait_ge(dve_done, 1)
            sp.dma_start(o.key_f.rearrange("(p c) -> p c", p=P), dst_f[:, :]).then_inc(stored, 16)
            sp.wait_ge(dve_done, 26)
            sp.dma_start(o.gk_d.rearrange("(p c) -> p c", p=P), gk_i[:, :]).then_inc(stored, 16)
            sp.dma_start(o.wk_d.rearrange("(p c) -> p c", p=P), wk_i[:, :]).then_inc(stored, 16)
            sp.wait_ge(stored, 48)
            sp.dma_start(o.gk[:, :], o.gk_d.rearrange("(a k) -> a k", a=1)).then_inc(listed, 16)
            sp.dma_start(o.wk[:, :], o.wk_d.rearrange("(a k) -> a k", a=1)).then_inc(listed, 16)
            sp.wait_ge(listed, 32)

        @block.gpsimd
        def _(pool):
            nc.gpsimd.iota(m.iota[:, :], [[1, P]], base=0, channel_multiplier=0,
                           allow_small_or_imprecise_dtypes=True).then_inc(pool_done, 1)
            nc.gpsimd.iota(m.node[:, :], [[P, WX]], base=0, channel_multiplier=1,
                           allow_small_or_imprecise_dtypes=True).then_inc(pool_done, 1)
            nc.gpsimd.iota(m.base[:, :], [[P, WX]], base=0, channel_multiplier=0,
                           allow_small_or_imprecise_dtypes=True).then_inc(pool_done, 1)
            nc.gpsimd.iota(k_i[:, :], [[1, KC]], base=0, channel_multiplier=KC).then_inc(pool_done, 1)

        @block.tensor
        def _(pe):
            pe.wait_ge(dve_done, 12)
            nc.tensor.matmul(ps[:, 0:NG + 1], count_b[:, :], below[:, :], start=True, stop=True)
            nc.tensor.matmul(ps[:, 256:256 + NG], wmin_b[:, :], m.ident[0:NG, 0:NG],
                             start=True, stop=True).then_inc(pe_done, 1)

        @block.vector
        def _(dve):
            n = [0]

            def link(ins):
                n[0] += 1
                ins.then_inc(dve_done, 1)
                dve.wait_ge(dve_done, n[0])

            dve.wait_ge(loaded, 32)
            dve.wait_ge(pool_done, 4)
            link(nc.vector.tensor_copy(dst_f[:, :], dst_i[:, :]))
            link(nc.vector.tensor_scalar(m.ident[:, :], m.iota[:, :], m.node[:, 0:1], None, ALU.is_equal))
            link(nc.vector.tensor_reduce(lim_f[:, 0:1], dst_rows[:, :], AX.X, ALU.min))
            link(nc.vector.tensor_reduce(lim_f[:, 1:2], dst_rows[:, :], AX.X, ALU.max))
            link(nc.vector.tensor_copy(lim_i[:, :], lim_f[:, :]))
            link(nc.vector.tensor_scalar(win_i[:, :], lim_i[:, :], 7, None, ALU.arith_shift_right))
            link(nc.vector.tensor_copy(win[:, :], win_i[:, :]))
            link(nc.vector.scalar_tensor_tensor(count[:, :], win[:, 1:2], 1.0, win[:, 0:1], ALU.add, ALU.subtract))
            link(nc.vector.tensor_copy(count_b[:, :], count[:, 0:1].broadcast_to([NG, P])))
            link(nc.vector.tensor_copy(wmin_b[:, :], win[:, 0:1].broadcast_to([NG, P])))
            link(nc.vector.tensor_scalar(below[:, :], m.iota[0:NG, 0:NG + 1], m.node[0:NG, 0:1], None, ALU.is_gt))
            link(nc.vector.tensor_copy(k_f[:, :], k_i[:, :]))
            dve.wait_ge(pe_done, 1)
            link(nc.vector.tensor_copy(start[:, :], ps[:, 0:NG + 1]))
            link(nc.vector.tensor_tensor(delta[:, :], ps[:, 256:256 + NG], start[:, 0:NG], ALU.subtract))
            link(nc.vector.tensor_tensor(delta_step[:, 1:NG], delta[:, 1:NG], delta[:, 0:NG - 1], ALU.subtract))
            link(nc.vector.tensor_copy(delta_step[:, 0:1], delta[:, 0:1]))
            start_b = start[:, 0:NG].unsqueeze(1).broadcast_to([P, KC, NG])
            k_b = k_f[:, :].unsqueeze(2).broadcast_to([P, KC, NG])
            link(nc.vector.tensor_tensor(le[:, :, :], start_b, k_b, ALU.is_le))
            link(nc.vector.tensor_reduce(gk[:, :], le[:, :, :], AX.X, ALU.add))
            link(nc.vector.tensor_scalar(gk[:, :], gk[:, :], -1.0, None, ALU.add))
            link(nc.vector.tensor_copy(gk_i[:, :], gk[:, :]))
            d_b = delta_step[:, :].unsqueeze(1).broadcast_to([P, KC, NG])
            link(nc.vector.tensor_tensor(le[:, :, :], le[:, :, :], d_b, ALU.mult))
            link(nc.vector.tensor_reduce(wk[:, :], le[:, :, :], AX.X, ALU.add))
            link(nc.vector.tensor_tensor(wk[:, :], wk[:, :], k_f[:, :], ALU.add))
            link(nc.vector.tensor_scalar(wk[:, :], wk[:, :], float(WX - 1), None, ALU.min))
            link(nc.vector.tensor_copy(wk_i[:, :], wk[:, :]))
            link(nc.vector.tensor_scalar(half_f[:, :], start[0:1, NG:NG + 1], 1.0, None, ALU.add))
            link(nc.vector.tensor_copy(half_i[:, :], half_f[:, :]))
            link(nc.vector.tensor_scalar(o.pairs[:, :], half_i[:, :], 1, None, ALU.arith_shift_right))


def drive(eng, o, front, back=None):
    pairs = eng.value_load(o.pairs[0:1, 0:1], min_val=1, max_val=KMAX // 2 - 1)
    if front:
        front(0, 0, 0)
    with eng.Fori(0, pairs) as i:
        if front:
            front(2 * i + 1, i, 1)
        if back:
            back(2 * i, i, 0)
        if front:
            front(2 * i + 2, i + 1, 0)
        if back:
            back(2 * i + 1, i, 1)


def window_of(eng, o, k):
    return eng.value_load(o.wk[0:1, bass.ds(k, 1)], min_val=0, max_val=WX - 1)


def group_of(eng, o, k):
    return eng.value_load(o.gk[0:1, bass.ds(k, 1)], min_val=0, max_val=o.groups - 1)


def over_groups(eng, n, front=None, middle=None, back=None):
    call = lambda f, k, i, b: f(k, i, b) if f else None
    call(front, 0, 0, 0)
    with eng.Fori(0, n // 2 - 1) as i:
        for b in range(2):
            call(middle, 2 * i + b, i, b)
            call(front, 2 * i + b + 1, i + b, 1 - b)
            call(back, 2 * i + b, i, b)
    call(middle, n - 2, n // 2 - 1, 0)
    call(front, n - 1, n // 2 - 1, 1)
    call(back, n - 2, n // 2 - 1, 0)
    call(middle, n - 1, n // 2 - 1, 1)
    call(back, n - 1, n // 2 - 1, 1)


def edge_sums(nc, m, o, tag, table, W, total, attr=None, prob=None, H=1):
    with ExitStack() as ctx:
        sb = lambda n, s, d=F32: [ctx.enter_context(nc.sbuf_tensor(f"{tag}_{n}{b}", s, d)) for b in range(2)]
        sem = lambda n: ctx.enter_context(nc.semaphore(f"{tag}_{n}"))
        A = attr.shape[-1] if attr is not None else 0
        idx, key_c = sb("idx", [P, J], I32), sb("key_c", [P, J])
        attrs = sb("attr", [P, J, A]) if A else None
        probs = sb("prob", [P, J, H]) if prob is not None else None
        rel, hot, rows = sb("rel", [P, J]), sb("hot", [P, J, P]), sb("rows", [P, J, table.shape[-1]])
        sums = [ctx.enter_context(nc.psum_tensor(f"{tag}_sums{b}", [P, 512], F32)) for b in range(2)]
        loaded = [sem(f"loaded{b}") for b in range(2)]
        gathered = [m.dma_sem(f"{tag}_gathered{b}") for b in range(2)]
        hots = Stages(sem("hots"), ["rel", "hot"])
        weighed = Stages(sem("weighed"), [f"tile{j}" for j in range(J)])
        pe_s = Stages(sem("pe"), ["sum"])
        merges = Stages(sem("merges"), ["merged"])
        zeroed = sem("zeroed")
        loads = 2 + (attr is not None) + (prob is not None)
        block = ctx.enter_context(nc.Block())

        @block.sync
        def _(sp):
            def front(k, i, b):
                g = group_of(sp, o, k)
                part = bass.ds(g * GE, GE)
                if prob is None:
                    sp.wait_ge(pe_s.sem, pe_s.at("sum", k - 2))
                else:
                    sp.wait_ge(weighed.sem, weighed.at(f"tile{J - 1}", k - 2))
                sp.dma_start(idx[b][:, :], o.other[part].rearrange("(p j) -> p j", j=J)).then_inc(loaded[b], 16)
                sp.dma_start(key_c[b][:, :], o.key_f[part].rearrange("(p j) -> p j", j=J)).then_inc(loaded[b], 16)
                if A:
                    sp.dma_start(attrs[b][:, :, :], attr[part, :].rearrange("(p j) c -> p j c", j=J)).then_inc(loaded[b], 16)
                if prob is not None:
                    sp.dma_start(probs[b][:, :, :], prob[part, :].rearrange("(p j) h -> p j h", j=J)).then_inc(loaded[b], 16)
            drive(sp, o, front)

        @block.gpsimd
        def _(pool):
            nc.gpsimd.memset(total[:, :, :], 0.0).then_inc(zeroed, 1)

            def front(k, i, b):
                pool.wait_ge(loaded[b], 16 * loads * (i + 1))
                pool.wait_ge(pe_s.sem, pe_s.at("sum", k - 2))
                settle(pool)
                for j in range(J):
                    pool.indirect_dma_start(
                        out=rows[b][:, j, :], out_offset=None, in_=table,
                        in_offset=bass.IndirectOffsetOnAxis(ap=idx[b][:, j:j + 1], axis=0)).then_inc(gathered[b], 16)
            drive(pool, o, front)

        @block.tensor
        def _(pe):
            pe.sem_inc(pe_s.sem, pe_s.start)

            def back(k, i, b):
                pe.wait_ge(hots.sem, hots.at("hot", k))
                pe.wait_ge(merges.sem, merges.at("merged", k - 2))
                if prob is None:
                    pe.wait_ge(gathered[b], 16 * J * (i + 1))
                for j in range(J):
                    if prob is not None:
                        pe.wait_ge(weighed.sem, weighed.at(f"tile{j}", k))
                    mm = nc.tensor.matmul(sums[b][:, 0:W], hot[b][:, j, :], rows[b][:, j, 0:W], start=(j == 0), stop=(j == J - 1))
                if A:
                    pe.wait_ge(loaded[b], 16 * loads * (i + 1))
                    for j in range(J):
                        mm = nc.tensor.matmul(sums[b][:, W:W + A], hot[b][:, j, :], attrs[b][:, j, :], start=(j == 0), stop=(j == J - 1))
                mm.then_inc(pe_s.sem, 1)
            drive(pe, o, None, back)

        @block.vector
        def _(dve):
            for s in (hots, weighed, merges):
                dve.sem_inc(s.sem, s.start)
            dve.wait_ge(zeroed, 1)

            def front(k, i, b):
                w = window_of(dve, o, k)
                dve.wait_ge(loaded[b], 16 * loads * (i + 1))
                nc.vector.tensor_scalar(rel[b][:, :], key_c[b][:, :], m.base[:, bass.ds(w, 1)], None, ALU.subtract).then_inc(hots.sem, 1)
                dve.wait_ge(hots.sem, hots.at("rel", k))
                dve.wait_ge(pe_s.sem, pe_s.at("sum", k - 2))
                for j in range(J):
                    ins = nc.vector.tensor_scalar(hot[b][:, j, :], m.iota[:, :], rel[b][:, j:j + 1], None, ALU.is_equal)
                ins.then_inc(hots.sem, 1)
                if prob is not None:
                    dve.wait_ge(gathered[b], 16 * J * (i + 1))
                    for j in range(J):
                        if H == 1:
                            ins = nc.vector.tensor_scalar(rows[b][:, j, 0:W], rows[b][:, j, 0:W], probs[b][:, j, 0:1], None, ALU.mult)
                        else:
                            heads = rows[b][:, j, 0:W].rearrange("p (h c) -> p h c", h=H)
                            ins = nc.vector.tensor_tensor(heads, heads, probs[b][:, j, :].unsqueeze(2).broadcast_to([P, H, W // H]), ALU.mult)
                        ins.then_inc(weighed.sem, 1)

            def back(k, i, b):
                w = window_of(dve, o, k)
                dve.wait_ge(pe_s.sem, pe_s.at("sum", k))
                dve.wait_ge(merges.sem, merges.at("merged", k - 1))
                a = total[:, bass.ds(w, 1), :].rearrange("p a c -> p (a c)")
                nc.vector.tensor_tensor(a, a, sums[b][:, 0:W + A], ALU.add).then_inc(merges.sem, 1)
            drive(dve, o, front, back)


def sort_edges(nc, m, o, tag):
    NG, EP = o.groups, o.edges
    with ExitStack() as ctx:
        one = lambda n, s, d=F32: ctx.enter_context(nc.sbuf_tensor(f"{tag}_{n}", s, d))
        two = lambda n, s, d=F32: [one(f"{n}{b}", s, d) for b in range(2)]
        bank = lambda n: ctx.enter_context(nc.psum_tensor(f"{tag}_{n}", [P, 512], F32))
        sem = lambda n: ctx.enter_context(nc.semaphore(f"{tag}_{n}"))
        run = two("run", [P, J, WX])
        lower = one("lower", [P, P])

        C = EP // P
        CB = max(n for n in range(1, 24) if C % n == 0)
        with ExitStack() as first:
            tmp = lambda n, s, d=F32: first.enter_context(nc.sbuf_tensor(f"{tag}_{n}", s, d))
            pair_all = tmp("pair_all", [P, C, 2], I32)
            lo_i, hi_i = tmp("lo_i", [P, C], I32), tmp("hi_i", [P, C], I32)
            row_i = tmp("row_i", [P, C], I32)
            cols = tmp("cols", [P, C, 3])
            flat = [tmp(f"flat{i}", [P, C]) for i in range(2)]
            hot, high = tmp("hot_all", [P, CB, P]), tmp("high_all", [P, CB, WX])
            zero, ones = tmp("zero", [P, P]), tmp("ones", [P, P])
            below = tmp("below", [P, P])
            per_window, before_window = tmp("per_window", [P, WX]), tmp("before_window", [P, WX])
            counts = tmp("counts", [P, WX])
            count_ps, pre_ps = bank("count"), bank("pre")
            loaded, stored, made, counted, dve_done, pe_done = (sem(n) for n in ("a_loaded", "a_stored", "a_made", "a_counted", "a_dve", "a_pe"))
            block = first.enter_context(nc.Block())

            @block.sync
            def _(sp):
                sp.dma_start(pair_all[:, :, :], o.unsorted.rearrange("(p c) t -> p c t", p=P)).then_inc(loaded, 16)
                sp.wait_ge(dve_done, 8)
                sp.dma_start(o.cols.rearrange("(p c) t -> p c t", p=P), cols[:, :, :]).then_inc(stored, 16)
                sp.dma_start(o.key_in_f.rearrange("(p c) -> p c", p=P), flat[0][:, :]).then_inc(stored, 16)
                sp.dma_start(o.key_in_lo.rearrange("(p c) -> p c", p=P), flat[1][:, :]).then_inc(stored, 16)
                sp.wait_ge(stored, 48)

            @block.gpsimd
            def _(pool):
                nc.gpsimd.memset(zero[:, :], 0.0).then_inc(loaded, 1)
                nc.gpsimd.memset(ones[:, :], 1.0).then_inc(loaded, 1)

            @block.tensor
            def _(pe):
                pe.wait_ge(loaded, 18)
                nc.tensor.matmul(count_ps[:, 0:WX], zero[:, :], zero[:, 0:WX], start=True, stop=True)
                with pe.Fori(0, C // CB) as i:
                    pe.wait_ge(made, i + 1)
                    for t in range(CB):
                        mm = nc.tensor.matmul(count_ps[:, 0:WX], hot[:, t, :], high[:, t, :], start=False, stop=True, skip_group_check=True)
                    mm.then_inc(counted, 1)
                pe.wait_ge(dve_done, 11)
                nc.tensor.matmul(pre_ps[:, 0:WX], below[:, :], counts[:, :], start=True, stop=True)
                nc.tensor.matmul(pre_ps[:, 64:64 + WX], ones[:, :], counts[:, :], start=True, stop=True).then_inc(pe_done, 1)

            @block.vector
            def _(dve):
                n = [0]

                def link(ins):
                    n[0] += 1
                    ins.then_inc(dve_done, 1)
                    dve.wait_ge(dve_done, n[0])

                dve.wait_ge(loaded, 18)
                link(nc.vector.tensor_copy(row_i[:, :], pair_all[:, :, 0:1].rearrange("p c a -> p (c a)")))
                link(nc.vector.tensor_scalar(lo_i[:, :], row_i[:, :], P - 1, None, ALU.bitwise_and))
                link(nc.vector.tensor_scalar(hi_i[:, :], row_i[:, :], 7, None, ALU.arith_shift_right))
                link(nc.vector.tensor_copy(cols[:, :, 0:1].rearrange("p c a -> p (c a)"), row_i[:, :]))
                link(nc.vector.tensor_copy(cols[:, :, 1:2].rearrange("p c a -> p (c a)"), lo_i[:, :]))
                link(nc.vector.tensor_copy(cols[:, :, 2:3].rearrange("p c a -> p (c a)"), hi_i[:, :]))
                link(nc.vector.tensor_copy(flat[0][:, :], row_i[:, :]))
                link(nc.vector.tensor_copy(flat[1][:, :], lo_i[:, :]))
                dve.sem_inc(counted, 1)
                with dve.Fori(0, C // CB) as i:
                    dve.wait_ge(counted, i + 1)
                    lo = cols[:, bass.ds(i * CB, CB), 1:2].broadcast_to([P, CB, P])
                    hi = cols[:, bass.ds(i * CB, CB), 2:3].broadcast_to([P, CB, WX])
                    nc.vector.tensor_tensor(hot[:, :, :], m.iota[:, :].unsqueeze(1).broadcast_to([P, CB, P]), lo, ALU.is_equal)
                    nc.vector.tensor_tensor(high[:, :, :], m.iota[:, 0:WX].unsqueeze(1).broadcast_to([P, CB, WX]), hi, ALU.is_equal).then_inc(made, 1)
                dve.wait_ge(counted, C // CB + 1)
                link(nc.vector.tensor_copy(counts[:, :], count_ps[:, 0:WX]))
                link(nc.vector.tensor_scalar(below[:, :], m.iota[:, :], m.node[:, 0:1], None, ALU.is_gt))
                link(nc.vector.tensor_scalar(lower[:, :], m.iota[:, :], m.node[:, 0:1], None, ALU.is_lt))
                dve.wait_ge(pe_done, 1)
                link(nc.vector.tensor_copy(per_window[:, :], pre_ps[:, 64:64 + WX]))
                link(nc.vector.tensor_tensor_scan(before_window[:, :], ones[:, 0:WX], per_window[:, :], 0.0, ALU.mult, ALU.add))
                link(nc.vector.tensor_tensor(before_window[:, :], before_window[:, :], per_window[:, :], ALU.subtract))
                link(nc.vector.tensor_tensor(run[0][:, 0, :], pre_ps[:, 0:WX], before_window[:, :], ALU.add))

        with ExitStack() as second:
            tmp = lambda n, s, d=F32: second.enter_context(nc.sbuf_tensor(f"{tag}_{n}", s, d))
            two = lambda n, s, d=F32: [tmp(f"{n}{b}", s, d) for b in range(2)]
            pair, col = two("pair", [P, J, 2], I32), two("col", [P, J, 3])
            row_r, lo_r = two("row_r", [P, GE]), two("lo_r", [P, GE])
            hot, hot_t, high = two("hot", [P, J, P]), two("hot_t", [P, J, P]), two("high", [P, J, WX])
            tied = tmp("tied", [P, J, P])
            tie, place = two("tie", [P, J]), tmp("place", [P, J])
            at_sel = tmp("at_sel", [P, J, WX])
            place_i = two("place_i", [P, J], I32)
            hist, at = [second.enter_context(nc.psum_tensor(f"{tag}_hist{b}", [P, 512], F32)) for b in range(2)], \
                [second.enter_context(nc.psum_tensor(f"{tag}_at{b}", [P, 512], F32)) for b in range(2)]
            loaded = [sem(f"b_loaded{b}") for b in range(2)]
            scattered = [m.dma_sem(f"{tag}_b_scattered{b}") for b in range(2)]
            front_s = Stages(sem("b_front"), ["hot_t", "hots", "tie"])
            back_s = Stages(sem("b_back"), [f"run{j}" for j in range(1, J + 1)] + ["picked", "place", "ranked", "placed"])
            hist_s, at_s = Stages(sem("b_hist"), ["hist"]), Stages(sem("b_at"), ["at"])
            pool_s = Stages(sem("b_pool"), ["scattered"])
            block = second.enter_context(nc.Block())

            @block.sync
            def _(sp):
                def front(k, i, b):
                    part = bass.ds(k * GE, GE)
                    sp.wait_ge(front_s.sem, front_s.at("tie", k - 2))
                    sp.wait_ge(back_s.sem, back_s.at("picked", k - 2))
                    sp.dma_start(col[b][:, :, :], o.cols[part, :].rearrange("(p j) t -> p j t", j=J)).then_inc(loaded[b], 16)
                    sp.dma_start(row_r[b][:, :], row_everywhere(o.key_in_f[part])).then_inc(loaded[b], 16)
                    sp.dma_start(lo_r[b][:, :], row_everywhere(o.key_in_lo[part])).then_inc(loaded[b], 16)
                    sp.wait_ge(pool_s.sem, pool_s.at("scattered", k - 2))
                    sp.dma_start(pair[b][:, :, :], o.unsorted[part, :].rearrange("(p j) t -> p j t", j=J)).then_inc(loaded[b], 16)
                over_groups(sp, NG, front)

            @block.gpsimd
            def _(pool):
                pool.sem_inc(pool_s.sem, pool_s.start)

                def back(k, i, b):
                    pool.wait_ge(loaded[b], 64 * (i + 1))
                    pool.wait_ge(back_s.sem, back_s.at("placed", k))
                    settle(pool)
                    for j in range(J):
                        pool.indirect_dma_start(
                            out=o.sorted, out_offset=bass.IndirectOffsetOnAxis(ap=place_i[b][:, j:j + 1], axis=0),
                            in_=pair[b][:, j, :], in_offset=None).then_inc(scattered[b], 16)
                    pool.wait_ge(scattered[b], 16 * J * (i + 1))
                    pool.sem_inc(pool_s.sem, 1)
                over_groups(pool, NG, back=back)

            @block.tensor
            def _(pe):
                pe.sem_inc(hist_s.sem, hist_s.start)
                pe.sem_inc(at_s.sem, at_s.start)

                def front(k, i, b):
                    pe.wait_ge(front_s.sem, front_s.at("hots", k))
                    pe.wait_ge(back_s.sem, back_s.at(f"run{J}", k - 2))
                    for j in range(J):
                        mm = nc.tensor.matmul(hist[b][:, j * WX:(j + 1) * WX], hot[b][:, j, :], high[b][:, j, :], start=True, stop=True)
                    mm.then_inc(hist_s.sem, 1)

                def back(k, i, b):
                    pe.wait_ge(back_s.sem, back_s.at("picked", k - 2))
                    pe.wait_ge(back_s.sem, back_s.at(f"run{J}", k))
                    for j in range(J):
                        mm = nc.tensor.matmul(at[b][:, j * WX:(j + 1) * WX], hot_t[b][:, j, :], run[b][:, j, :], start=True, stop=True)
                    mm.then_inc(at_s.sem, 1)
                over_groups(pe, NG, front=front, middle=back)

            @block.vector
            def _(dve):
                dve.sem_inc(front_s.sem, front_s.start)
                dve.sem_inc(back_s.sem, back_s.start)

                def front(k, i, b):
                    dve.wait_ge(loaded[b], 64 * (i + 1))
                    dve.wait_ge(at_s.sem, at_s.at("at", k - 2))
                    nc.vector.tensor_scalar(hot_t[b][:, :, :], lo_r[b][:, :].rearrange("p (e j) -> p j e", j=J),
                                            m.node[:, 0:1], None, ALU.is_equal).then_inc(front_s.sem, 1)
                    for j in range(J):
                        nc.vector.tensor_scalar(hot[b][:, j, :], m.iota[:, :], col[b][:, j, 1:2], None, ALU.is_equal)
                    nc.vector.tensor_tensor(high[b][:, :, :], m.iota[:, 0:WX].unsqueeze(1).broadcast_to([P, J, WX]),
                                            col[b][:, :, 2:3].broadcast_to([P, J, WX]), ALU.is_equal).then_inc(front_s.sem, 1)
                    for j in range(J):
                        ins = nc.vector.scalar_tensor_tensor(tied[:, j, :], row_r[b][:, :].rearrange("p (e j) -> p j e", j=J)[:, j, :],
                                                             col[b][:, j, 0:1], lower[:, :], ALU.is_equal, ALU.mult, accum_out=tie[b][:, j:j + 1])
                    ins.then_inc(front_s.sem, 1)

                def middle(k, i, b):
                    dve.wait_ge(hist_s.sem, hist_s.at("hist", k))
                    dve.wait_ge(back_s.sem, back_s.at(f"run{J}", k - 1))
                    for j in range(J):
                        to = run[b][:, j + 1, :] if j < J - 1 else run[1 - b][:, 0, :]
                        if j == J - 1:
                            dve.wait_ge(at_s.sem, at_s.at("at", k - 1))
                        nc.vector.tensor_tensor(to, run[b][:, j, :], hist[b][:, j * WX:(j + 1) * WX], ALU.add).then_inc(back_s.sem, 1)
                        dve.wait_ge(back_s.sem, back_s.at(f"run{j + 1}", k))

                def back(k, i, b):
                    def link(name, ins):
                        ins.then_inc(back_s.sem, 1)
                        dve.wait_ge(back_s.sem, back_s.at(name, k))

                    dve.wait_ge(front_s.sem, front_s.at("tie", k))
                    dve.wait_ge(at_s.sem, at_s.at("at", k))
                    link("picked", nc.vector.tensor_tensor(at_sel[:, :, :], at[b][:, 0:J * WX].rearrange("p (j w) -> p j w", j=J), high[b][:, :, :], ALU.mult))
                    link("place", nc.vector.tensor_reduce(place[:, :], at_sel[:, :, :], AX.X, ALU.add))
                    link("ranked", nc.vector.tensor_tensor(place[:, :], place[:, :], tie[b][:, :], ALU.add))
                    dve.wait_ge(pool_s.sem, pool_s.at("scattered", k - 2))
                    link("placed", nc.vector.tensor_copy(place_i[b][:, :], place[:, :]))
                over_groups(dve, NG, front, middle, back)

        with ExitStack() as third:
            tmp = lambda n, s, d=F32: third.enter_context(nc.sbuf_tensor(f"{tag}_{n}", s, d))
            pair_all, row, col = tmp("pairs", [P, C, 2], I32), tmp("row", [P, C], I32), tmp("col_s", [P, C], I32)
            loaded, split, stored = sem("c_loaded"), sem("c_split"), sem("c_stored")
            ends = tmp("ends", [1, 2])
            block = third.enter_context(nc.Block())

            @block.sync
            def _(sp):
                sp.dma_start(pair_all[:, :, :], o.sorted.rearrange("(p c) t -> p c t", p=P)).then_inc(loaded, 16)
                sp.wait_ge(split, 3)
                sp.dma_start(o.key.rearrange("(p c) -> p c", p=P), row[:, :]).then_inc(stored, 16)
                sp.dma_start(o.other.rearrange("(p c) -> p c", p=P), col[:, :]).then_inc(stored, 16)
                sp.dma_start(o.key_around[0:1].rearrange("(a c) -> a c", a=1), ends[:, 0:1]).then_inc(stored, 16)
                sp.dma_start(o.key_around[EP + 1:EP + 2].rearrange("(a c) -> a c", a=1), ends[:, 1:2]).then_inc(stored, 16)
                sp.wait_ge(stored, 64)

            @block.vector
            def _(dve):
                nc.vector.memset(ends[:, :], -1.0).then_inc(split, 1)
                dve.wait_ge(loaded, 16)
                nc.vector.tensor_copy(row[:, :], pair_all[:, :, 0:1].rearrange("p c a -> p (c a)")).then_inc(split, 1)
                nc.vector.tensor_copy(col[:, :], pair_all[:, :, 1:2].rearrange("p c a -> p (c a)")).then_inc(split, 1)


def edge_scores(nc, m, o, tag, H, C, source, target, scores, att=None):
    W, JH = H * C, J * H
    TW = W + H if att is not None else W
    with ExitStack() as ctx:
        two = lambda n, s, d=F32: [ctx.enter_context(nc.sbuf_tensor(f"{tag}_{n}{b}", s, d)) for b in range(2)]
        sem = lambda n: ctx.enter_context(nc.semaphore(f"{tag}_{n}"))
        idx = two("idx", [P, J, 2], I32)
        near, far = two("near", [P, J, TW]), two("far", [P, J, TW])
        part = two("part", [P, JH])
        loaded = [sem(f"loaded{b}") for b in range(2)]
        gathered = [m.dma_sem(f"{tag}_gathered{b}") for b in range(2)]
        sums = Stages(sem("sums"), [f"sum{j}" for j in range(J)])
        relus = Stages(sem("relus"), [f"relu{j}" for j in range(J)])
        done = Stages(sem("done"), ["part", "score"])
        block = ctx.enter_context(nc.Block())

        @block.sync
        def _(sp):
            pairs = o.sorted.rearrange("(p c) t -> p c t", p=P)

            def front(k, i, b):
                sp.wait_ge(sums.sem, sums.at("sum0", k - 2))
                sp.dma_start(idx[b][:, :, :], pairs[:, bass.ds(k * J, J), :]).then_inc(loaded[b], 16)
            over_groups(sp, o.groups, front)

        @block.gpsimd
        def _(pool):
            def front(k, i, b):
                pool.wait_ge(loaded[b], 16 * (i + 1))
                pool.wait_ge(done.sem, done.at("score", k - 2))
                settle(pool)
                for j in range(J):
                    for t, (to, table) in enumerate(((near, target), (far, source))):
                        pool.indirect_dma_start(
                            out=to[b][:, j, :], out_offset=None, in_=table,
                            in_offset=bass.IndirectOffsetOnAxis(ap=idx[b][:, j, t:t + 1], axis=0)).then_inc(gathered[b], 16)
            over_groups(pool, o.groups, front)

        @block.scalar
        def _(act):
            def back(k, i, b):
                for j in range(J):
                    act.wait_ge(sums.sem, sums.at(f"sum{j}", k))
                    nc.scalar.activation(near[b][:, j, 0:W], near[b][:, j, 0:W], ACT.Relu).then_inc(relus.sem, 1)
            if att is not None:
                act.sem_inc(relus.sem, relus.start)
                over_groups(act, o.groups, back=back)

        @block.vector
        def _(dve):
            for s in (sums, done):
                dve.sem_inc(s.sem, s.start)

            def back(k, i, b):
                dve.wait_ge(gathered[b], 16 * 2 * J * (i + 1))
                for j in range(J):
                    nc.vector.tensor_tensor(near[b][:, j, :], near[b][:, j, :], far[b][:, j, :],
                                            ALU.add if att is not None else ALU.mult).then_inc(sums.sem, 1)
                if att is None:
                    dve.wait_ge(sums.sem, sums.at(f"sum{J - 1}", k))
                    nc.vector.tensor_reduce(part[b][:, :], near[b][:, :, :].rearrange("p j (h c) -> p (j h) c", h=H), AX.X, ALU.add).then_inc(done.sem, 1)
                    dve.wait_ge(done.sem, done.at("part", k))
                    settle(dve)
                    nc.vector.tensor_copy(scores[:, bass.ds(k * J, J), :].rearrange("p j h -> p (j h)"), part[b][:, :]).then_inc(done.sem, 1)
                else:
                    for j in range(J):
                        dve.wait_ge(relus.sem, relus.at(f"relu{j}", k))
                        settle(dve)
                        for h in range(H):
                            span = near[b][:, j, h * C:(h + 1) * C]
                            r = j * H + h
                            ins = nc.vector.tensor_tensor_reduce(span, span, att[:, h * C:(h + 1) * C], 1.0 - SLOPE, 0.0,
                                                                 ALU.mult, ALU.add, part[b][:, r:r + 1])
                    ins.then_inc(done.sem, 1)
                    dve.wait_ge(done.sem, done.at("part", k))
                    nc.vector.tensor_tensor(scores[:, bass.ds(k * J, J), :], part[b][:, :].rearrange("p (j h) -> p j h", j=J),
                                            near[b][:, :, W:W + H], ALU.add).then_inc(done.sem, 1)
            over_groups(dve, o.groups, back=back)


def segment_softmax(nc, m, o, tag, H, scores, prob):
    C = o.edges // P
    with ExitStack() as ctx:
        one = lambda n, s, d=F32: ctx.enter_context(nc.sbuf_tensor(f"{tag}_{n}", s, d))
        sem = lambda n: ctx.enter_context(nc.semaphore(f"{tag}_{n}"))
        key, before, after = one("key", [P, C]), one("before", [P, C]), one("after", [P, C])
        first, last = one("first", [P, C]), one("last", [P, C])
        fence = one("fence", [P, C])
        same_before, same_after = one("same_before", [P, C]), one("same_after", [P, C])
        up, down = one("up", [P, C, H]), one("down", [P, C, H])
        any_first, any_last = one("any_first", [P, 1]), one("any_last", [P, 1])
        row_fence, row_first, row_last = (one(n, [H, P]) for n in ("row_fence", "row_first", "row_last"))
        carried = one("carried", [H, P + 2])
        ends, rows_in, initial = one("ends", [P, H]), one("rows_in", [H, P]), one("initial", [P, H])
        turned = ctx.enter_context(nc.psum_tensor(f"{tag}_turned", [P, 512], F32))
        loaded, stored = sem("loaded"), sem("stored")
        passes = ("max", "max_back", "sum", "sum_back")
        one_scan = lambda s: [f"{s}_own", f"{s}_ends", f"{s}_clear", f"{s}_row", f"{s}_shift", f"{s}_initial", f"{s}_all"]
        dve_s = Chain(sem("dve"), ["first", "same_before", "last", "same_after", "fence", "any_first", "any_last",
                                   "row_fence", "row_first", "row_last"]
                      + one_scan("max") + ["max_at_last"] + one_scan("max_back") + ["arg"]
                      + one_scan("sum") + ["sum_at_last"] + one_scan("sum_back") + ["inverse", "prob"])
        pe_s = Chain(sem("pe"), ["any"] + [f"{s}_{n}" for s in passes for n in ("row", "column")])
        act_s = Chain(sem("act"), ["exp"])
        block = ctx.enter_context(nc.Block())

        @block.sync
        def _(sp):
            for to, shift in ((key, 1), (before, 0), (after, 2)):
                sp.dma_start(to[:, :], o.key_around[shift:shift + o.edges].rearrange("(p c) -> p c", p=P)).then_inc(loaded, 16)
            sp.wait_ge(dve_s.sem, dve_s.at("prob"))
            sp.dma_start(prob.rearrange("(p c) h -> p c h", p=P), scores[:, :, :]).then_inc(stored, 16)
            sp.wait_ge(stored, 16)

        @block.tensor
        def _(pe):
            pe.wait_ge(dve_s.sem, dve_s.at("any_last"))
            nc.tensor.matmul(turned[0:H, 0:P], any_first[:, :].broadcast_to([P, H]), m.ident[:, :], start=True, stop=True)
            nc.tensor.matmul(turned[0:H, P:2 * P], any_last[:, :].broadcast_to([P, H]), m.ident[:, :], start=True, stop=True).then_inc(pe_s.sem, 1)
            for s in passes:
                pe.wait_ge(dve_s.sem, dve_s.at(f"{s}_ends"))
                nc.tensor.transpose(turned[0:H, 0:P], ends[:, :], m.ident[:, :]).then_inc(pe_s.sem, 1)
                pe.wait_ge(dve_s.sem, dve_s.at(f"{s}_shift"))
                nc.tensor.transpose(turned[:, 0:H], rows_in[:, :], m.ident[0:H, 0:H]).then_inc(pe_s.sem, 1)

        @block.scalar
        def _(act):
            act.wait_ge(dve_s.sem, dve_s.at("arg"))
            nc.scalar.activation(scores[:, :, :], scores[:, :, :], ACT.Exp).then_inc(act_s.sem, 1)

        @block.vector
        def _(dve):
            def link(name, ins):
                ins.then_inc(dve_s.sem, 1)
                dve.wait_ge(dve_s.sem, dve_s.at(name))

            def scans(name, out, data0, data1, initial, op0, op1, step):
                for h in range(H):
                    start = initial if isinstance(initial, float) else initial[:, h:h + 1]
                    ins = nc.vector.tensor_tensor_scan(out[:, ::step, h], data0[:, ::step], data1[:, ::step, h], start, op0, op1)
                link(name, ins)

            def scan(s, out, data0, data1, neutral, op0, op1, row, step):
                scans(f"{s}_own", out, data0, data1, neutral, op0, op1, step)
                edge = C - 1 if step > 0 else 0
                link(f"{s}_ends", nc.vector.tensor_copy(ends[:, :], out[:, edge, :]))
                link(f"{s}_clear", nc.vector.memset(carried[:, :], neutral))
                dve.wait_ge(pe_s.sem, pe_s.at(f"{s}_row"))
                link(f"{s}_row", nc.vector.tensor_tensor_scan(carried[:, 1:P + 1][:, ::step], row[:, ::step], turned[0:H, 0:P][:, ::step],
                                                              neutral, op0, op1))
                link(f"{s}_shift", nc.vector.tensor_copy(rows_in[:, :], carried[:, 0:P] if step > 0 else carried[:, 2:P + 2]))
                dve.wait_ge(pe_s.sem, pe_s.at(f"{s}_column"))
                link(f"{s}_initial", nc.vector.tensor_copy(initial[:, :], turned[:, 0:H]))
                scans(f"{s}_all", out, data0, data1, initial, op0, op1, step)

            dve.wait_ge(loaded, 48)
            link("first", nc.vector.tensor_tensor(first[:, :], key[:, :], before[:, :], ALU.not_equal))
            link("same_before", nc.vector.tensor_tensor(same_before[:, :], key[:, :], before[:, :], ALU.is_equal))
            link("last", nc.vector.tensor_tensor(last[:, :], key[:, :], after[:, :], ALU.not_equal))
            link("same_after", nc.vector.tensor_tensor(same_after[:, :], key[:, :], after[:, :], ALU.is_equal))
            link("fence", nc.vector.tensor_scalar(fence[:, :], first[:, :], -BIG, None, ALU.mult))
            link("any_first", nc.vector.tensor_reduce(any_first[:, :], first[:, :], AX.X, ALU.max))
            link("any_last", nc.vector.tensor_reduce(any_last[:, :], last[:, :], AX.X, ALU.max))
            dve.wait_ge(pe_s.sem, pe_s.at("any"))
            link("row_fence", nc.vector.tensor_scalar(row_fence[:, :], turned[0:H, 0:P], -BIG, None, ALU.mult))
            link("row_first", nc.vector.tensor_scalar(row_first[:, :], turned[0:H, 0:P], 0.0, None, ALU.is_equal))
            link("row_last", nc.vector.tensor_scalar(row_last[:, :], turned[0:H, P:2 * P], 0.0, None, ALU.is_equal))
            last_b = last[:, :].unsqueeze(2).broadcast_to([P, C, H])
            scan("max", up, fence, scores, -BIG, ALU.add, ALU.max, row_fence, 1)
            link("max_at_last", nc.vector.tensor_tensor(up[:, :, :], up[:, :, :], last_b, ALU.mult))
            scan("max_back", down, same_after, up, 0.0, ALU.mult, ALU.add, row_last, -1)
            link("arg", nc.vector.tensor_tensor(scores[:, :, :], scores[:, :, :], down[:, :, :], ALU.subtract))
            dve.wait_ge(act_s.sem, act_s.at("exp"))
            scan("sum", up, same_before, scores, 0.0, ALU.mult, ALU.add, row_first, 1)
            link("sum_at_last", nc.vector.tensor_tensor(up[:, :, :], up[:, :, :], last_b, ALU.mult))
            scan("sum_back", down, same_after, up, 0.0, ALU.mult, ALU.add, row_last, -1)
            link("inverse", nc.vector.reciprocal(down[:, :, :], down[:, :, :]))
            link("prob", nc.vector.tensor_tensor(scores[:, :, :], scores[:, :, :], down[:, :, :], ALU.mult))


def attention(nc, m, o, tag, H, C, source, target, value, prob, total, att=None):
    with ExitStack() as ctx:
        scores = ctx.enter_context(nc.sbuf_tensor(f"{tag}_scores", [P, o.edges // P, H], F32))
        edge_scores(nc, m, o, f"{tag}s", H, C, source, target, scores, att)
        segment_softmax(nc, m, o, f"{tag}m", H, scores, prob)
    edge_sums(nc, m, o, f"{tag}v", value, H * C, total, prob=prob, H=H)


def norm_stages(t):
    return [f"{t}_stats", f"{t}_moments", f"{t}_eps", f"{t}_rstd", f"{t}_normed"]


def layer_norm(dve, link, act_s, c, t, src, dst, nb, eps):
    for w in range(CW):
        ins = nc_of(dve).vector.bn_stats(nb.stats[:, w, :], src[:, w, :])
    link(f"{t}_stats", ins)
    settle(dve)
    for w in range(CW):
        ins = nc_of(dve).vector.bn_aggr(nb.moments[:, w, :], nb.stats[:, w, :])
    link(f"{t}_moments", ins)
    link(f"{t}_eps", nc_of(dve).vector.tensor_scalar(nb.var[:, :], nb.moments[:, :, 1:2].rearrange("p w a -> p (w a)"), eps, None, ALU.add))
    dve.wait_ge(act_s.sem, act_s.at(f"{t}_std", c))
    link(f"{t}_rstd", nc_of(dve).vector.reciprocal(nb.rstd[:, :], nb.std[:, :]))
    for w in range(CW):
        ins = nc_of(dve).vector.tensor_scalar(dst[:, w, :], src[:, w, :], nb.moments[:, w, 0:1], nb.rstd[:, w:w + 1], ALU.subtract, ALU.mult)
    link(f"{t}_normed", ins)


def nc_of(eng):
    return eng.bass


def standard_deviation(act, dve_s, act_s, c, t, nb):
    act.wait_ge(dve_s.sem, dve_s.at(f"{t}_eps", c))
    nc_of(act).scalar.activation(nb.std[:, :], nb.var[:, :], ACT.Sqrt).then_inc(act_s.sem, 1)


class NormBuffers:
    def __init__(self, one):
        self.stats, self.moments = one("stats", [P, CW, 6]), one("moments", [P, CW, 2])
        self.var, self.std, self.rstd = one("var", [P, CW]), one("std", [P, CW]), one("rstd", [P, CW])


class LinearWeights:
    def __init__(self, one, k, H, C):
        self.sums, self.products = one("w_lin", [P, k, 2 * H]), one("w_lin_products", [P, C])


def over_windows(row, n=CW):
    return row.unsqueeze(1).broadcast_to([P, n, row.shape[-1]])


def project_stages(outs):
    return [f"proj{w}_{o}" for w in range(CW) for o in range(outs)]


def project(pe, pe_s, act_s, c, lhs, weights, bias, ring, ones_row):
    n = 0
    for w in range(CW):
        for o, wt in enumerate(weights):
            width = wt[0].shape[-1]
            to = ring[:, n % 3, 0:width]
            if n >= 3:
                pe.wait_ge(act_s.sem, act_s.at(f"proj{(n - 3) // len(weights)}_{(n - 3) % len(weights)}", c))
            for kc, piece in enumerate(wt):
                mm = nc_of(pe).tensor.matmul(to, lhs(kc, w), piece, start=(kc == 0), stop=(kc == len(wt) - 1 and not bias))
            if bias:
                mm = nc_of(pe).tensor.matmul(to, ones_row, bias[o], start=False, stop=True)
            mm.then_inc(pe_s.sem, 1)
            n += 1


def linear_weights(dve, w_lin, weights, att, H, C, ready):
    for o, wt in enumerate(weights):
        for kc in range(wt.shape[1]):
            for h in range(H):
                n = (o * wt.shape[1] + kc) * H + h
                if n:
                    dve.wait_ge(ready, n)
                nc_of(dve).vector.tensor_tensor_reduce(w_lin.products[:, :], wt[:, kc, h * C:(h + 1) * C], att[:, h * C:(h + 1) * C], SLOPE, 0.0,
                                                       ALU.mult, ALU.add, w_lin.sums[:, kc, o * H + h:o * H + h + 1]).then_inc(ready, 1)


def pieces(weight, k, lo, hi):
    return [weight[:, kc, lo:hi] for kc in range(k)]


def project_linear(pe, pe_s, lhs, w_lin, k, H, turn):
    for w in range(CW):
        for kc in range(k):
            mm = nc_of(pe).tensor.matmul(turn[:, 0, w * 2 * H:(w + 1) * 2 * H], lhs(kc, w), w_lin.sums[:, kc, :], start=(kc == 0), stop=(kc == k - 1))
    mm.then_inc(pe_s.sem, 1)


def keep_linear(act, pe_s, act_s, c, turn, stages, widths, H):
    act.wait_ge(pe_s.sem, pe_s.at("lin", c))
    both = turn[:, 0, 0:CW * 2 * H].rearrange("p (w t h) -> p w t h", w=CW, t=2)
    for o in range(2):
        ins = nc_of(act).scalar.copy(stages[o][:, :, widths[o]:widths[o] + H], both[:, :, o, :])
    ins.then_inc(act_s.sem, 1)


def chunk_rows(table, c):
    return table[bass.ds(c * CW * P, CW * P), :].rearrange("(w p) n -> p w n", p=P)


def nodes_0(nc, m, agg, source, target, att, H, C):
    with ExitStack() as ctx:
        one = lambda n, s, d=F32: ctx.enter_context(nc.sbuf_tensor(f"n0_{n}", s, d))
        sem = lambda n: ctx.enter_context(nc.semaphore(f"n0_{n}"))
        sums = one("sums", [P, CW, D + D_EA64])
        sums_t = one("sums_t", [P, 3 * CW, P])
        h = one("h", [P, CW, D])
        h_t, y = one("h_t", [P, 2, CW * P]), one("y", [P, 2, CW * P])
        x_t = one("x_t", [P, 2 * CW, P])
        stage = [one(f"stage{o}", [P, CW, 512 + H]) for o in range(2)]
        w_lin = LinearWeights(one, 2, H, C)
        nb = NormBuffers(one)
        w_msg, w_edge = one("w_msg", [P, 2, D]), one("w_edge", [D_EA64, D])
        w_mlp = [one(f"w_mlp{l}", [P, 2, D]) for l in range(3)]
        b_mlp = [one(f"b_mlp{l}", [P, 2]) for l in range(3)]
        rows = {n: one(n, [P, D]) for n in ("ln_aggr_scale", "ln_aggr_bias", "ln_out_scale", "ln_out_bias")}
        w_l, w_r = one("w_l", [P, 2, 512]), one("w_r", [P, 2, 512])
        turn = ctx.enter_context(nc.psum_tensor("n0_turn", [P, 16, P], F32))
        mlp_ps = turn[:, :, :].rearrange("p (b t) c -> p b (t c)", b=4)[:, :, 0:CW * P // 2]
        ring = ctx.enter_context(nc.psum_tensor("n0_ring", [P, 3, 512], F32))
        flat = ring[:, :, :].rearrange("p b c -> p (b c)")[:, 0:CW * D].rearrange("p (w c) -> p w c", w=CW)
        weights_in, taken, stored, lin_ready = sem("weights"), sem("taken"), sem("stored"), sem("lin_ready")
        pe_s = Stages(sem("pe"), ["sums_t", "msg", "h_t", "mlp0", "mlp1", "mlp2", "out", "x_t", "lin"] + project_stages(2))
        act_s = Stages(sem("act"), ["sums_t", "a_std", "h_t", "mlp0", "mlp1", "mlp2", "b_std", "c_std", "x_t", "lin"] + project_stages(2))
        dve_s = Stages(sem("dve"), ["h"] + norm_stages("a") + ["a_scale", "a_bias", "skip0", "skip1", "skip2", "r"] + norm_stages("b")
                       + ["b_scale", "b_bias", "xr"] + norm_stages("c") + ["kept"])
        n_weights = 2 + 3 + 6 + 4 + 2
        block = ctx.enter_context(nc.Block())

        @block.sync
        def _(sp):
            load = lambda to, of: sp.dma_start(to, of).then_inc(weights_in, 16)
            load(w_msg[:, :, :], m.inputs["L0_W_message"][0:D, :].rearrange("(k p) n -> p k n", p=P))
            load(w_edge[:, :], m.inputs["L0_W_message"][D:D + D_EA64, :])
            for l in range(3):
                w, bias = [(m.inputs["L0_mlp_W0"], m.inputs["L0_mlp_b0"]), (m.inputs["L0_mlp_W1"], m.inputs["L0_mlp_b1"]), (m.inputs["L0_mlp_W2"], m.inputs["L0_mlp_b2"])][l]
                load(w_mlp[l][:, :, :], w.rearrange("(k p) n -> p k n", p=P))
                for f in range(2):
                    load(b_mlp[l][:, f:f + 1], column(bias[f * P:(f + 1) * P]))
            for name, of in (("ln_aggr_scale", m.inputs["L0_ln_aggr_scale"]), ("ln_aggr_bias", m.inputs["L0_ln_aggr_bias"]),
                             ("ln_out_scale", m.inputs["L0_ln_out_scale"]), ("ln_out_bias", m.inputs["L0_ln_out_bias"])):
                load(rows[name][:, :], row_everywhere(of))
            load(w_l[:, :, :], m.inputs["L1_W1l"].rearrange("(k p) n -> p k n", p=P))
            load(w_r[:, :, :], m.inputs["L1_W1r"].rearrange("(k p) n -> p k n", p=P))
            with sp.Fori(0, CHUNKS) as c:
                sp.wait_ge(pe_s.sem, pe_s.at("sums_t", c - 1))
                sp.dma_start(sums[:, :, :], agg[:, bass.ds(c * CW, CW), :]).then_inc(taken, 16)
                sp.wait_ge(act_s.sem, act_s.at(f"proj{CW - 1}_1", c))
                for table, t in ((source, stage[0]), (target, stage[1])):
                    sp.dma_start(chunk_rows(table, c), t[:, :, :]).then_inc(stored, 16)
            sp.wait_ge(stored, 32 * (CHUNKS + 1))

        @block.tensor
        def _(pe):
            pe.sem_inc(pe_s.sem, pe_s.start)
            pe.wait_ge(weights_in, 16 * n_weights)
            pe.wait_ge(lin_ready, 4 * H)
            with pe.Fori(0, CHUNKS) as c:
                pe.wait_ge(taken, 16 * (c + 1))
                pe.wait_ge(act_s.sem, act_s.at("lin", c - 1))
                for w in range(CW):
                    for kc in range(2):
                        nc.tensor.transpose(turn[:, kc * CW + w, :], sums[:, w, kc * P:(kc + 1) * P], m.ident[:, :])
                    mm = nc.tensor.transpose(turn[0:D_EA64, 2 * CW + w, :], sums[:, w, D:D + D_EA64], m.ident[:, :])
                mm.then_inc(pe_s.sem, 1)
                pe.wait_ge(act_s.sem, act_s.at("sums_t", c))
                pe.wait_ge(act_s.sem, act_s.at(f"proj{CW - 1}_1", c - 1))
                for w in range(CW):
                    nc.tensor.matmul(flat[:, w, :], sums_t[:, w, :], w_msg[:, 0, :], start=True, stop=False)
                    nc.tensor.matmul(flat[:, w, :], sums_t[:, CW + w, :], w_msg[:, 1, :], start=False, stop=False)
                    mm = nc.tensor.matmul(flat[:, w, :], sums_t[0:D_EA64, 2 * CW + w, :], w_edge[:, :], start=False, stop=True)
                mm.then_inc(pe_s.sem, 1)
                pe.wait_ge(dve_s.sem, dve_s.at("a_bias", c))
                for w in range(CW):
                    for kc in range(2):
                        mm = nc.tensor.transpose(turn[:, kc * CW + w, :], h[:, w, kc * P:(kc + 1) * P], m.ident[:, :])
                mm.then_inc(pe_s.sem, 1)
                for l in range(3):
                    pe.wait_ge(act_s.sem, act_s.at("h_t" if l == 0 else f"mlp{l - 1}", c))
                    if l:
                        pe.wait_ge(dve_s.sem, dve_s.at(f"skip{l - 1}", c))
                    for f in range(2):
                        for half in range(2):
                            for kc in range(2):
                                mm = nc.tensor.matmul(mlp_ps[:, 2 * f + half, :], w_mlp[l][:, kc, f * P:(f + 1) * P],
                                                      h_t[:, kc, half * CW * P // 2:(half + 1) * CW * P // 2], start=(kc == 0), stop=(kc == 1))
                    mm.then_inc(pe_s.sem, 1)
                pe.wait_ge(dve_s.sem, dve_s.at("skip2", c))
                for w in range(CW):
                    for kc in range(2):
                        mm = nc.tensor.transpose(flat[:, w, kc * P:(kc + 1) * P], h_t[:, kc, w * P:(w + 1) * P], m.ident[:, :])
                mm.then_inc(pe_s.sem, 1)
                pe.wait_ge(dve_s.sem, dve_s.at("c_normed", c))
                for w in range(CW):
                    for kc in range(2):
                        mm = nc.tensor.transpose(turn[:, kc * CW + w, :], h[:, w, kc * P:(kc + 1) * P], m.ident[:, :])
                mm.then_inc(pe_s.sem, 1)
                pe.wait_ge(act_s.sem, act_s.at("x_t", c))
                project_linear(pe, pe_s, lambda kc, w: x_t[:, kc * CW + w, :], w_lin, 2, H, turn)
                project(pe, pe_s, act_s, c, lambda kc, w: x_t[:, kc * CW + w, :], [pieces(w_l, 2, 0, 512), pieces(w_r, 2, 0, 512)], None, ring, None)

        @block.scalar
        def _(act):
            act.sem_inc(act_s.sem, act_s.start)
            act.sem_inc(stored, 32)
            act.wait_ge(weights_in, 16 * n_weights)
            with act.Fori(0, CHUNKS) as c:
                act.wait_ge(pe_s.sem, pe_s.at("sums_t", c))
                nc.scalar.copy(sums_t[:, 0:2 * CW, :], turn[:, 0:2 * CW, :])
                nc.scalar.copy(sums_t[0:D_EA64, 2 * CW:3 * CW, :], turn[0:D_EA64, 2 * CW:3 * CW, :]).then_inc(act_s.sem, 1)
                standard_deviation(act, dve_s, act_s, c, "a", nb)
                act.wait_ge(pe_s.sem, pe_s.at("h_t", c))
                nc.scalar.copy(h_t[:, :, :].rearrange("p k (w e) -> p (k w) e", e=P), turn[:, 0:2 * CW, :]).then_inc(act_s.sem, 1)
                for l in range(3):
                    act.wait_ge(pe_s.sem, pe_s.at(f"mlp{l}", c))
                    if l:
                        act.wait_ge(dve_s.sem, dve_s.at(f"skip{l - 1}", c))
                    for f in range(2):
                        ins = nc.scalar.activation(y[:, f, :].rearrange("p (b e) -> p b e", b=2), mlp_ps[:, 2 * f:2 * f + 2, :],
                                                   ACT.Relu if l < 2 else ACT.Identity, bias=b_mlp[l][:, f:f + 1])
                    ins.then_inc(act_s.sem, 1)
                standard_deviation(act, dve_s, act_s, c, "b", nb)
                standard_deviation(act, dve_s, act_s, c, "c", nb)
                act.wait_ge(pe_s.sem, pe_s.at("x_t", c))
                nc.scalar.copy(x_t[:, :, :], turn[:, 0:2 * CW, :]).then_inc(act_s.sem, 1)
                act.wait_ge(stored, 32 * (c + 1))
                keep_linear(act, pe_s, act_s, c, turn, stage, (512, 512), H)
                for w in range(CW):
                    act.wait_ge(pe_s.sem, pe_s.at(f"proj{w}_0", c))
                    nc.scalar.copy(stage[0][:, w, 0:512], ring[:, (2 * w) % 3, :]).then_inc(act_s.sem, 1)
                    act.wait_ge(pe_s.sem, pe_s.at(f"proj{w}_1", c))
                    nc.scalar.copy(stage[1][:, w, 0:512], ring[:, (2 * w + 1) % 3, :]).then_inc(act_s.sem, 1)

        @block.vector
        def _(dve):
            dve.sem_inc(dve_s.sem, dve_s.start)
            dve.wait_ge(weights_in, 16 * n_weights)
            linear_weights(dve, w_lin, (w_l, w_r), att, H, C, lin_ready)
            with dve.Fori(0, CHUNKS) as c:
                def link(name, ins):
                    ins.then_inc(dve_s.sem, 1)
                    dve.wait_ge(dve_s.sem, dve_s.at(name, c))

                x = m.xs[:, bass.ds(c * CW, CW), :]
                dve.wait_ge(pe_s.sem, pe_s.at("x_t", c - 1))
                dve.wait_ge(pe_s.sem, pe_s.at("msg", c))
                link("h", nc.vector.scalar_tensor_tensor(h[:, :, :], flat, 0.0, x, ALU.max, ALU.add))
                layer_norm(dve, link, act_s, c, "a", h, h, nb, 1e-6)
                link("a_scale", nc.vector.tensor_tensor(h[:, :, :], h[:, :, :], over_windows(rows["ln_aggr_scale"][:, :]), ALU.mult))
                link("a_bias", nc.vector.tensor_tensor(h[:, :, :], h[:, :, :], over_windows(rows["ln_aggr_bias"][:, :]), ALU.add))
                for l in range(3):
                    dve.wait_ge(act_s.sem, act_s.at(f"mlp{l}", c))
                    link(f"skip{l}", nc.vector.tensor_tensor(h_t[:, :, :], h_t[:, :, :], y[:, :, :], ALU.add))
                dve.wait_ge(pe_s.sem, pe_s.at("out", c))
                link("r", nc.vector.tensor_tensor(h[:, :, :], flat, x, ALU.add))
                layer_norm(dve, link, act_s, c, "b", h, h, nb, 1e-6)
                link("b_scale", nc.vector.tensor_tensor(h[:, :, :], h[:, :, :], over_windows(rows["ln_out_scale"][:, :]), ALU.mult))
                link("b_bias", nc.vector.tensor_tensor(h[:, :, :], h[:, :, :], over_windows(rows["ln_out_bias"][:, :]), ALU.add))
                link("xr", nc.vector.tensor_tensor(h[:, :, :], h[:, :, :], x, ALU.add))
                layer_norm(dve, link, act_s, c, "c", h, h, nb, 1e-5)
                settle(dve)
                link("kept", nc.vector.tensor_copy(x, h[:, :, :]))


def nodes_att(nc, m, tag, total, W, bias, outs, w_out=None, w_in=None, b_in=None, own=None, own_scale=1.0, residual=True,
              next_att=None):
    LH = next_att[1] if next_att else 0
    KI = W // P
    KX = KI if w_in else 4
    PX = P if w_in else C3
    widths = [v.shape[-1] for v in w_in] if w_in else [D, D]
    with ExitStack() as ctx:
        one = lambda n, s, d=F32: ctx.enter_context(nc.sbuf_tensor(f"{tag}_{n}", s, d))
        sem = lambda n: ctx.enter_context(nc.semaphore(f"{tag}_{n}"))
        y = one("y", [P, CW, W])
        x_t = one("x_t", [P, KX * CW, P])
        stage = [one(f"stage{o}", [P, CW, widths[o] + LH]) for o in range(2 if w_in else 1)]
        if next_att:
            w_lin = LinearWeights(one, KI, LH, next_att[2])
        bias_row = one("bias", [P, bias.shape[-1]])
        ones_row = one("ones", [1, P])
        w_sb = [one(f"w{o}", [P, KI, n]) for o, n in enumerate(widths)] if w_in else [one("w3", [C3, 4, 2, C3])]
        b_sb = [one(f"b{o}", [1, n]) for o, n in enumerate(widths)] if b_in else []
        nb = NormBuffers(one)
        if w_out is not None:
            w_o, y_t = one("w_o", [P, KI, D]), one("y_t", [P, KI * CW, P])
        turn = ctx.enter_context(nc.psum_tensor(f"{tag}_turn", [P, 20, P], F32))
        ring = ctx.enter_context(nc.psum_tensor(f"{tag}_ring", [P, 3, 512], F32))
        flat = ring[:, :, :].rearrange("p b c -> p (b c)")[:, 0:CW * D].rearrange("p (w c) -> p w c", w=CW)
        weights_in, stored, ready, lin_ready = sem("weights"), sem("stored"), sem("ready"), sem("lin_ready")
        n_outs = 2 if w_in else 1
        first = ["y_t", "out"] if w_out is not None else []
        pe_s = Stages(sem("pe"), first + ["x_t"] + (["lin"] if next_att else []) + project_stages(n_outs))
        act_s = Stages(sem("act"), first[:1] + (["c_std"] if residual else []) + ["x_t"] + (["lin"] if next_att else []) + project_stages(n_outs))
        dve_s = Stages(sem("dve"), ["taken", "biased"]
                       + (["xr"] + norm_stages("c") + ["kept"] if residual else ["relu"]))
        block = ctx.enter_context(nc.Block())
        n_in = 1 + (2 if w_in else 8) + len(b_sb) + (w_out is not None)

        @block.sync
        def _(sp):
            load = lambda to, of: sp.dma_start(to, of).then_inc(weights_in, 16)
            load(bias_row[:, :], row_everywhere(bias))
            if w_in:
                for o in range(2):
                    load(w_sb[o][:, :, :], w_in[o].rearrange("(k p) n -> p k n", p=P))
            else:
                for i in range(4):
                    load(w_sb[0][:, i, 0, :], m.inputs["L3_W_up1"] if i else m.inputs["L3_W_up0"])
                    load(w_sb[0][:, i, 1, :], m.inputs["L3_Wsc1"] if i else m.inputs["L3_Wsc0"])
            for o, t in enumerate(b_sb):
                load(t[:, :], b_in[o].rearrange("(a n) -> a n", a=1))
            if w_out is not None:
                load(w_o[:, :, :], w_out.rearrange("(k p) n -> p k n", p=P))
            with sp.Fori(0, CHUNKS) as c:
                sp.wait_ge(act_s.sem, act_s.at(f"proj{CW - 1}_{n_outs - 1}", c))
                for table, product, low, high in outs:
                    sp.dma_start(chunk_rows(table, c), stage[product][:, :, low:high]).then_inc(stored, 16)
            sp.wait_ge(stored, 16 * len(outs) * (CHUNKS + 1))

        @block.gpsimd
        def _(pool):
            nc.gpsimd.memset(ones_row[:, :], 1.0).then_inc(ready, 1)

        @block.tensor
        def _(pe):
            pe.sem_inc(pe_s.sem, pe_s.start)
            pe.wait_ge(weights_in, 16 * n_in)
            pe.wait_ge(ready, 1)
            if next_att:
                pe.wait_ge(lin_ready, 2 * KI * LH)
            with pe.Fori(0, CHUNKS) as c:
                if w_out is not None:
                    pe.wait_ge(dve_s.sem, dve_s.at("taken", c))
                    pe.wait_ge(act_s.sem, act_s.at("x_t", c - 1))
                    for w in range(CW):
                        for kc in range(KI):
                            mm = nc.tensor.transpose(turn[:, kc * CW + w, :], y[:, w, kc * P:(kc + 1) * P], m.ident[:, :])
                    mm.then_inc(pe_s.sem, 1)
                    pe.wait_ge(act_s.sem, act_s.at("y_t", c))
                    pe.wait_ge(act_s.sem, act_s.at(f"proj{CW - 1}_{n_outs - 1}", c - 1))
                    for w in range(CW):
                        for kc in range(KI):
                            mm = nc.tensor.matmul(flat[:, w, :], y_t[:, kc * CW + w, :], w_o[:, kc, :], start=(kc == 0), stop=(kc == KI - 1))
                    mm.then_inc(pe_s.sem, 1)
                pe.wait_ge(dve_s.sem, dve_s.at("c_normed" if residual else "relu", c))
                pe.wait_ge(act_s.sem, act_s.at("lin" if next_att else "x_t", c - 1))
                settle(pe)
                for w in range(CW):
                    for kc in range(KX):
                        if w_in:
                            piece = y[:, w, kc * P:(kc + 1) * P]
                        else:
                            piece = y[:, w, 0:C3] if kc == 0 else y[:, w, C3 + kc - 1:D:3]
                        mm = nc.tensor.transpose(turn[0:PX, kc * CW + w, :], piece, m.ident[:, :])
                mm.then_inc(pe_s.sem, 1)
                pe.wait_ge(act_s.sem, act_s.at("x_t", c))
                pe.wait_ge(act_s.sem, act_s.at(f"proj{CW - 1}_{n_outs - 1}", c - 1))
                if next_att:
                    project_linear(pe, pe_s, lambda kc, w: x_t[:, kc * CW + w, :], w_lin, KI, LH, turn)
                if w_in:
                    project(pe, pe_s, act_s, c, lambda kc, w: x_t[:, kc * CW + w, :],
                            [pieces(w_sb[o], KI, 0, widths[o]) for o in range(2)], [b[:, :] for b in b_sb], ring, ones_row[:, :])
                else:
                    for w in range(CW):
                        if w >= 3:
                            pe.wait_ge(act_s.sem, act_s.at(f"proj{w - 3}_0", c))
                        for i in range(4):
                            mm = nc.tensor.matmul(ring[:, w % 3, i * P:(i + 1) * P], x_t[0:C3, i * CW + w, :],
                                                  w_sb[0][:, i, :, :].rearrange("p t c -> p (t c)"), start=True, stop=True)
                        mm.then_inc(pe_s.sem, 1)

        @block.scalar
        def _(act):
            act.sem_inc(act_s.sem, act_s.start)
            act.sem_inc(stored, 16 * len(outs))
            with act.Fori(0, CHUNKS) as c:
                if w_out is not None:
                    act.wait_ge(pe_s.sem, pe_s.at("y_t", c))
                    nc.scalar.copy(y_t[:, :, :], turn[:, 0:KI * CW, :]).then_inc(act_s.sem, 1)
                if residual:
                    standard_deviation(act, dve_s, act_s, c, "c", nb)
                act.wait_ge(pe_s.sem, pe_s.at("x_t", c))
                nc.scalar.copy(x_t[0:PX, :, :], turn[0:PX, 0:KX * CW, :]).then_inc(act_s.sem, 1)
                act.wait_ge(stored, 16 * len(outs) * (c + 1))
                if next_att:
                    keep_linear(act, pe_s, act_s, c, turn, stage, widths, LH)
                for w in range(CW):
                    act.wait_ge(pe_s.sem, pe_s.at(f"proj{w}_0", c))
                    if w_in:
                        nc.scalar.copy(stage[0][:, w, 0:widths[0]], ring[:, (2 * w) % 3, 0:widths[0]]).then_inc(act_s.sem, 1)
                        act.wait_ge(pe_s.sem, pe_s.at(f"proj{w}_1", c))
                        nc.scalar.mul(stage[1][:, w, 0:widths[1]], ring[:, (2 * w + 1) % 3, 0:widths[1]], own_scale).then_inc(act_s.sem, 1)
                    else:
                        both = ring[:, w % 3, :].rearrange("p (i t c) -> p i t c", i=4, t=2)
                        nc.scalar.copy(stage[0][:, w, :].rearrange("p (i c) -> p i c", i=4), both[:, :, 0, :])
                        to_own = own[:, bass.ds(c * CW + w, 1), :].rearrange("p a n -> p (a n)")
                        nc.scalar.copy(to_own.rearrange("p (i c) -> p i c", i=4), both[:, :, 1, :]).then_inc(act_s.sem, 1)

        @block.vector
        def _(dve):
            dve.sem_inc(dve_s.sem, dve_s.start)
            dve.wait_ge(weights_in, 16 * n_in)
            if next_att:
                linear_weights(dve, w_lin, w_sb, *next_att, lin_ready)
            with dve.Fori(0, CHUNKS) as c:
                def link(name, ins):
                    ins.then_inc(dve_s.sem, 1)
                    dve.wait_ge(dve_s.sem, dve_s.at(name, c))

                dve.wait_ge(pe_s.sem, pe_s.at("x_t", c - 1))
                chunk = total[:, bass.ds(c * CW, CW), :]
                if w_out is not None:
                    settle(dve)
                    link("taken", nc.vector.tensor_copy(y[:, :, :], chunk))
                else:
                    dve.sem_inc(dve_s.sem, 1)
                if w_out is not None:
                    dve.wait_ge(pe_s.sem, pe_s.at("out", c))
                    link("biased", nc.vector.tensor_tensor(y[:, :, :], flat, over_windows(bias_row[:, :]), ALU.add))
                else:
                    link("biased", nc.vector.tensor_tensor(y[:, :, :], chunk, over_windows(bias_row[:, :]), ALU.add))
                if residual:
                    x = m.xs[:, bass.ds(c * CW, CW), :]
                    link("xr", nc.vector.tensor_tensor(y[:, :, :], y[:, :, :], x, ALU.add))
                    layer_norm(dve, link, act_s, c, "c", y, y, nb, 1e-5)
                    settle(dve)
                    link("kept", nc.vector.tensor_copy(x, y[:, :, :]))
                else:
                    link("relu", nc.vector.tensor_scalar(y[:, :, :], y[:, :, :], 0.0, None, ALU.max))


def reload_steps(nc, o):
    with ExitStack() as ctx:
        listed = ctx.enter_context(nc.semaphore("relisted"))
        block = ctx.enter_context(nc.Block())

        @block.sync
        def _(sp):
            sp.dma_start(o.gk[:, :], o.gk_d.rearrange("(a k) -> a k", a=1)).then_inc(listed, 16)
            sp.dma_start(o.wk[:, :], o.wk_d.rearrange("(a k) -> a k", a=1)).then_inc(listed, 16)
            sp.wait_ge(listed, 32)


def edge_messages(nc, m, o, table, total):
    with ExitStack() as ctx:
        one = lambda n, s, d=F32: ctx.enter_context(nc.sbuf_tensor(f"e3_{n}", s, d))
        two = lambda n, s, d=F32: [one(f"{n}{b}", s, d) for b in range(2)]
        bank = lambda n, w=512: ctx.enter_context(nc.psum_tensor(f"e3_{n}", [P, w], F32))
        sem = lambda n: ctx.enter_context(nc.semaphore(f"e3_{n}"))
        idx, dst_c = two("idx", [P, J], I32), two("dst_c", [P, J])
        sh, rbf = two("sh", [P, J, 4]), two("rbf", [D_EA16, GE])
        rel, hot = two("rel", [P, J]), two("hot", [P, J, P])
        rows = two("rows", [P, J, D])
        by_sh = two("by_sh", [P, J, 3, C3])
        dot = two("dot", [P, J, C3])
        by_sh0 = two("by_sh0", [P, J, 4, C3])
        scalar_part, x0_part = one("scalar_part", [P, J, C3]), one("x0_part", [P, J, C3])
        vector_part = one("vector_part", [P, J, 3, C3])
        message = two("message", [P, J, 4, C3])
        m1, m2, m3, m4 = one("m1", [D_EA16, C3]), one("m2", [C3, C3]), one("m3", [C3, C3]), one("m4", [C3, D])
        r = [one(f"r{l}", [C3, GE]) for l in range(3)]
        z = [bank(f"z{l}") for l in range(2)]
        tp = [bank(f"tp{b}", J * D) for b in range(2)]
        sums = [bank(f"sums{b}") for b in range(2)]
        weights_in, zeroed = sem("weights"), sem("zeroed")
        loaded = [sem(f"loaded{b}") for b in range(2)]
        gathered = [m.dma_sem(f"e3_gathered{b}") for b in range(2)]
        pe_f, act_f = Stages(sem("mlp"), ["z0", "z1", "z2", "tp"]), Stages(sem("silu"), ["r0", "r1", "r2"])
        pe_b = Stages(sem("sums"), ["sum"])
        dve_f = Stages(sem("dve_front"), ["rel", "hot", "by_sh0", "by_sh", "dot2", "dot"])
        dve_b = Stages(sem("dve_back"), ["tp0", "tp3", "m0", "x0_part", "tp2", "tp1", "m1", "merged"])
        block = ctx.enter_context(nc.Block())

        @block.sync
        def _(sp):
            for to, of in ((m1, m.inputs["L3_M1"]), (m2, m.inputs["L3_M2"]), (m3, m.inputs["L3_M3"]), (m4, m.inputs["L3_M4"])):
                sp.dma_start(to[:, :], of).then_inc(weights_in, 16)

            def front(k, i, b):
                g = group_of(sp, o, k)
                part = bass.ds(g * GE, GE)
                sp.wait_ge(dve_b.sem, dve_b.at("m1", k - 2))
                settle(sp)
                sp.wait_ge(pe_f.sem, pe_f.at("z0", k - 2))
                settle(sp)
                sp.dma_start(idx[b][:, :], o.other[part].rearrange("(p j) -> p j", j=J)).then_inc(loaded[b], 16)
                sp.dma_start(dst_c[b][:, :], o.key_f[part].rearrange("(p j) -> p j", j=J)).then_inc(loaded[b], 16)
                sp.dma_start(sh[b][:, :, :], m.inputs["ea4"][part, :].rearrange("(p j) c -> p j c", j=J)).then_inc(loaded[b], 16)
                sp.dma_start(rbf[b][:, :], m.inputs["rbf_t"][bass.ds(g * D_EA16, D_EA16), :]).then_inc(loaded[b], 16)
            drive(sp, o, front)

        @block.gpsimd
        def _(pool):
            nc.gpsimd.memset(total[:, :, :], 0.0).then_inc(zeroed, 1)

            def front(k, i, b):
                pool.wait_ge(loaded[b], 64 * (i + 1))
                settle(pool)
                for j in range(J):
                    pool.indirect_dma_start(
                        out=rows[b][:, j, :], out_offset=None, in_=table,
                        in_offset=bass.IndirectOffsetOnAxis(ap=idx[b][:, j:j + 1], axis=0)).then_inc(gathered[b], 16)
            drive(pool, o, front)

        @block.tensor
        def _(pe):
            for s in (pe_f, pe_b):
                pe.sem_inc(s.sem, s.start)
            pe.wait_ge(weights_in, 64)

            def front(k, i, b):
                pe.wait_ge(loaded[b], 64 * (i + 1))
                pe.wait_ge(act_f.sem, act_f.at("r2", k - 1))
                nc.tensor.matmul(z[0][0:C3, :], m1[:, :], rbf[b][:, :], start=True, stop=True).then_inc(pe_f.sem, 1)
                pe.wait_ge(act_f.sem, act_f.at("r0", k))
                settle(pe)
                nc.tensor.matmul(z[1][0:C3, :], m2[:, :], r[0][:, :], start=True, stop=True).then_inc(pe_f.sem, 1)
                pe.wait_ge(act_f.sem, act_f.at("r1", k))
                settle(pe)
                nc.tensor.matmul(z[0][0:C3, :], m3[:, :], r[1][:, :], start=True, stop=True).then_inc(pe_f.sem, 1)
                pe.wait_ge(act_f.sem, act_f.at("r2", k))
                pe.wait_ge(dve_b.sem, dve_b.at("tp1", k - 2))
                for j in range(J):
                    mm = nc.tensor.matmul(tp[b][:, j * D:(j + 1) * D], r[2][:, j * P:(j + 1) * P], m4[:, :], start=True, stop=True)
                mm.then_inc(pe_f.sem, 1)

            def back(k, i, b):
                pe.wait_ge(dve_b.sem, dve_b.at("merged", k - 2))
                pe.wait_ge(dve_b.sem, dve_b.at("m1", k))
                for j in range(J):
                    mm = nc.tensor.matmul(sums[b][:, 0:D], hot[b][:, j, :], message[b][:, j, :, :].rearrange("p t c -> p (t c)"),
                                          start=(j == 0), stop=(j == J - 1))
                mm.then_inc(pe_b.sem, 1)
            drive(pe, o, front, back)

        @block.scalar
        def _(act):
            act.sem_inc(act_f.sem, act_f.start)

            def front(k, i, b):
                for l in range(3):
                    if l == 0:
                        act.wait_ge(pe_f.sem, pe_f.at("tp", k - 1))
                    act.wait_ge(pe_f.sem, pe_f.at(f"z{l}", k))
                    nc.scalar.activation(r[l][:, :], z[l % 2][0:C3, :], ACT.Silu).then_inc(act_f.sem, 1)
            drive(act, o, front, None)

        @block.vector
        def _(dve):
            for s in (dve_f, dve_b):
                dve.sem_inc(s.sem, s.start)
            dve.wait_ge(zeroed, 1)

            def front(k, i, b):
                def link(name, ins):
                    ins.then_inc(dve_f.sem, 1)
                    dve.wait_ge(dve_f.sem, dve_f.at(name, k))

                w = window_of(dve, o, k)
                dve.wait_ge(loaded[b], 64 * (i + 1))
                link("rel", nc.vector.tensor_scalar(rel[b][:, :], dst_c[b][:, :], m.base[:, bass.ds(w, 1)], None, ALU.subtract))
                dve.wait_ge(pe_b.sem, pe_b.at("sum", k - 2))
                for j in range(J):
                    ins = nc.vector.tensor_scalar(hot[b][:, j, :], m.iota[:, :], rel[b][:, j:j + 1], None, ALU.is_equal)
                ins.then_inc(dve_f.sem, 1)
                dve.wait_ge(gathered[b], 16 * J * (i + 1))
                x = rows[b][:, :, :].rearrange("p j (t c) -> p j t c", t=4)
                nc.vector.tensor_tensor(by_sh0[b][:, :, :, :].rearrange("p j t c -> p j (t c)"), rows[b][:, :, :],
                                        sh[b][:, :, 0:1].broadcast_to([P, J, D]), ALU.mult).then_inc(dve_f.sem, 1)
                link("by_sh", nc.vector.tensor_tensor(by_sh[b][:, :, :, :], x[:, :, 1:4, :], sh[b][:, :, 1:4].unsqueeze(3).broadcast_to([P, J, 3, C3]), ALU.mult))
                link("dot2", nc.vector.tensor_tensor(dot[b][:, :, :], by_sh[b][:, :, 0, :], by_sh[b][:, :, 1, :], ALU.add))
                nc.vector.tensor_tensor(dot[b][:, :, :], dot[b][:, :, :], by_sh[b][:, :, 2, :], ALU.add).then_inc(dve_f.sem, 1)

            def back(k, i, b):
                def link(name, ins):
                    ins.then_inc(dve_b.sem, 1)
                    dve.wait_ge(dve_b.sem, dve_b.at(name, k))

                w = window_of(dve, o, k)
                x = rows[b][:, :, :].rearrange("p j (t c) -> p j t c", t=4)
                t = tp[b][:, :].rearrange("p (j t c) -> p j t c", j=J, t=4)
                dve.wait_ge(dve_f.sem, dve_f.at("dot", k))
                dve.wait_ge(pe_f.sem, pe_f.at("tp", k))
                dve.wait_ge(pe_b.sem, pe_b.at("sum", k - 2))
                nc.vector.tensor_tensor(message[b][:, :, 0, :], t[:, :, 0, :], by_sh0[b][:, :, 0, :], ALU.mult).then_inc(dve_b.sem, 1)
                link("tp3", nc.vector.scalar_tensor_tensor(scalar_part[:, :, :], t[:, :, 3, :], float(3 ** -0.5), dot[b][:, :, :], ALU.mult, ALU.mult))
                nc.vector.tensor_tensor(message[b][:, :, 0, :], message[b][:, :, 0, :], scalar_part[:, :, :], ALU.add).then_inc(dve_b.sem, 1)
                link("x0_part", nc.vector.tensor_tensor(x0_part[:, :, :], t[:, :, 1, :], x[:, :, 0, :], ALU.mult))
                nc.vector.tensor_tensor(message[b][:, :, 1:4, :], by_sh0[b][:, :, 1:4, :],
                                        t[:, :, 2:3, :].broadcast_to([P, J, 3, C3]), ALU.mult).then_inc(dve_b.sem, 1)
                link("tp1", nc.vector.tensor_tensor(vector_part[:, :, :, :], x0_part[:, :, :].unsqueeze(2).broadcast_to([P, J, 3, C3]),
                                                    sh[b][:, :, 1:4].unsqueeze(3).broadcast_to([P, J, 3, C3]), ALU.mult))
                nc.vector.tensor_tensor(message[b][:, :, 1:4, :], message[b][:, :, 1:4, :], vector_part[:, :, :, :], ALU.add).then_inc(dve_b.sem, 1)
                dve.wait_ge(pe_b.sem, pe_b.at("sum", k))
                dve.wait_ge(dve_b.sem, dve_b.at("merged", k - 1))
                a = total[:, bass.ds(w, 1), :].rearrange("p a c -> p (a c)")
                nc.vector.tensor_tensor(a, a, sums[b][:, 0:D], ALU.add).then_inc(dve_b.sem, 1)
            drive(dve, o, front, back)


def nodes_3(nc, m, total, own, out):
    with ExitStack() as ctx:
        one = lambda n, s, d=F32: ctx.enter_context(nc.sbuf_tensor(f"n4_{n}", s, d))
        sem = lambda n: ctx.enter_context(nc.semaphore(f"n4_{n}"))
        rows = {n: one(n, [P, C3]) for n in ("gamma0", "beta0", "gamma1")}
        coef = one("coef", [P, 9, C3])
        w_lin, w_b = one("w_lin", [C3, 4, C3]), one("w_b", [C3, 4, C3])
        weights_in = sem("weights")

        with ExitStack() as first:
            tmp = lambda n, s: first.enter_context(nc.sbuf_tensor(f"n4_{n}", s, F32))
            turned = tmp("turned", [C3, 4 * CW, P])
            a, b = tmp("a", [P, CW, 4, C3]), tmp("b", [P, CW, 4, C3])
            squares = tmp("squares", [P, CW, 3, C3])
            vv, aa, part, poly0, poly1 = (tmp(n, [P, CW, C3]) for n in ("vv", "aa", "part", "poly0", "poly1"))
            turn = first.enter_context(nc.psum_tensor("n4_turn", [P, 20, P], F32))
            ring = first.enter_context(nc.psum_tensor("n4_ring", [P, 1536], F32))
            flat = ring[:, 0:CW * D].rearrange("p (w i c) -> p w i c", w=CW, i=4)
            pe_s = Stages(sem("pe"), ["msg_t", "a", "b_t", "o"])
            act_s = Stages(sem("act"), ["msg", "msg_t", "a", "b_t"])
            steps = ["aa", "sq", "vv2", "vv", "w1", "w0", "w3", "+w3", "w4", "+w4", "poly0", "w2", "b0",
                     "w6", "w5", "w7", "+w7", "w8", "+w8", "b1", "o"]
            dve_s = Stages(sem("dve"), steps)
            block = first.enter_context(nc.Block())

            @block.sync
            def _(sp):
                load = lambda to, of: sp.dma_start(to, of).then_inc(weights_in, 16)
                for n, of in (("gamma0", m.inputs["L3_gamma0"]), ("beta0", m.inputs["L3_beta0"]), ("gamma1", m.inputs["L3_gamma1"])):
                    load(rows[n][:, :], row_everywhere(of))
                load(coef[:, :, :].rearrange("p t c -> p (t c)"), row_everywhere(m.inputs["L3_Wc"]))
                for i in range(4):
                    load(w_lin[:, i, :], m.inputs["L3_W_lin1"] if i else m.inputs["L3_W_lin0"])
                    load(w_b[:, i, :], m.inputs["L3_WB1"] if i else m.inputs["L3_WB0"])
                sp.wait_ge(weights_in, 12 * 16)

            @block.tensor
            def _(pe):
                pe.sem_inc(pe_s.sem, pe_s.start)
                pe.wait_ge(weights_in, 12 * 16)
                with pe.Fori(0, CHUNKS) as c:
                    for phase in range(2):
                        if phase:
                            pe.wait_ge(dve_s.sem, dve_s.at("b1", c))
                        else:
                            pe.wait_ge(act_s.sem, act_s.at("msg", c))
                        settle(pe)
                        for i in range(4):
                            for w in range(CW):
                                mm = nc.tensor.transpose(turn[0:C3, i * CW + w, :], (b if phase else a)[:, w, i, :], m.ident[:, :])
                        mm.then_inc(pe_s.sem, 1)
                        pe.wait_ge(act_s.sem, act_s.at("b_t" if phase else "msg_t", c))
                        if phase == 0:
                            pe.wait_ge(dve_s.sem, dve_s.at("o", c - 1))
                        for w in range(CW):
                            for i in range(4):
                                mm = nc.tensor.matmul(flat[:, w, i, :], turned[:, i * CW + w, :], (w_b if phase else w_lin)[:, i, :], start=True, stop=True)
                        mm.then_inc(pe_s.sem, 1)

            @block.scalar
            def _(act):
                act.sem_inc(act_s.sem, act_s.start)
                with act.Fori(0, CHUNKS) as c:
                    act.wait_ge(dve_s.sem, dve_s.at("b1", c - 1))
                    nc.scalar.copy(a[:, :, :, :].rearrange("p w i c -> p w (i c)"), total[:, bass.ds(c * CW, CW), :]).then_inc(act_s.sem, 1)
                    act.wait_ge(pe_s.sem, pe_s.at("msg_t", c))
                    nc.scalar.copy(turned[:, :, :], turn[0:C3, :, :]).then_inc(act_s.sem, 1)
                    act.wait_ge(pe_s.sem, pe_s.at("a", c))
                    nc.scalar.copy(a[:, :, :, :], flat).then_inc(act_s.sem, 1)
                    act.wait_ge(pe_s.sem, pe_s.at("b_t", c))
                    nc.scalar.copy(turned[:, :, :], turn[0:C3, :, :]).then_inc(act_s.sem, 1)

            @block.vector
            def _(dve):
                dve.sem_inc(dve_s.sem, dve_s.start)
                dve.wait_ge(weights_in, 12 * 16)
                with dve.Fori(0, CHUNKS) as c:
                    def link(name, ins):
                        ins.then_inc(dve_s.sem, 1)
                        dve.wait_ge(dve_s.sem, dve_s.at(name, c))

                    tt = nc.vector.tensor_tensor
                    row = lambda t: over_windows(coef[:, t, :])
                    a0 = a[:, :, 0, :]
                    dve.wait_ge(act_s.sem, act_s.at("a", c))
                    link("aa", tt(aa[:, :, :], a0, a0, ALU.mult))
                    link("sq", tt(squares[:, :, :, :], a[:, :, 1:4, :], a[:, :, 1:4, :], ALU.mult))
                    link("vv2", tt(vv[:, :, :], squares[:, :, 0, :], squares[:, :, 1, :], ALU.add))
                    link("vv", tt(vv[:, :, :], vv[:, :, :], squares[:, :, 2, :], ALU.add))
                    link("w1", tt(poly0[:, :, :], a0, row(1), ALU.mult))
                    link("w0", tt(poly0[:, :, :], poly0[:, :, :], row(0), ALU.add))
                    for name, t, factor in (("w3", 3, aa), ("w4", 4, vv)):
                        link(name, tt(part[:, :, :], factor[:, :, :], row(t), ALU.mult))
                        link("+" + name, tt(poly0[:, :, :], poly0[:, :, :], part[:, :, :], ALU.add))
                    link("poly0", tt(poly0[:, :, :], poly0[:, :, :], a0, ALU.mult))
                    link("w2", tt(part[:, :, :], vv[:, :, :], row(2), ALU.mult))
                    link("b0", tt(b[:, :, 0, :], poly0[:, :, :], part[:, :, :], ALU.add))
                    link("w6", tt(poly1[:, :, :], a0, row(6), ALU.mult))
                    link("w5", tt(poly1[:, :, :], poly1[:, :, :], row(5), ALU.add))
                    for name, t, factor in (("w7", 7, aa), ("w8", 8, vv)):
                        link(name, tt(part[:, :, :], factor[:, :, :], row(t), ALU.mult))
                        link("+" + name, tt(poly1[:, :, :], poly1[:, :, :], part[:, :, :], ALU.add))
                    link("b1", tt(b[:, :, 1:4, :], a[:, :, 1:4, :], poly1[:, :, :].unsqueeze(2).broadcast_to([P, CW, 3, C3]), ALU.mult))
                    dve.wait_ge(pe_s.sem, pe_s.at("o", c))
                    chunk = bass.ds(c * CW, CW)
                    tt(total[:, chunk, :].rearrange("p w (i n) -> p w i n", i=4), flat, own[:, chunk, :].rearrange("p w (i n) -> p w i n", i=4),
                       ALU.add).then_inc(dve_s.sem, 1)

        with ExitStack() as second:
            tmp = lambda n, s: second.enter_context(nc.sbuf_tensor(f"n4_{n}", s, F32))
            ones, real = tmp("ones", [P, P]), tmp("real", [P, P])
            mean, moment = tmp("mean", [P, C3]), tmp("moment", [P, 2, C3])
            root, scale = tmp("root", [P, 2, C3]), tmp("scale", [P, 2, C3])
            squares = tmp("squares_o", [P, CW, D])
            y = [tmp(f"y{i}", [P, CW, D]) for i in range(2)]
            nb = NormBuffers(tmp)
            mean_ps = second.enter_context(nc.psum_tensor("n4_mean_ps", [P, 512], F32))
            square_ps = second.enter_context(nc.psum_tensor("n4_square_ps", [P, 512], F32))
            ready, stat, pe_done, act_done = sem("ready"), sem("stat"), sem("stat_pe"), sem("stat_act")
            squared, used = Stages(sem("squared"), ["centred", "square"]), sem("used")
            stored = sem("stored")
            act_s = Stages(sem("norm_act"), ["c_std"])
            dve_s = Stages(sem("norm_dve"), ["scaled0", "scaled1", "shifted", "xr"] + norm_stages("c"))
            block = second.enter_context(nc.Block())

            @block.sync
            def _(sp):
                def store(c, i):
                    sp.wait_ge(dve_s.sem, dve_s.at("c_normed", c))
                    settle(sp)
                    sp.dma_start(out[bass.ds(c * CW * P, CW * P), :].rearrange("(w p) d -> p w d", p=P), y[i][:, :, :]).then_inc(stored, 16)

                with sp.Fori(0, CHUNKS // 2) as h:
                    for i in range(2):
                        store(2 * h + i, i)
                store(CHUNKS - 1, 0)
                sp.wait_ge(stored, 16 * (CHUNKS + 1))

            @block.gpsimd
            def _(pool):
                nc.gpsimd.memset(ones[:, :], 1.0).then_inc(ready, 1)

            @block.tensor
            def _(pe):
                pe.wait_ge(stat, 1)
                nc.tensor.matmul(mean_ps[:, 0:C3], real[:, :], total[:, WN - 1, 0:C3], start=True, stop=True)
                with pe.Fori(0, WN - 2) as w:
                    nc.tensor.matmul(mean_ps[:, 0:C3], ones[:, :], total[:, bass.ds(w, 1), 0:C3].rearrange("p a c -> p (a c)"),
                                     start=False, stop=True, skip_group_check=True)
                nc.tensor.matmul(mean_ps[:, 0:C3], ones[:, :], total[:, WN - 2, 0:C3], start=False, stop=True, skip_group_check=True).then_inc(pe_done, 1)

                def squares_of(c, first=False, last=False):
                    pe.wait_ge(squared.sem, squared.at("square", c))
                    for w in range(CW):
                        mm = nc.tensor.matmul(square_ps[:, 0:D], (real if last and w == CW - 1 else ones)[:, :], squares[:, w, :],
                                              start=first and w == 0, stop=True, skip_group_check=True)
                    mm.then_inc(used, 1)

                squares_of(0, first=True)
                with pe.Fori(1, CHUNKS - 1) as c:
                    squares_of(c)
                squares_of(CHUNKS - 1, last=True)

            @block.scalar
            def _(act):
                act.sem_inc(act_s.sem, act_s.start)
                act.wait_ge(stat, 5)
                nc.scalar.activation(root[:, :, :], moment[:, :, :], ACT.Sqrt).then_inc(act_done, 1)
                with act.Fori(0, CHUNKS) as c:
                    standard_deviation(act, dve_s, act_s, c, "c", nb)

            @block.vector
            def _(dve):
                n = [0]

                def stage(ins):
                    n[0] += 1
                    ins.then_inc(stat, 1)
                    dve.wait_ge(stat, n[0])

                dve.sem_inc(squared.sem, squared.start)
                dve.sem_inc(dve_s.sem, dve_s.start)
                dve.sem_inc(used, 1)
                dve.sem_inc(stored, 16)
                dve.wait_ge(ready, 1)
                stage(nc.vector.tensor_scalar(real[:, :], m.node[:, 0:1].broadcast_to([P, P]), float(N_NODES - (WN - 1) * P), None, ALU.is_lt))
                dve.wait_ge(pe_done, 1)
                stage(nc.vector.tensor_scalar(mean[:, :], mean_ps[:, 0:C3], 1.0 / N_NODES, None, ALU.mult))
                with dve.Fori(0, CHUNKS) as c:
                    centred = total[:, bass.ds(c * CW, CW), 0:C3]
                    nc.vector.tensor_tensor(centred, centred, over_windows(mean[:, :]), ALU.subtract).then_inc(squared.sem, 1)
                    dve.wait_ge(squared.sem, squared.at("centred", c))
                    dve.wait_ge(used, c + 1)
                    chunk = total[:, bass.ds(c * CW, CW), :]
                    nc.vector.tensor_tensor(squares[:, :, :], chunk, chunk, ALU.mult).then_inc(squared.sem, 1)
                dve.wait_ge(used, CHUNKS + 1)
                eps = 1e-5
                stage(nc.vector.tensor_scalar(moment[:, 0, :], square_ps[:, 0:C3], 1.0 / N_NODES, eps, ALU.mult, ALU.add))
                stage(nc.vector.tensor_reduce(moment[:, 1, :], square_ps[:, C3:D].rearrange("p (x c) -> p c x", x=3), AX.X, ALU.add))
                stage(nc.vector.tensor_scalar(moment[:, 1, :], moment[:, 1, :], 1.0 / (3.0 * N_NODES), eps, ALU.mult, ALU.add))
                dve.wait_ge(act_done, 1)
                stage(nc.vector.reciprocal(scale[:, :, :], root[:, :, :]))
                stage(nc.vector.tensor_tensor(scale[:, 0, :], scale[:, 0, :], rows["gamma0"][:, :], ALU.mult))
                stage(nc.vector.tensor_tensor(scale[:, 1, :], scale[:, 1, :], rows["gamma1"][:, :], ALU.mult))

                def finish(c, i, before):
                    def link(name, ins):
                        ins.then_inc(dve_s.sem, 1)
                        dve.wait_ge(dve_s.sem, dve_s.at(name, c))

                    chunk = bass.ds(c * CW, CW)
                    dve.wait_ge(stored, before)
                    nc.vector.tensor_tensor(y[i][:, :, 0:C3], total[:, chunk, 0:C3], over_windows(scale[:, 0, :]), ALU.mult).then_inc(dve_s.sem, 1)
                    link("scaled1", nc.vector.tensor_tensor(y[i][:, :, C3:D].rearrange("p w (c x) -> p w x c", x=3),
                                                            total[:, chunk, C3:D].rearrange("p w (x c) -> p w x c", x=3),
                                                            scale[:, 1:2, :].unsqueeze(1).broadcast_to([P, CW, 3, C3]), ALU.mult))
                    link("shifted", nc.vector.tensor_tensor(y[i][:, :, 0:C3], y[i][:, :, 0:C3], over_windows(rows["beta0"][:, :]), ALU.add))
                    link("xr", nc.vector.tensor_tensor(y[i][:, :, :], y[i][:, :, :], m.xs[:, chunk, :], ALU.add))
                    layer_norm(dve, link, act_s, c, "c", y[i], y[i], nb, 1e-5)

                with dve.Fori(0, CHUNKS // 2) as h:
                    for i in range(2):
                        finish(2 * h + i, i, 16 * 2 * h + 16)
                finish(CHUNKS - 1, 0, 16 * CHUNKS)
def build(nc, a, out):
    m = Model(a)
    dram = lambda n, s, d=F32: nc.dram_tensor(n, s, d, kind="Internal").ap()
    as_given = Order(dram, "as_given", NG, a["dst"], a["src"])
    by_dst, by_row = Sorted(dram, "by_dst", NGS, a["pairs_by_dst"]), Sorted(dram, "by_row", NG, a["pairs_by_row"])
    source_1, target_1 = dram("source_1", (NP, 512 + 4)), dram("target_1", (NP + P, 512 + 4))
    source_2, target_2 = dram("source_2", (NP, 256 + 1)), dram("target_2", (NP + P, 256 + 1))
    table_k, table_v, table_q = dram("table_k", (NP, 256)), dram("table_v", (NP, 256)), dram("table_q", (NP + P, 256))
    table_up = dram("table_up", (NP, 256))
    prob_1, prob_2, prob_3 = dram("prob_1", (EPS, 4)), dram("prob_2", (EPS, 1)), dram("prob_3", (EP, 8))
    with ExitStack() as ctx:
        sb = lambda n, s, d=F32: ctx.enter_context(nc.sbuf_tensor(n, s, d))
        m.dma_sem = lambda n: ctx.enter_context(nc.semaphore(n))
        m.ident, m.iota = sb("ident", [P, P]), sb("iota", [P, P])
        m.node, m.base = sb("node", [P, WX]), sb("base", [P, WX])
        gk, wk = sb("gk", [1, KMAX], I32), sb("wk", [1, KMAX], I32)
        for n, o in (("as_given", as_given), ("by_dst", by_dst), ("by_row", by_row)):
            o.gk, o.wk, o.pairs = gk, wk, sb(f"{n}_pairs", [1, 1], I32)
        att = {"a1": sb("att1", [P, 512]), "a2": sb("att2", [P, 256])}
        build_steps(nc, m, as_given, "d_")
        m.xs = sb("xs", [P, WN, D])
        load_nodes(nc, m, att, (target_1, target_2, table_q))
        own = sb("own", [P, WX, D])
        with ExitStack() as life:
            agg = life.enter_context(nc.sbuf_tensor("agg", [P, WX, D + D_EA64], F32))
            edge_sums(nc, m, as_given, "e0", a["x"], D, agg, attr=a["ea64"])
            nodes_0(nc, m, agg, source_1, target_1, att["a1"], 4, 128)
        sort_edges(nc, m, by_dst, "sd")
        build_steps(nc, m, by_dst, "s_")
        with ExitStack() as life:
            total = life.enter_context(nc.sbuf_tensor("total_1", [P, WX, 512], F32))
            attention(nc, m, by_dst, "a1", 4, 128, source_1, target_1, source_1, prob_1, total, att["a1"])
            nodes_att(nc, m, "n1", total, 512, a["L1_b1"], [(source_2, 0, 0, 257), (target_2, 1, 0, 257)],
                      w_in=(a["L1_W2l"], a["L1_W2r"]), residual=False, next_att=(att["a2"], 1, 256))
        total = sb("total", [P, WX, D])
        attention(nc, m, by_dst, "a2", 1, 256, source_2, target_2, source_2, prob_2, total, att["a2"])
        nodes_att(nc, m, "n2", total, 256, a["L1_b2"], [(table_k, 0, 0, 256), (table_v, 0, 256, 512), (table_q, 1, 0, 256)],
                  w_in=(a["L2_Wkv"], a["L2_Wq"]), b_in=(a["L2_bkv"], a["L2_bq"]), own_scale=float(32 ** -0.5))
        clear_semaphores(nc)
        sort_edges(nc, m, by_row, "sr")
        build_steps(nc, m, by_row, "r_")
        attention(nc, m, by_row, "a3", 8, 32, table_k, table_q, table_v, prob_3, total)
        nodes_att(nc, m, "n3", total, 256, a["L2_bo"], [(table_up, 0, 0, 256)], w_out=a["L2_Wo"], own=own)
        reload_steps(nc, as_given)
        edge_messages(nc, m, as_given, table_up, total)
        nodes_3(nc, m, total, own, out)


def clear_semaphores(nc):
    done = sorted(nc.released_uncleared_semaphores)
    nc.gpsimd.sem_clear(range(done[0], done[-1] + 1))
    nc.all_engine_barrier()


def load_nodes(nc, m, att, targets):
    with ExitStack() as ctx:
        loaded, zeroed = ctx.enter_context(nc.semaphore("x_loaded")), ctx.enter_context(nc.semaphore("x_zeroed"))
        zeros = ctx.enter_context(nc.sbuf_tensor("x_zeros", [P, 516], F32))
        block = ctx.enter_context(nc.Block())

        @block.sync
        def _(sp):
            sp.dma_start(m.xs[:, :, :], m.inputs["x"].rearrange("(w p) d -> p w d", p=P)).then_inc(loaded, 16)
            sp.dma_start(att["a1"][:, :], row_everywhere(m.inputs["L1_a1"])).then_inc(loaded, 16)
            sp.dma_start(att["a2"][:, :], row_everywhere(m.inputs["L1_a2"])).then_inc(loaded, 16)
            sp.wait_ge(zeroed, 1)
            for t in targets:
                sp.dma_start(t[NP:NP + P, :], zeros[:, 0:t.shape[-1]]).then_inc(loaded, 16)
            sp.wait_ge(loaded, 16 * (3 + len(targets)))

        @block.gpsimd
        def _(pool):
            nc.gpsimd.memset(zeros[:, :], 0.0).then_inc(zeroed, 1)


def kernel(**inputs):
    import numpy as _np
    import concourse.bacc as _bacc
    from concourse.bass_utils import run_bass_kernel_spmd as _run

    raw = {k: _np.asarray(v) for k, v in inputs.items()}
    edges = EP - N_EDGES
    loop = _np.arange(N_NODES, dtype=raw["src"].dtype)
    rbf = _np.pad(raw["edge_attr_16"], ((0, edges), (0, 0)))
    arrays = {
        "x": _np.pad(raw["x"], ((0, NP - N_NODES), (0, 0))),
        "src": _np.pad(raw["src"], (0, edges)),
        "dst": _np.pad(raw["dst"], (0, edges), constant_values=NP),
        "pairs_by_row": _np.stack([_np.pad(raw["src"], (0, edges), constant_values=NP), _np.pad(raw["dst"], (0, edges))], axis=1),
        "pairs_by_dst": _np.stack([_np.concatenate([raw["dst"], loop, _np.full(EPS - ES, NP, loop.dtype)]),
                                   _np.concatenate([raw["src"], loop, _np.zeros(EPS - ES, loop.dtype)])], axis=1),
        "ea64": _np.pad(raw["edge_attr_64"], ((0, edges), (0, 0))),
        "ea4": _np.pad(raw["edge_attr_4"], ((0, edges), (0, 0))),
        "rbf_t": _np.ascontiguousarray(rbf.reshape(NG, P, J, D_EA16).transpose(0, 3, 2, 1)).reshape(NG * D_EA16, GE),
        "L1_a1": raw["L1_gnn_a1"].reshape(-1), "L1_a2": raw["L1_gnn_a2"].reshape(-1),
        "L2_Wkv": _np.concatenate([raw["L2_gnn_Wk"], raw["L2_gnn_Wv"]], axis=1),
        "L2_bkv": _np.concatenate([raw["L2_gnn_bk"], raw["L2_gnn_bv"]]),
        "L3_Wc": _np.ascontiguousarray(_np.concatenate([raw["L3_gnn_Wc0"], raw["L3_gnn_Wc1"]], axis=1).T).reshape(-1),
    }
    taken = {"L1_gnn_a1", "L1_gnn_a2", "L2_gnn_Wk", "L2_gnn_Wv", "L2_gnn_bk", "L2_gnn_bv", "L3_gnn_Wc0", "L3_gnn_Wc1"}
    arrays.update({k.replace("_gnn", ""): _np.ascontiguousarray(v) for k, v in raw.items() if "_gnn_" in k and k not in taken})
    nc = _bacc.Bacc("TRN2", target_bir_lowering=False, num_devices=1)
    args = {n: nc.dram_tensor(f"in_{n}", v.shape, mybir.dt.from_np(v.dtype), kind="ExternalInput").ap() for n, v in arrays.items()}
    out = nc.dram_tensor("out_0", (NP, D), F32, kind="ExternalOutput").ap()
    build(nc, args, out)
    r = _run(nc, [{f"in_{n}": v for n, v in arrays.items()}], core_ids=[0])
    return r.results[0]["out_0"][:N_NODES]
```

```python
from contextlib import ExitStack

import concourse.bass as bass
from concourse import mybir

ALU = mybir.AluOpType
ACT = mybir.ActivationFunctionType
AX = mybir.AxisListType
F32 = mybir.dt.float32
I32 = mybir.dt.int32

P = 128
N_NODES = 3125
N_EDGES = 53125
D = 256
D_EA64, D_EA16 = 64, 16
WN = -(-N_NODES // P)
CW = 5
CHUNKS = WN // CW
NP = WN * P
WX = WN + 1
J = 4
NB = 4
GE = P * J
NG = -(-N_EDGES // GE)
EP = NG * GE
ES = N_EDGES + N_NODES
NGS = -(-ES // GE)
EPS = NGS * GE
KC = -(-(max(NG, NGS) * WX + NB + 2) // P)
KMAX = KC * P
BIG = 1e30
SLOPE = 0.2
C3 = 64
assert WN % CW == 0 and NG % 2 == 0 and NGS % 2 == 0


class Model:

    def __init__(self, inputs):
        self.inputs = inputs


class Order:

    def __init__(self, dram, name, groups, key, other):
        self.groups, self.edges = groups, groups * GE
        self.key, self.other = key, other
        self.key_around = dram(name + "_key_f", (self.edges + 2,))
        self.key_f = self.key_around[1:self.edges + 1]
        self.gk_d, self.wk_d = dram(name + "_group", (KMAX,), I32), dram(name + "_window", (KMAX,), I32)


class Sorted(Order):

    def __init__(self, dram, name, groups, pairs):
        dr = lambda n, s, d=F32: dram(f"{name}_{n}", s, d)
        edges = groups * GE
        Order.__init__(self, dram, name, groups, dr("key", (edges,), I32), dr("other", (edges,), I32))
        self.unsorted, self.sorted = pairs, dr("sorted", (edges, 2), I32)
        self.cols, self.key_in_f, self.key_in_lo = dr("cols", (edges, 3)), dr("key_in", (edges,)), dr("key_in_lo", (edges,))


class Stages:

    def __init__(self, sem, names):
        self.sem, self.names = sem, list(names)
        self.n = len(self.names)
        self.start = NB * self.n

    def at(self, name, step):
        return (step + NB) * self.n + self.names.index(name) + 1


class Chain:

    def __init__(self, sem, names):
        self.sem, self.names = sem, list(names)

    def at(self, name):
        return self.names.index(name) + 1


def settle(eng):
    eng.nop(nofuse=True)


def column(v):
    return v.rearrange("(p a) -> p a", a=1)


def row_everywhere(v):
    return v.rearrange("(a n) -> a n", a=1).broadcast_to([P, v.shape[-1]])


def build_steps(nc, m, o, tag):
    NG, EP = o.groups, o.edges
    with ExitStack() as ctx:
        sb = lambda n, s, d=F32: ctx.enter_context(nc.sbuf_tensor(tag + n, s, d))
        sem = lambda n: ctx.enter_context(nc.semaphore(tag + n))
        dst_rows = sb("st_dst_rows", [NG, GE], I32)
        dst_i = sb("st_dst_i", [P, EP // P], I32)
        dst_f = sb("st_dst_f", [P, EP // P])
        lim_f = sb("st_lim_f", [NG, 2])
        lim_i = sb("st_lim_i", [NG, 2], I32)
        win_i = sb("st_win_i", [NG, 2], I32)
        win = sb("st_win", [NG, 2])
        count = sb("st_count", [NG, 1])
        count_b = sb("st_count_b", [NG, P])
        wmin_b = sb("st_wmin_b", [NG, P])
        below = sb("st_below", [NG, NG + 1])
        start = sb("st_start", [P, NG + 1])
        delta = sb("st_delta", [P, NG])
        delta_step = sb("st_delta_step", [P, NG])
        k_i = sb("st_k_i", [P, KC], I32)
        k_f = sb("st_k_f", [P, KC])
        le = sb("st_le", [P, KC, NG])
        gk = sb("st_gk", [P, KC])
        wk = sb("st_wk", [P, KC])
        gk_i = sb("st_gk_i", [P, KC], I32)
        wk_i = sb("st_wk_i", [P, KC], I32)
        last_f = sb("st_last_f", [1, 1])
        last_i = sb("st_last_i", [1, 1], I32)
        ps = ctx.enter_context(nc.psum_tensor(tag + "st_ps", [P, 512], F32))
        loaded, stored, listed = sem("st_loaded"), sem("st_stored"), sem("st_listed")
        pool_done, dve_done, pe_done = sem("st_pool"), sem("st_dve"), sem("st_pe")
        block = ctx.enter_context(nc.Block())

        @block.sync
        def _(sp):
            sp.dma_start(dst_rows[:, :], o.key.rearrange("(g e) -> g e", e=GE)).then_inc(loaded, 16)
            sp.dma_start(dst_i[:, :], o.key.rearrange("(p c) -> p c", p=P)).then_inc(loaded, 16)
            sp.wait_ge(dve_done, 1)
            sp.dma_start(o.key_f.rearrange("(p c) -> p c", p=P), dst_f[:, :]).then_inc(stored, 16)
            sp.wait_ge(dve_done, 26)
            sp.dma_start(o.gk_d.rearrange("(p c) -> p c", p=P), gk_i[:, :]).then_inc(stored, 16)
            sp.dma_start(o.wk_d.rearrange("(p c) -> p c", p=P), wk_i[:, :]).then_inc(stored, 16)
            sp.wait_ge(stored, 48)
            sp.dma_start(o.gk[:, :], o.gk_d.rearrange("(a k) -> a k", a=1)).then_inc(listed, 16)
            sp.dma_start(o.wk[:, :], o.wk_d.rearrange("(a k) -> a k", a=1)).then_inc(listed, 16)
            sp.wait_ge(listed, 32)

        @block.gpsimd
        def _(pool):
            nc.gpsimd.iota(m.iota[:, :], [[1, P]], base=0, channel_multiplier=0,
                           allow_small_or_imprecise_dtypes=True).then_inc(pool_done, 1)
            nc.gpsimd.iota(m.node[:, :], [[P, WX]], base=0, channel_multiplier=1,
                           allow_small_or_imprecise_dtypes=True).then_inc(pool_done, 1)
            nc.gpsimd.iota(m.base[:, :], [[P, WX]], base=0, channel_multiplier=0,
                           allow_small_or_imprecise_dtypes=True).then_inc(pool_done, 1)
            nc.gpsimd.iota(m.end[:, :], [[P, WX]], base=P, channel_multiplier=0,
                           allow_small_or_imprecise_dtypes=True).then_inc(pool_done, 1)
            nc.gpsimd.iota(k_i[:, :], [[1, KC]], base=0, channel_multiplier=KC).then_inc(pool_done, 1)

        @block.tensor
        def _(pe):
            pe.wait_ge(dve_done, 12)
            nc.tensor.matmul(ps[:, 0:NG + 1], count_b[:, :], below[:, :], start=True, stop=True)
            nc.tensor.matmul(ps[:, 256:256 + NG], wmin_b[:, :], m.ident[0:NG, 0:NG],
                             start=True, stop=True).then_inc(pe_done, 1)

        @block.vector
        def _(dve):
            n = [0]

            def link(ins):
                n[0] += 1
                ins.then_inc(dve_done, 1)
                dve.wait_ge(dve_done, n[0])

            dve.wait_ge(loaded, 32)
            dve.wait_ge(pool_done, 5)
            link(nc.vector.tensor_copy(dst_f[:, :], dst_i[:, :]))
            link(nc.vector.tensor_scalar(m.ident[:, :], m.iota[:, :], m.node[:, 0:1], None, ALU.is_equal))
            link(nc.vector.tensor_reduce(lim_f[:, 0:1], dst_rows[:, :], AX.X, ALU.min))
            link(nc.vector.tensor_reduce(lim_f[:, 1:2], dst_rows[:, :], AX.X, ALU.max))
            link(nc.vector.tensor_copy(lim_i[:, :], lim_f[:, :]))
            link(nc.vector.tensor_scalar(win_i[:, :], lim_i[:, :], 7, None, ALU.arith_shift_right))
            link(nc.vector.tensor_copy(win[:, :], win_i[:, :]))
            link(nc.vector.scalar_tensor_tensor(count[:, :], win[:, 1:2], 1.0, win[:, 0:1], ALU.add, ALU.subtract))
            link(nc.vector.tensor_copy(count_b[:, :], count[:, 0:1].broadcast_to([NG, P])))
            link(nc.vector.tensor_copy(wmin_b[:, :], win[:, 0:1].broadcast_to([NG, P])))
            link(nc.vector.tensor_scalar(below[:, :], m.iota[0:NG, 0:NG + 1], m.node[0:NG, 0:1], None, ALU.is_gt))
            link(nc.vector.tensor_copy(k_f[:, :], k_i[:, :]))
            dve.wait_ge(pe_done, 1)
            link(nc.vector.tensor_copy(start[:, :], ps[:, 0:NG + 1]))
            link(nc.vector.tensor_tensor(delta[:, :], ps[:, 256:256 + NG], start[:, 0:NG], ALU.subtract))
            link(nc.vector.tensor_tensor(delta_step[:, 1:NG], delta[:, 1:NG], delta[:, 0:NG - 1], ALU.subtract))
            link(nc.vector.tensor_copy(delta_step[:, 0:1], delta[:, 0:1]))
            start_b = start[:, 0:NG].unsqueeze(1).broadcast_to([P, KC, NG])
            k_b = k_f[:, :].unsqueeze(2).broadcast_to([P, KC, NG])
            link(nc.vector.tensor_tensor(le[:, :, :], start_b, k_b, ALU.is_le))
            link(nc.vector.tensor_reduce(gk[:, :], le[:, :, :], AX.X, ALU.add))
            link(nc.vector.tensor_scalar(gk[:, :], gk[:, :], -1.0, None, ALU.add))
            link(nc.vector.tensor_copy(gk_i[:, :], gk[:, :]))
            d_b = delta_step[:, :].unsqueeze(1).broadcast_to([P, KC, NG])
            link(nc.vector.tensor_tensor(le[:, :, :], le[:, :, :], d_b, ALU.mult))
            link(nc.vector.tensor_reduce(wk[:, :], le[:, :, :], AX.X, ALU.add))
            link(nc.vector.tensor_tensor(wk[:, :], wk[:, :], k_f[:, :], ALU.add))
            link(nc.vector.tensor_scalar(wk[:, :], wk[:, :], float(WX - 1), None, ALU.min))
            link(nc.vector.tensor_copy(wk_i[:, :], wk[:, :]))
            link(nc.vector.tensor_scalar(last_f[:, :], start[0:1, NG:NG + 1], NB - 1.0, None, ALU.add))
            link(nc.vector.tensor_copy(last_i[:, :], last_f[:, :]))
            link(nc.vector.tensor_scalar(o.rounds[:, :], last_i[:, :], NB.bit_length() - 1, None, ALU.arith_shift_right))


def rounds_of(eng, o):
    return eng.value_load(o.rounds[0:1, 0:1], min_val=1, max_val=KMAX // NB - 1)


def drive(eng, o, front, back=None):
    rounds = rounds_of(eng, o)
    if front:
        front(0, 0, 0)
    with eng.Fori(0, rounds) as i:
        for b in range(NB):
            if front:
                front(NB * i + b + 1, i + (b + 1) // NB, (b + 1) % NB)
            if back:
                back(NB * i + b, i, b)


def drive_two_ahead(eng, o, front, middle=None, back=None):
    call = lambda f, k, i, b: f(k, i, b) if f else None
    rounds = rounds_of(eng, o)
    call(front, 0, 0, 0)
    call(front, 1, 0, 1)
    with eng.Fori(0, rounds) as i:
        for b in range(NB):
            call(middle, NB * i + b, i, b)
            call(front, NB * i + b + 2, i + (b + 2) // NB, (b + 2) % NB)
            call(back, NB * i + b, i, b)


def drive_late(eng, o, front, middle, back):
    rounds = rounds_of(eng, o)
    front(0, 0, 0)
    with eng.Fori(0, rounds) as i:
        for b in range(NB):
            front(NB * i + b + 1, i + (b + 1) // NB, (b + 1) % NB)
            middle(NB * i + b, i, b)
            if b:
                back(NB * i + b - 1, i, b - 1)
        back(NB * i + NB - 1, i, NB - 1)


def window_of(eng, o, k):
    return eng.value_load(o.wk[0:1, bass.ds(k, 1)], min_val=0, max_val=WX - 1)


def group_of(eng, o, k):
    return eng.value_load(o.gk[0:1, bass.ds(k, 1)], min_val=0, max_val=o.groups - 1)


def over_groups(eng, n, front=None, middle=None, back=None):
    call = lambda f, k, i, b: f(k, i, b) if f else None
    call(front, 0, 0, 0)
    with eng.Fori(0, n // 2 - 1) as i:
        for b in range(2):
            call(middle, 2 * i + b, i, b)
            call(front, 2 * i + b + 1, i + b, 1 - b)
            call(back, 2 * i + b, i, b)
    call(middle, n - 2, n // 2 - 1, 0)
    call(front, n - 1, n // 2 - 1, 1)
    call(back, n - 2, n // 2 - 1, 0)
    call(middle, n - 1, n // 2 - 1, 1)
    call(back, n - 1, n // 2 - 1, 1)


def edge_sums(nc, m, o, tag, table, W, total, attr=None, prob=None, H=1):
    with ExitStack() as ctx:
        sb = lambda n, s, d=F32: [ctx.enter_context(nc.sbuf_tensor(f"{tag}_{n}{b}", s, d)) for b in range(NB)]
        sem = lambda n: ctx.enter_context(nc.semaphore(f"{tag}_{n}"))
        A = attr.shape[-1] if attr is not None else 0
        idx, key_c = sb("idx", [P, J], I32), sb("key_c", [P, J])
        attrs = sb("attr", [P, J, A]) if A else None
        probs = sb("prob", [P, J, H]) if prob is not None else None
        rel, hot, rows = sb("rel", [P, J]), sb("hot", [P, J, P]), sb("rows", [P, J, table.shape[-1]])
        sums = [ctx.enter_context(nc.psum_tensor(f"{tag}_sums{b}", [P, 512], F32)) for b in range(2)] * 2
        loaded = [sem(f"loaded{b}") for b in range(NB)]
        gathered = [m.dma_sem(f"{tag}_gathered{b}") for b in range(NB)]
        hots = Stages(sem("hots"), ["rel", "hot"])
        weighed = Stages(sem("weighed"), [f"tile{j}" for j in range(J)])
        pe_s = Stages(sem("pe"), ["sum"])
        merges = Stages(sem("merges"), ["merged"])
        zeroed = sem("zeroed")
        loads = 2 + (attr is not None) + (prob is not None)
        block = ctx.enter_context(nc.Block())

        @block.sync
        def _(sp):
            def front(k, i, b):
                g = group_of(sp, o, k)
                part = bass.ds(g * GE, GE)
                if prob is None:
                    sp.wait_ge(pe_s.sem, pe_s.at("sum", k - NB))
                else:
                    sp.wait_ge(weighed.sem, weighed.at(f"tile{J - 1}", k - NB))
                sp.dma_start(idx[b][:, :], o.other[part].rearrange("(p j) -> p j", j=J)).then_inc(loaded[b], 16)
                sp.dma_start(key_c[b][:, :], o.key_f[part].rearrange("(p j) -> p j", j=J)).then_inc(loaded[b], 16)
                if A:
                    sp.dma_start(attrs[b][:, :, :], attr[part, :].rearrange("(p j) c -> p j c", j=J)).then_inc(loaded[b], 16)
                if prob is not None:
                    sp.dma_start(probs[b][:, :, :], prob[part, :].rearrange("(p j) h -> p j h", j=J)).then_inc(loaded[b], 16)
            drive(sp, o, front)

        @block.gpsimd
        def _(pool):
            nc.gpsimd.memset(total[:, :, :], 0.0).then_inc(zeroed, 1)

            def front(k, i, b):
                pool.wait_ge(loaded[b], 16 * loads * (i + 1))
                pool.wait_ge(pe_s.sem, pe_s.at("sum", k - NB))
                settle(pool)
                for j in range(J):
                    pool.indirect_dma_start(
                        out=rows[b][:, j, :], out_offset=None, in_=table,
                        in_offset=bass.IndirectOffsetOnAxis(ap=idx[b][:, j:j + 1], axis=0)).then_inc(gathered[b], 16)
            drive(pool, o, front)

        @block.tensor
        def _(pe):
            pe.sem_inc(pe_s.sem, pe_s.start)

            def back(k, i, b):
                pe.wait_ge(hots.sem, hots.at("hot", k))
                pe.wait_ge(merges.sem, merges.at("merged", k - 2))
                if prob is None:
                    pe.wait_ge(gathered[b], 16 * J * (i + 1))
                for j in range(J):
                    if prob is not None:
                        pe.wait_ge(weighed.sem, weighed.at(f"tile{j}", k))
                    mm = nc.tensor.matmul(sums[b][:, 0:W], hot[b][:, j, :], rows[b][:, j, 0:W], start=(j == 0), stop=(j == J - 1))
                if A:
                    pe.wait_ge(loaded[b], 16 * loads * (i + 1))
                    for j in range(J):
                        mm = nc.tensor.matmul(sums[b][:, W:W + A], hot[b][:, j, :], attrs[b][:, j, :], start=(j == 0), stop=(j == J - 1))
                mm.then_inc(pe_s.sem, 1)
            drive(pe, o, None, back)

        @block.vector
        def _(dve):
            for s in (hots, weighed, merges):
                dve.sem_inc(s.sem, s.start)
            dve.wait_ge(zeroed, 1)

            def front(k, i, b):
                w = window_of(dve, o, k)
                dve.wait_ge(loaded[b], 16 * loads * (i + 1))
                nc.vector.tensor_scalar(rel[b][:, :], key_c[b][:, :], m.base[:, bass.ds(w, 1)], None, ALU.subtract).then_inc(hots.sem, 1)
                dve.wait_ge(hots.sem, hots.at("rel", k))
                dve.wait_ge(pe_s.sem, pe_s.at("sum", k - NB))
                for j in range(J):
                    ins = nc.vector.tensor_scalar(hot[b][:, j, :], m.iota[:, :], rel[b][:, j:j + 1], None, ALU.is_equal)
                ins.then_inc(hots.sem, 1)
                if prob is not None:
                    dve.wait_ge(gathered[b], 16 * J * (i + 1))
                    for j in range(J):
                        if H == 1:
                            ins = nc.vector.tensor_scalar(rows[b][:, j, 0:W], rows[b][:, j, 0:W], probs[b][:, j, 0:1], None, ALU.mult)
                        else:
                            heads = rows[b][:, j, 0:W].rearrange("p (h c) -> p h c", h=H)
                            ins = nc.vector.tensor_tensor(heads, heads, probs[b][:, j, :].unsqueeze(2).broadcast_to([P, H, W // H]), ALU.mult)
                        ins.then_inc(weighed.sem, 1)

            def back(k, i, b):
                w = window_of(dve, o, k)
                dve.wait_ge(pe_s.sem, pe_s.at("sum", k))
                dve.wait_ge(merges.sem, merges.at("merged", k - 1))
                a = total[:, bass.ds(w, 1), :].rearrange("p a c -> p (a c)")
                nc.vector.tensor_tensor(a, a, sums[b][:, 0:W + A], ALU.add).then_inc(merges.sem, 1)
            drive(dve, o, front, back)


def sort_edges(nc, m, o, tag):
    NG, EP = o.groups, o.edges
    with ExitStack() as ctx:
        one = lambda n, s, d=F32: ctx.enter_context(nc.sbuf_tensor(f"{tag}_{n}", s, d))
        two = lambda n, s, d=F32: [one(f"{n}{b}", s, d) for b in range(2)]
        bank = lambda n: ctx.enter_context(nc.psum_tensor(f"{tag}_{n}", [P, 512], F32))
        sem = lambda n: ctx.enter_context(nc.semaphore(f"{tag}_{n}"))
        run = two("run", [P, J, WX])
        lower = one("lower", [P, P])

        C = EP // P
        CB = max(n for n in range(1, 24) if C % (2 * n) == 0)
        with ExitStack() as first:
            tmp = lambda n, s, d=F32: first.enter_context(nc.sbuf_tensor(f"{tag}_{n}", s, d))
            pair_all = tmp("pair_all", [P, C, 2], I32)
            lo_i, hi_i = tmp("lo_i", [P, C], I32), tmp("hi_i", [P, C], I32)
            row_i = tmp("row_i", [P, C], I32)
            cols = tmp("cols", [P, C, 3])
            flat = [tmp(f"flat{i}", [P, C]) for i in range(2)]
            hot, high = [[tmp(f"{n}{b}", [P, CB, w]) for b in range(2)] for n, w in (("hot_all", P), ("high_all", WX))]
            zero, ones = tmp("zero", [P, P]), tmp("ones", [P, P])
            below = tmp("below", [P, P])
            per_window, before_window = tmp("per_window", [P, WX]), tmp("before_window", [P, WX])
            counts = tmp("counts", [P, WX])
            count_ps, pre_ps = bank("count"), bank("pre")
            loaded, stored, made, counted, dve_done, pe_done = (sem(n) for n in ("a_loaded", "a_stored", "a_made", "a_counted", "a_dve", "a_pe"))
            block = first.enter_context(nc.Block())

            @block.sync
            def _(sp):
                sp.dma_start(pair_all[:, :, :], o.unsorted.rearrange("(p c) t -> p c t", p=P)).then_inc(loaded, 16)
                sp.wait_ge(dve_done, 8)
                sp.dma_start(o.cols.rearrange("(p c) t -> p c t", p=P), cols[:, :, :]).then_inc(stored, 16)
                sp.dma_start(o.key_in_f.rearrange("(p c) -> p c", p=P), flat[0][:, :]).then_inc(stored, 16)
                sp.dma_start(o.key_in_lo.rearrange("(p c) -> p c", p=P), flat[1][:, :]).then_inc(stored, 16)
                sp.wait_ge(stored, 48)

            @block.gpsimd
            def _(pool):
                nc.gpsimd.memset(zero[:, :], 0.0).then_inc(loaded, 1)
                nc.gpsimd.memset(ones[:, :], 1.0).then_inc(loaded, 1)

            @block.tensor
            def _(pe):
                pe.wait_ge(loaded, 18)
                nc.tensor.matmul(count_ps[:, 0:WX], zero[:, :], zero[:, 0:WX], start=True, stop=True)
                with pe.Fori(0, C // CB // 2) as i:
                    for b in range(2):
                        pe.wait_ge(made, 2 * i + b + 1)
                        for t in range(CB):
                            mm = nc.tensor.matmul(count_ps[:, 0:WX], hot[b][:, t, :], high[b][:, t, :], start=False, stop=True, skip_group_check=True)
                        mm.then_inc(counted, 1)
                pe.wait_ge(dve_done, 11)
                nc.tensor.matmul(pre_ps[:, 0:WX], below[:, :], counts[:, :], start=True, stop=True)
                nc.tensor.matmul(pre_ps[:, 64:64 + WX], ones[:, :], counts[:, :], start=True, stop=True).then_inc(pe_done, 1)

            @block.vector
            def _(dve):
                n = [0]

                def link(ins):
                    n[0] += 1
                    ins.then_inc(dve_done, 1)
                    dve.wait_ge(dve_done, n[0])

                dve.wait_ge(loaded, 18)
                link(nc.vector.tensor_copy(row_i[:, :], pair_all[:, :, 0:1].rearrange("p c a -> p (c a)")))
                link(nc.vector.tensor_scalar(lo_i[:, :], row_i[:, :], P - 1, None, ALU.bitwise_and))
                link(nc.vector.tensor_scalar(hi_i[:, :], row_i[:, :], 7, None, ALU.arith_shift_right))
                link(nc.vector.tensor_copy(cols[:, :, 0:1].rearrange("p c a -> p (c a)"), row_i[:, :]))
                link(nc.vector.tensor_copy(cols[:, :, 1:2].rearrange("p c a -> p (c a)"), lo_i[:, :]))
                link(nc.vector.tensor_copy(cols[:, :, 2:3].rearrange("p c a -> p (c a)"), hi_i[:, :]))
                link(nc.vector.tensor_copy(flat[0][:, :], row_i[:, :]))
                link(nc.vector.tensor_copy(flat[1][:, :], lo_i[:, :]))
                dve.sem_inc(counted, 2)
                with dve.Fori(0, C // CB // 2) as i:
                    for b in range(2):
                        dve.wait_ge(counted, 2 * i + b + 1)
                        part = bass.ds((2 * i + b) * CB, CB)
                        lo, hi = cols[:, part, 1:2].broadcast_to([P, CB, P]), cols[:, part, 2:3].broadcast_to([P, CB, WX])
                        nc.vector.tensor_tensor(hot[b][:, :, :], m.iota[:, :].unsqueeze(1).broadcast_to([P, CB, P]), lo, ALU.is_equal)
                        nc.vector.tensor_tensor(high[b][:, :, :], m.iota[:, 0:WX].unsqueeze(1).broadcast_to([P, CB, WX]), hi, ALU.is_equal).then_inc(made, 1)
                dve.wait_ge(counted, C // CB + 2)
                link(nc.vector.tensor_copy(counts[:, :], count_ps[:, 0:WX]))
                link(nc.vector.tensor_scalar(below[:, :], m.iota[:, :], m.node[:, 0:1], None, ALU.is_gt))
                link(nc.vector.tensor_scalar(lower[:, :], m.iota[:, :], m.node[:, 0:1], None, ALU.is_lt))
                dve.wait_ge(pe_done, 1)
                link(nc.vector.tensor_copy(per_window[:, :], pre_ps[:, 64:64 + WX]))
                link(nc.vector.tensor_tensor_scan(before_window[:, :], ones[:, 0:WX], per_window[:, :], 0.0, ALU.mult, ALU.add))
                link(nc.vector.tensor_tensor(before_window[:, :], before_window[:, :], per_window[:, :], ALU.subtract))
                link(nc.vector.tensor_tensor(run[0][:, 0, :], pre_ps[:, 0:WX], before_window[:, :], ALU.add))

        with ExitStack() as second:
            tmp = lambda n, s, d=F32: second.enter_context(nc.sbuf_tensor(f"{tag}_{n}", s, d))
            two = lambda n, s, d=F32: [tmp(f"{n}{b}", s, d) for b in range(2)]
            pair, col = two("pair", [P, J, 2], I32), two("col", [P, J, 3])
            row_r, lo_r = two("row_r", [P, GE]), two("lo_r", [P, GE])
            hot, hot_t, high = two("hot", [P, J, P]), two("hot_t", [P, J, P]), two("high", [P, J, WX])
            tied = tmp("tied", [P, J, P])
            tie, place = two("tie", [P, J]), tmp("place", [P, J])
            at_sel = tmp("at_sel", [P, J, WX])
            place_i = two("place_i", [P, J], I32)
            hist, at = [second.enter_context(nc.psum_tensor(f"{tag}_hist{b}", [P, 512], F32)) for b in range(2)], \
                [second.enter_context(nc.psum_tensor(f"{tag}_at{b}", [P, 512], F32)) for b in range(2)]
            loaded = [sem(f"b_loaded{b}") for b in range(2)]
            pair_loaded = [sem(f"b_pair_loaded{b}") for b in range(2)]
            scattered = [m.dma_sem(f"{tag}_b_scattered{b}") for b in range(2)]
            front_s = Stages(sem("b_front"), ["hot_t", "hots", "tie"])
            back_s = Stages(sem("b_back"), [f"run{j}" for j in range(1, J + 1)] + ["picked", "place", "placed"])
            hist_s, at_s = Stages(sem("b_hist"), ["hist"]), Stages(sem("b_at"), ["at"])
            pool_s = Stages(sem("b_pool"), ["scattered"])
            block = second.enter_context(nc.Block())

            @block.sync
            def _(sp):
                def front(k, i, b):
                    part = bass.ds(k * GE, GE)
                    sp.wait_ge(front_s.sem, front_s.at("tie", k - 2))
                    sp.dma_start(col[b][:, :, :], o.cols[part, :].rearrange("(p j) t -> p j t", j=J)).then_inc(loaded[b], 16)
                    sp.dma_start(row_r[b][:, :], row_everywhere(o.key_in_f[part])).then_inc(loaded[b], 16)
                    sp.dma_start(lo_r[b][:, :], row_everywhere(o.key_in_lo[part])).then_inc(loaded[b], 16)
                over_groups(sp, NG, front)

            @block.scalar
            def _(act):
                def front(k, i, b):
                    act.wait_ge(pool_s.sem, pool_s.at("scattered", k - 2))
                    nc.scalar.dma_start(pair[b][:, :, :], o.unsorted[bass.ds(k * GE, GE), :].rearrange("(p j) t -> p j t", j=J)).then_inc(pair_loaded[b], 16)
                over_groups(act, NG, front)

            @block.gpsimd
            def _(pool):
                pool.sem_inc(pool_s.sem, pool_s.start)

                def front(k, i, b):
                    pool.wait_ge(pair_loaded[b], 16 * (i + 1))
                    pool.wait_ge(back_s.sem, back_s.at("placed", k))
                    settle(pool)
                    for j in range(J):
                        pool.indirect_dma_start(
                            out=o.sorted, out_offset=bass.IndirectOffsetOnAxis(ap=place_i[b][:, j:j + 1], axis=0),
                            in_=pair[b][:, j, :], in_offset=None).then_inc(scattered[b], 16)

                def back(k, i, b):
                    pool.wait_ge(scattered[b], 16 * J * (i + 1))
                    pool.sem_inc(pool_s.sem, 1)
                over_groups(pool, NG, front, back=back)

            @block.tensor
            def _(pe):
                pe.sem_inc(hist_s.sem, hist_s.start)
                pe.sem_inc(at_s.sem, at_s.start)

                def front(k, i, b):
                    pe.wait_ge(front_s.sem, front_s.at("hots", k))
                    pe.wait_ge(back_s.sem, back_s.at(f"run{J}", k - 2))
                    for j in range(J):
                        mm = nc.tensor.matmul(hist[b][:, j * WX:(j + 1) * WX], hot[b][:, j, :], high[b][:, j, :], start=True, stop=True)
                    mm.then_inc(hist_s.sem, 1)

                def back(k, i, b):
                    pe.wait_ge(back_s.sem, back_s.at("picked", k - 2))
                    pe.wait_ge(back_s.sem, back_s.at(f"run{J}", k))
                    for j in range(J):
                        mm = nc.tensor.matmul(at[b][:, j * WX:(j + 1) * WX], hot_t[b][:, j, :], run[b][:, j, :], start=True, stop=True)
                    mm.then_inc(at_s.sem, 1)
                over_groups(pe, NG, front=front, middle=back)

            @block.vector
            def _(dve):
                dve.sem_inc(front_s.sem, front_s.start)
                dve.sem_inc(back_s.sem, back_s.start)

                def front(k, i, b):
                    dve.wait_ge(loaded[b], 48 * (i + 1))
                    dve.wait_ge(at_s.sem, at_s.at("at", k - 2))
                    nc.vector.tensor_scalar(hot_t[b][:, :, :], lo_r[b][:, :].rearrange("p (e j) -> p j e", j=J),
                                            m.node[:, 0:1], None, ALU.is_equal).then_inc(front_s.sem, 1)
                    nc.vector.tensor_tensor(hot[b][:, :, :], m.iota[:, :].unsqueeze(1).broadcast_to([P, J, P]),
                                            col[b][:, :, 1:2].broadcast_to([P, J, P]), ALU.is_equal)
                    nc.vector.tensor_tensor(high[b][:, :, :], m.iota[:, 0:WX].unsqueeze(1).broadcast_to([P, J, WX]),
                                            col[b][:, :, 2:3].broadcast_to([P, J, WX]), ALU.is_equal).then_inc(front_s.sem, 1)
                    for j in range(J):
                        ins = nc.vector.scalar_tensor_tensor(tied[:, j, :], row_r[b][:, :].rearrange("p (e j) -> p j e", j=J)[:, j, :],
                                                             col[b][:, j, 0:1], lower[:, :], ALU.is_equal, ALU.mult, accum_out=tie[b][:, j:j + 1])
                    ins.then_inc(front_s.sem, 1)

                def middle(k, i, b):
                    dve.wait_ge(hist_s.sem, hist_s.at("hist", k))
                    dve.wait_ge(back_s.sem, back_s.at(f"run{J}", k - 1))
                    for j in range(J):
                        to = run[b][:, j + 1, :] if j < J - 1 else run[1 - b][:, 0, :]
                        if j == J - 1:
                            dve.wait_ge(at_s.sem, at_s.at("at", k - 1))
                        nc.vector.tensor_tensor(to, run[b][:, j, :], hist[b][:, j * WX:(j + 1) * WX], ALU.add).then_inc(back_s.sem, 1)
                        dve.wait_ge(back_s.sem, back_s.at(f"run{j + 1}", k))

                def back(k, i, b):
                    def link(name, ins):
                        ins.then_inc(back_s.sem, 1)
                        dve.wait_ge(back_s.sem, back_s.at(name, k))

                    dve.wait_ge(front_s.sem, front_s.at("tie", k))
                    dve.wait_ge(at_s.sem, at_s.at("at", k))
                    link("picked", nc.vector.tensor_tensor(at_sel[:, :, :], at[b][:, 0:J * WX].rearrange("p (j w) -> p j w", j=J), high[b][:, :, :], ALU.mult))
                    link("place", nc.vector.tensor_reduce(place[:, :], at_sel[:, :, :], AX.X, ALU.add))
                    dve.wait_ge(pool_s.sem, pool_s.at("scattered", k - 2))
                    link("placed", nc.vector.tensor_tensor(place_i[b][:, :], place[:, :], tie[b][:, :], ALU.add))
                over_groups(dve, NG, front, middle, back)

        with ExitStack() as third:
            tmp = lambda n, s, d=F32: third.enter_context(nc.sbuf_tensor(f"{tag}_{n}", s, d))
            pair_all, row, col = tmp("pairs", [P, C, 2], I32), tmp("row", [P, C], I32), tmp("col_s", [P, C], I32)
            loaded, split, stored = sem("c_loaded"), sem("c_split"), sem("c_stored")
            ends = tmp("ends", [1, 2])
            block = third.enter_context(nc.Block())

            @block.sync
            def _(sp):
                sp.dma_start(pair_all[:, :, :], o.sorted.rearrange("(p c) t -> p c t", p=P)).then_inc(loaded, 16)
                sp.wait_ge(split, 3)
                sp.dma_start(o.key.rearrange("(p c) -> p c", p=P), row[:, :]).then_inc(stored, 16)
                sp.dma_start(o.other.rearrange("(p c) -> p c", p=P), col[:, :]).then_inc(stored, 16)
                sp.dma_start(o.key_around[0:1].rearrange("(a c) -> a c", a=1), ends[:, 0:1]).then_inc(stored, 16)
                sp.dma_start(o.key_around[EP + 1:EP + 2].rearrange("(a c) -> a c", a=1), ends[:, 1:2]).then_inc(stored, 16)
                sp.wait_ge(stored, 64)

            @block.vector
            def _(dve):
                nc.vector.memset(ends[:, :], -1.0).then_inc(split, 1)
                dve.wait_ge(loaded, 16)
                nc.vector.tensor_copy(row[:, :], pair_all[:, :, 0:1].rearrange("p c a -> p (c a)")).then_inc(split, 1)
                nc.vector.tensor_copy(col[:, :], pair_all[:, :, 1:2].rearrange("p c a -> p (c a)")).then_inc(split, 1)


def edge_scores(nc, m, o, tag, H, C, source, target, scores, att=None):
    W, JH = H * C, J * H
    TW = W + H if att is not None else W
    with ExitStack() as ctx:
        two = lambda n, s, d=F32: [ctx.enter_context(nc.sbuf_tensor(f"{tag}_{n}{b}", s, d)) for b in range(2)]
        sem = lambda n: ctx.enter_context(nc.semaphore(f"{tag}_{n}"))
        idx = two("idx", [P, J, 2], I32)
        near, far = two("near", [P, J, TW]), two("far", [P, J, TW])
        part = two("part", [P, JH])
        loaded = [sem(f"loaded{b}") for b in range(2)]
        gathered = [m.dma_sem(f"{tag}_gathered{b}") for b in range(2)]
        sums = Stages(sem("sums"), [f"sum{j}" for j in range(J)])
        relus = Stages(sem("relus"), [f"relu{j}" for j in range(J)])
        done = Stages(sem("done"), ["part", "score"])
        block = ctx.enter_context(nc.Block())

        @block.sync
        def _(sp):
            pairs = o.sorted.rearrange("(p c) t -> p c t", p=P)

            def front(k, i, b):
                sp.wait_ge(sums.sem, sums.at("sum0", k - 2))
                sp.dma_start(idx[b][:, :, :], pairs[:, bass.ds(k * J, J), :]).then_inc(loaded[b], 16)
            over_groups(sp, o.groups, front)

        @block.gpsimd
        def _(pool):
            def front(k, i, b):
                pool.wait_ge(loaded[b], 16 * (i + 1))
                pool.wait_ge(done.sem, done.at("score", k - 2))
                settle(pool)
                for j in range(J):
                    for t, (to, table) in enumerate(((near, target), (far, source))):
                        pool.indirect_dma_start(
                            out=to[b][:, j, :], out_offset=None, in_=table,
                            in_offset=bass.IndirectOffsetOnAxis(ap=idx[b][:, j, t:t + 1], axis=0)).then_inc(gathered[b], 16)
            over_groups(pool, o.groups, front)

        @block.scalar
        def _(act):
            def back(k, i, b):
                for j in range(J):
                    act.wait_ge(sums.sem, sums.at(f"sum{j}", k))
                    nc.scalar.activation(near[b][:, j, 0:W], near[b][:, j, 0:W], ACT.Relu).then_inc(relus.sem, 1)
            if att is not None:
                act.sem_inc(relus.sem, relus.start)
                over_groups(act, o.groups, back=back)

        @block.vector
        def _(dve):
            for s in (sums, done):
                dve.sem_inc(s.sem, s.start)

            def back(k, i, b):
                dve.wait_ge(gathered[b], 16 * 2 * J * (i + 1))
                for j in range(J):
                    nc.vector.tensor_tensor(near[b][:, j, :], near[b][:, j, :], far[b][:, j, :],
                                            ALU.add if att is not None else ALU.mult).then_inc(sums.sem, 1)
                if att is None:
                    dve.wait_ge(sums.sem, sums.at(f"sum{J - 1}", k))
                    nc.vector.tensor_reduce(part[b][:, :], near[b][:, :, :].rearrange("p j (h c) -> p (j h) c", h=H), AX.X, ALU.add).then_inc(done.sem, 1)
                    dve.wait_ge(done.sem, done.at("part", k))
                    settle(dve)
                    nc.vector.tensor_copy(scores[:, bass.ds(k * J, J), :].rearrange("p j h -> p (j h)"), part[b][:, :]).then_inc(done.sem, 1)
                else:
                    for j in range(J):
                        dve.wait_ge(relus.sem, relus.at(f"relu{j}", k))
                        settle(dve)
                        for h in range(H):
                            span = near[b][:, j, h * C:(h + 1) * C]
                            r = j * H + h
                            ins = nc.vector.tensor_tensor_reduce(span, span, att[:, h * C:(h + 1) * C], 1.0 - SLOPE, 0.0,
                                                                 ALU.mult, ALU.add, part[b][:, r:r + 1])
                    ins.then_inc(done.sem, 1)
                    dve.wait_ge(done.sem, done.at("part", k))
                    nc.vector.tensor_tensor(scores[:, bass.ds(k * J, J), :], part[b][:, :].rearrange("p (j h) -> p j h", j=J),
                                            near[b][:, :, W:W + H], ALU.add).then_inc(done.sem, 1)
            over_groups(dve, o.groups, back=back)


def edge_scores_by_window(nc, m, o, tag, H, C, source, own, scores_d, att=None):
    W, JH = H * C, J * H
    G = o.groups
    with ExitStack() as ctx:
        one = lambda n, s, d=F32: ctx.enter_context(nc.sbuf_tensor(f"{tag}_{n}", s, d))
        sem = lambda n: ctx.enter_context(nc.semaphore(f"{tag}_{n}"))
        some = lambda c, n, s, d=F32: [one(f"{n}{b}", s, d) for b in range(c)]
        idx, key_c, key_r = some(NB, "idx", [P, J], I32), some(NB, "key_c", [P, J]), some(NB, "key_r", [P, GE])
        rows = some(NB, "rows", [P, J, source.shape[-1]])
        hot_t = some(NB, "hot_t", [P, J, P])
        not_below, inside = some(NB, "not_below", [P, J]), some(NB, "inside", [P, J])
        mixed, part, lin = one("mixed", [P, J, W]), one("part", [P, JH]), one("lin", [P, JH])
        scores = one("scores", [P, G * J, H])
        at_edge = [ctx.enter_context(nc.psum_tensor(f"{tag}_at_edge{b}", [P, J, 512], F32)) for b in range(2)]
        loaded = [sem(f"loaded{b}") for b in range(NB)]
        gathered = [m.dma_sem(f"{tag}_gathered{b}") for b in range(NB)]
        zeroed, stored = sem("zeroed"), sem("stored")
        hots = Stages(sem("hots"), ["hot_t"] + (["not_below", "inside"] if att is not None else []))
        owns = Stages(sem("owns"), [f"own{j}" for j in range(J)])
        relus = Stages(sem("relus"), ["relu0", "relu1"])
        done = Stages(sem("done"), ["sum0", "sum1"] + (["lin"] if att is not None else []) + ["part"]
                      + (["masked"] if att is not None else []) + ["score"])
        block = ctx.enter_context(nc.Block())

        @block.sync
        def _(sp):
            def front(k, i, b):
                g = group_of(sp, o, k)
                part = bass.ds(g * GE, GE)
                sp.wait_ge(done.sem, done.at("score", k - NB))
                sp.dma_start(idx[b][:, :], o.other[part].rearrange("(p j) -> p j", j=J)).then_inc(loaded[b], 16)
                sp.dma_start(key_c[b][:, :], o.key_f[part].rearrange("(p j) -> p j", j=J)).then_inc(loaded[b], 16)
                sp.dma_start(key_r[b][:, :], row_everywhere(o.key_f[part])).then_inc(loaded[b], 16)
            drive_two_ahead(sp, o, front)
            sp.wait_ge(stored, 1)
            sp.dma_start(scores_d.rearrange("(g p j) h -> p g (j h)", p=P, j=J), scores[:, :, :].rearrange("p (g j) h -> p g (j h)", j=J)).then_inc(stored, 16)
            sp.wait_ge(stored, 17)

        @block.gpsimd
        def _(pool):
            nc.gpsimd.memset(scores[:, :, :], 0.0).then_inc(zeroed, 1)
            nc.gpsimd.memset(own[:, WX - 1, :], 0.0).then_inc(zeroed, 1)

            def front(k, i, b):
                pool.wait_ge(loaded[b], 48 * (i + 1))
                settle(pool)
                for j in range(J):
                    pool.indirect_dma_start(
                        out=rows[b][:, j, :], out_offset=None, in_=source,
                        in_offset=bass.IndirectOffsetOnAxis(ap=idx[b][:, j:j + 1], axis=0)).then_inc(gathered[b], 16)
            drive_two_ahead(pool, o, front)

        @block.tensor
        def _(pe):
            pe.sem_inc(owns.sem, owns.start)
            pe.wait_ge(zeroed, 2)

            def front(k, i, b):
                w = window_of(pe, o, k)
                pe.wait_ge(hots.sem, hots.at("hot_t", k))
                for j in range(J):
                    pe.wait_ge(done.sem, done.at("lin" if att is not None else "sum1", k - 2))
                    nc.tensor.matmul(at_edge[b % 2][:, j, 0:own.shape[-1]], hot_t[b][:, j, :], own[:, bass.ds(w, 1), :].rearrange("p a c -> p (a c)"),
                                     start=True, stop=True).then_inc(owns.sem, 1)
            drive_two_ahead(pe, o, front)

        @block.scalar
        def _(act):
            def back(k, i, b):
                for half in range(2):
                    act.wait_ge(done.sem, done.at(f"sum{half}", k))
                    tiles = mixed[:, half * J // 2:(half + 1) * J // 2, :]
                    nc.scalar.activation(tiles, tiles, ACT.Relu).then_inc(relus.sem, 1)
            if att is not None:
                act.sem_inc(relus.sem, relus.start)
                drive_two_ahead(act, o, None, back=back)

        @block.vector
        def _(dve):
            for s in (hots, done):
                dve.sem_inc(s.sem, s.start)
            dve.wait_ge(zeroed, 2)

            def front(k, i, b):
                w = window_of(dve, o, k)
                dve.wait_ge(loaded[b], 48 * (i + 1))
                dve.wait_ge(owns.sem, owns.at(f"own{J - 1}", k - NB))
                nc.vector.tensor_scalar(hot_t[b][:, :, :], key_r[b][:, :].rearrange("p (e j) -> p j e", j=J),
                                        m.node[:, bass.ds(w, 1)], None, ALU.is_equal).then_inc(hots.sem, 1)
                if att is not None:
                    dve.wait_ge(done.sem, done.at("masked", k - NB))
                    nc.vector.tensor_scalar(not_below[b][:, :], key_c[b][:, :], m.base[:, bass.ds(w, 1)], None, ALU.is_ge).then_inc(hots.sem, 1)
                    dve.wait_ge(hots.sem, hots.at("not_below", k))
                    nc.vector.scalar_tensor_tensor(inside[b][:, :], key_c[b][:, :], m.end[:, bass.ds(w, 1)], not_below[b][:, :],
                                                   ALU.is_lt, ALU.mult).then_inc(hots.sem, 1)

            def middle(k, i, b):
                dve.wait_ge(gathered[b], 16 * J * (i + 1))
                dve.wait_ge(done.sem, done.at("part", k - 1))
                for half in range(2):
                    tiles = slice(half * J // 2, (half + 1) * J // 2)
                    dve.wait_ge(owns.sem, owns.at(f"own{(half + 1) * J // 2 - 1}", k))
                    nc.vector.tensor_tensor(mixed[:, tiles, :], rows[b][:, tiles, 0:W], at_edge[b % 2][:, tiles, 0:W],
                                            ALU.add if att is not None else ALU.mult).then_inc(done.sem, 1)
                if att is not None:
                    nc.vector.tensor_tensor(lin[:, :].rearrange("p (j h) -> p j h", j=J), rows[b][:, :, W:W + H],
                                            at_edge[b % 2][:, :, W:W + H], ALU.add).then_inc(done.sem, 1)

            def back(k, i, b):
                def link(name, ins):
                    ins.then_inc(done.sem, 1)
                    dve.wait_ge(done.sem, done.at(name, k))

                g = group_of(dve, o, k)
                if att is None:
                    dve.wait_ge(done.sem, done.at("sum1", k))
                    link("part", nc.vector.tensor_reduce(part[:, :], mixed[:, :, :].rearrange("p j (h c) -> p (j h) c", h=H), AX.X, ALU.add))
                else:
                    dve.wait_ge(done.sem, done.at("lin", k))
                    for j in range(J):
                        if j % (J // 2) == 0:
                            dve.wait_ge(relus.sem, relus.at(f"relu{j // (J // 2)}", k))
                            settle(dve)
                        for h in range(H):
                            span = mixed[:, j, h * C:(h + 1) * C]
                            r = j * H + h
                            ins = nc.vector.tensor_tensor_reduce(span, span, att[:, h * C:(h + 1) * C], 1.0 - SLOPE, lin[:, r:r + 1],
                                                                 ALU.mult, ALU.add, part[:, r:r + 1])
                    link("part", ins)
                    part_h = part[:, :].rearrange("p (j h) -> p j h", j=J)
                    link("masked", nc.vector.tensor_tensor(part_h, part_h, inside[b][:, :].unsqueeze(2).broadcast_to([P, J, H]), ALU.mult))
                dve.wait_ge(done.sem, done.at("score", k - 1))
                here = scores[:, bass.ds(g * J, J), :]
                nc.vector.tensor_tensor(here, here, part[:, :].rearrange("p (j h) -> p j h", j=J), ALU.add).then_inc(done.sem, 1)
            drive_two_ahead(dve, o, front, middle, back)
            dve.wait_ge(done.sem, done.at("score", NB * rounds_of(dve, o) - 1))
            dve.sem_inc(stored, 1)


def segment_softmax(nc, m, o, tag, H, scores, prob, load):
    C = o.edges // P
    with ExitStack() as ctx:
        one = lambda n, s, d=F32: ctx.enter_context(nc.sbuf_tensor(f"{tag}_{n}", s, d))
        sem = lambda n: ctx.enter_context(nc.semaphore(f"{tag}_{n}"))
        key, before, after = one("key", [P, C]), one("before", [P, C]), one("after", [P, C])
        first, last = one("first", [P, C]), one("last", [P, C])
        fence = one("fence", [P, C])
        same_before, same_after = one("same_before", [P, C]), one("same_after", [P, C])
        up, down = one("up", [P, C, H]), one("down", [P, C, H])
        any_first, any_last = one("any_first", [P, 1]), one("any_last", [P, 1])
        row_fence, row_first, row_last = (one(n, [H, P]) for n in ("row_fence", "row_first", "row_last"))
        carried = one("carried", [H, P + 2])
        ends, rows_in, initial = one("ends", [P, H]), one("rows_in", [H, P]), one("initial", [P, H])
        turned = ctx.enter_context(nc.psum_tensor(f"{tag}_turned", [P, 512], F32))
        loaded, stored = sem("loaded"), sem("stored")
        passes = ("max", "max_back", "sum", "sum_back")
        one_scan = lambda s: [f"{s}_own", f"{s}_ends", f"{s}_clear", f"{s}_row", f"{s}_shift", f"{s}_initial", f"{s}_all"]
        dve_s = Chain(sem("dve"), ["first", "same_before", "last", "same_after", "fence", "any_first", "any_last",
                                   "row_fence", "row_first", "row_last"]
                      + one_scan("max") + ["max_at_last"] + one_scan("max_back") + ["arg"]
                      + one_scan("sum") + ["sum_at_last"] + one_scan("sum_back") + ["inverse", "prob"])
        pe_s = Chain(sem("pe"), ["any"] + [f"{s}_{n}" for s in passes for n in ("row", "column")])
        act_s = Chain(sem("act"), ["exp"])
        block = ctx.enter_context(nc.Block())

        @block.sync
        def _(sp):
            for to, shift in ((key, 1), (before, 0), (after, 2)):
                sp.dma_start(to[:, :], o.key_around[shift:shift + o.edges].rearrange("(p c) -> p c", p=P)).then_inc(loaded, 16)
            if load:
                sp.dma_start(scores[:, :, :], prob.rearrange("(p c) h -> p c h", p=P)).then_inc(loaded, 16)
            sp.wait_ge(dve_s.sem, dve_s.at("prob"))
            sp.dma_start(prob.rearrange("(p c) h -> p c h", p=P), scores[:, :, :]).then_inc(stored, 16)
            sp.wait_ge(stored, 16)

        @block.tensor
        def _(pe):
            pe.wait_ge(dve_s.sem, dve_s.at("any_last"))
            nc.tensor.matmul(turned[0:H, 0:P], any_first[:, :].broadcast_to([P, H]), m.ident[:, :], start=True, stop=True)
            nc.tensor.matmul(turned[0:H, P:2 * P], any_last[:, :].broadcast_to([P, H]), m.ident[:, :], start=True, stop=True).then_inc(pe_s.sem, 1)
            for s in passes:
                pe.wait_ge(dve_s.sem, dve_s.at(f"{s}_ends"))
                nc.tensor.transpose(turned[0:H, 0:P], ends[:, :], m.ident[:, :]).then_inc(pe_s.sem, 1)
                pe.wait_ge(dve_s.sem, dve_s.at(f"{s}_shift"))
                nc.tensor.transpose(turned[:, 0:H], rows_in[:, :], m.ident[0:H, 0:H]).then_inc(pe_s.sem, 1)

        @block.scalar
        def _(act):
            act.wait_ge(dve_s.sem, dve_s.at("arg"))
            nc.scalar.activation(scores[:, :, :], scores[:, :, :], ACT.Exp).then_inc(act_s.sem, 1)

        @block.vector
        def _(dve):
            def link(name, ins):
                ins.then_inc(dve_s.sem, 1)
                dve.wait_ge(dve_s.sem, dve_s.at(name))

            def scans(name, out, data0, data1, initial, op0, op1, step):
                for h in range(H):
                    start = initial if isinstance(initial, float) else initial[:, h:h + 1]
                    ins = nc.vector.tensor_tensor_scan(out[:, ::step, h], data0[:, ::step], data1[:, ::step, h], start, op0, op1)
                link(name, ins)

            def scan(s, out, data0, data1, neutral, op0, op1, row, step):
                scans(f"{s}_own", out, data0, data1, neutral, op0, op1, step)
                edge = C - 1 if step > 0 else 0
                link(f"{s}_ends", nc.vector.tensor_copy(ends[:, :], out[:, edge, :]))
                link(f"{s}_clear", nc.vector.memset(carried[:, :], neutral))
                dve.wait_ge(pe_s.sem, pe_s.at(f"{s}_row"))
                link(f"{s}_row", nc.vector.tensor_tensor_scan(carried[:, 1:P + 1][:, ::step], row[:, ::step], turned[0:H, 0:P][:, ::step],
                                                              neutral, op0, op1))
                link(f"{s}_shift", nc.vector.tensor_copy(rows_in[:, :], carried[:, 0:P] if step > 0 else carried[:, 2:P + 2]))
                dve.wait_ge(pe_s.sem, pe_s.at(f"{s}_column"))
                link(f"{s}_initial", nc.vector.tensor_copy(initial[:, :], turned[:, 0:H]))
                scans(f"{s}_all", out, data0, data1, initial, op0, op1, step)

            dve.wait_ge(loaded, 64 if load else 48)
            link("first", nc.vector.tensor_tensor(first[:, :], key[:, :], before[:, :], ALU.not_equal))
            link("same_before", nc.vector.tensor_tensor(same_before[:, :], key[:, :], before[:, :], ALU.is_equal))
            link("last", nc.vector.tensor_tensor(last[:, :], key[:, :], after[:, :], ALU.not_equal))
            link("same_after", nc.vector.tensor_tensor(same_after[:, :], key[:, :], after[:, :], ALU.is_equal))
            link("fence", nc.vector.tensor_scalar(fence[:, :], first[:, :], -BIG, None, ALU.mult))
            link("any_first", nc.vector.tensor_reduce(any_first[:, :], first[:, :], AX.X, ALU.max))
            link("any_last", nc.vector.tensor_reduce(any_last[:, :], last[:, :], AX.X, ALU.max))
            dve.wait_ge(pe_s.sem, pe_s.at("any"))
            link("row_fence", nc.vector.tensor_scalar(row_fence[:, :], turned[0:H, 0:P], -BIG, None, ALU.mult))
            link("row_first", nc.vector.tensor_scalar(row_first[:, :], turned[0:H, 0:P], 0.0, None, ALU.is_equal))
            link("row_last", nc.vector.tensor_scalar(row_last[:, :], turned[0:H, P:2 * P], 0.0, None, ALU.is_equal))
            last_b = last[:, :].unsqueeze(2).broadcast_to([P, C, H])
            scan("max", up, fence, scores, -BIG, ALU.add, ALU.max, row_fence, 1)
            link("max_at_last", nc.vector.tensor_tensor(up[:, :, :], up[:, :, :], last_b, ALU.mult))
            scan("max_back", down, same_after, up, 0.0, ALU.mult, ALU.add, row_last, -1)
            link("arg", nc.vector.tensor_tensor(scores[:, :, :], scores[:, :, :], down[:, :, :], ALU.subtract))
            dve.wait_ge(act_s.sem, act_s.at("exp"))
            scan("sum", up, same_before, scores, 0.0, ALU.mult, ALU.add, row_first, 1)
            link("sum_at_last", nc.vector.tensor_tensor(up[:, :, :], up[:, :, :], last_b, ALU.mult))
            scan("sum_back", down, same_after, up, 0.0, ALU.mult, ALU.add, row_last, -1)
            link("inverse", nc.vector.reciprocal(down[:, :, :], down[:, :, :]))
            link("prob", nc.vector.tensor_tensor(scores[:, :, :], scores[:, :, :], down[:, :, :], ALU.mult))


def attention_probs(nc, m, o, tag, H, C, source, target, prob, att=None):
    in_sbuf = len(target.shape) == 3
    with ExitStack() as ctx:
        if in_sbuf:
            edge_scores_by_window(nc, m, o, f"{tag}s", H, C, source, target, prob, att)
        scores = ctx.enter_context(nc.sbuf_tensor(f"{tag}_scores", [P, o.edges // P, H], F32))
        if not in_sbuf:
            edge_scores(nc, m, o, f"{tag}s", H, C, source, target, scores, att)
        segment_softmax(nc, m, o, f"{tag}m", H, scores, prob, load=in_sbuf)


def norm_stages(t):
    return [f"{t}_stats", f"{t}_moments", f"{t}_eps", f"{t}_rstd", f"{t}_normed"]


def layer_norm(dve, link, act_s, c, t, src, dst, nb, eps):
    for w in range(CW):
        ins = nc_of(dve).vector.bn_stats(nb.stats[:, w, :], src[:, w, :])
    link(f"{t}_stats", ins)
    settle(dve)
    for w in range(CW):
        ins = nc_of(dve).vector.bn_aggr(nb.moments[:, w, :], nb.stats[:, w, :])
    link(f"{t}_moments", ins)
    link(f"{t}_eps", nc_of(dve).vector.tensor_scalar(nb.var[:, :], nb.moments[:, :, 1:2].rearrange("p w a -> p (w a)"), eps, None, ALU.add))
    dve.wait_ge(act_s.sem, act_s.at(f"{t}_std", c))
    link(f"{t}_rstd", nc_of(dve).vector.reciprocal(nb.rstd[:, :], nb.std[:, :]))
    for w in range(CW):
        ins = nc_of(dve).vector.tensor_scalar(dst[:, w, :], src[:, w, :], nb.moments[:, w, 0:1], nb.rstd[:, w:w + 1], ALU.subtract, ALU.mult)
    link(f"{t}_normed", ins)


def nc_of(eng):
    return eng.bass


def standard_deviation(act, dve_s, act_s, c, t, nb):
    act.wait_ge(dve_s.sem, dve_s.at(f"{t}_eps", c))
    nc_of(act).scalar.activation(nb.std[:, :], nb.var[:, :], ACT.Sqrt).then_inc(act_s.sem, 1)


class NormBuffers:
    def __init__(self, one):
        self.stats, self.moments = one("stats", [P, CW, 6]), one("moments", [P, CW, 2])
        self.var, self.std, self.rstd = one("var", [P, CW]), one("std", [P, CW]), one("rstd", [P, CW])


class LinearWeights:
    def __init__(self, one, k, H, C):
        self.sums, self.products = one("w_lin", [P, k, 2 * H]), one("w_lin_products", [P, C])


def over_windows(row, n=CW):
    return row.unsqueeze(1).broadcast_to([P, n, row.shape[-1]])


def project_stages(outs):
    return [f"proj{w}_{o}" for w in range(CW) for o in range(outs)]


def project(pe, pe_s, act_s, c, lhs, weights, bias, ring, ones_row):
    n = 0
    for w in range(CW):
        for o, wt in enumerate(weights):
            width = wt[0].shape[-1]
            to = ring[:, n % 3, 0:width]
            if n >= 3:
                pe.wait_ge(act_s.sem, act_s.at(f"proj{(n - 3) // len(weights)}_{(n - 3) % len(weights)}", c))
            for kc, piece in enumerate(wt):
                mm = nc_of(pe).tensor.matmul(to, lhs(kc, w), piece, start=(kc == 0), stop=(kc == len(wt) - 1 and not bias))
            if bias:
                mm = nc_of(pe).tensor.matmul(to, ones_row, bias[o], start=False, stop=True)
            mm.then_inc(pe_s.sem, 1)
            n += 1


def linear_weights(dve, w_lin, weights, att, H, C, ready):
    for o, wt in enumerate(weights):
        for kc in range(wt.shape[1]):
            for h in range(H):
                n = (o * wt.shape[1] + kc) * H + h
                if n:
                    dve.wait_ge(ready, n)
                nc_of(dve).vector.tensor_tensor_reduce(w_lin.products[:, :], wt[:, kc, h * C:(h + 1) * C], att[:, h * C:(h + 1) * C], SLOPE, 0.0,
                                                       ALU.mult, ALU.add, w_lin.sums[:, kc, o * H + h:o * H + h + 1]).then_inc(ready, 1)


def pieces(weight, k, lo, hi):
    return [weight[:, kc, lo:hi] for kc in range(k)]


def project_linear(pe, pe_s, lhs, w_lin, k, H, turn):
    for w in range(CW):
        for kc in range(k):
            mm = nc_of(pe).tensor.matmul(turn[:, 0, w * 2 * H:(w + 1) * 2 * H], lhs(kc, w), w_lin.sums[:, kc, :], start=(kc == 0), stop=(kc == k - 1))
    mm.then_inc(pe_s.sem, 1)


def keep_linear(act, pe_s, act_s, c, turn, stages, widths, H):
    act.wait_ge(pe_s.sem, pe_s.at("lin", c))
    both = turn[:, 0, 0:CW * 2 * H].rearrange("p (w t h) -> p w t h", w=CW, t=2)
    for o in range(2):
        ins = nc_of(act).scalar.copy(stages[o][:, :, widths[o]:widths[o] + H], both[:, :, o, :])
    ins.then_inc(act_s.sem, 1)


def chunk_rows(table, c):
    return table[bass.ds(c * CW * P, CW * P), :].rearrange("(w p) n -> p w n", p=P)


def nodes_0(nc, m, agg, source, target, att, H, C):
    with ExitStack() as ctx:
        one = lambda n, s, d=F32: ctx.enter_context(nc.sbuf_tensor(f"n0_{n}", s, d))
        sem = lambda n: ctx.enter_context(nc.semaphore(f"n0_{n}"))
        sums = one("sums", [P, CW, D + D_EA64])
        sums_t = one("sums_t", [P, 3 * CW, P])
        h = one("h", [P, CW, D])
        h_t, y = one("h_t", [P, 2, CW * P]), one("y", [P, 2, CW * P])
        x_t = one("x_t", [P, 2 * CW, P])
        stage = [one(f"stage{o}", [P, CW, 512 + H]) for o in range(2)]
        w_lin = LinearWeights(one, 2, H, C)
        nb = NormBuffers(one)
        w_msg, w_edge = one("w_msg", [P, 2, D]), one("w_edge", [D_EA64, D])
        w_mlp = [one(f"w_mlp{l}", [P, 2, D]) for l in range(3)]
        b_mlp = [one(f"b_mlp{l}", [P, 2]) for l in range(3)]
        rows = {n: one(n, [P, D]) for n in ("ln_aggr_scale", "ln_aggr_bias", "ln_out_scale", "ln_out_bias")}
        w_l, w_r = one("w_l", [P, 2, 512]), one("w_r", [P, 2, 512])
        turn = ctx.enter_context(nc.psum_tensor("n0_turn", [P, 16, P], F32))
        mlp_ps = turn[:, :, :].rearrange("p (b t) c -> p b (t c)", b=4)[:, :, 0:CW * P // 2]
        ring = ctx.enter_context(nc.psum_tensor("n0_ring", [P, 3, 512], F32))
        flat = ring[:, :, :].rearrange("p b c -> p (b c)")[:, 0:CW * D].rearrange("p (w c) -> p w c", w=CW)
        weights_in, taken, stored, lin_ready = sem("weights"), sem("taken"), sem("stored"), sem("lin_ready")
        pe_s = Stages(sem("pe"), ["sums_t", "msg", "h_t", "mlp0", "mlp1", "mlp2", "out", "x_t", "lin"] + project_stages(2))
        act_s = Stages(sem("act"), ["sums_t", "a_std", "h_t", "mlp0", "mlp1", "mlp2", "b_std", "c_std", "x_t", "lin"] + project_stages(2))
        dve_s = Stages(sem("dve"), ["h"] + norm_stages("a") + ["a_scale", "a_bias", "skip0", "skip1", "skip2", "r"] + norm_stages("b")
                       + ["b_scale", "b_bias", "xr"] + norm_stages("c") + ["kept"])
        n_weights = 2 + 3 + 6 + 4 + 2
        block = ctx.enter_context(nc.Block())

        @block.sync
        def _(sp):
            load = lambda to, of: sp.dma_start(to, of).then_inc(weights_in, 16)
            load(w_msg[:, :, :], m.inputs["L0_W_message"][0:D, :].rearrange("(k p) n -> p k n", p=P))
            load(w_edge[:, :], m.inputs["L0_W_message"][D:D + D_EA64, :])
            for l in range(3):
                w, bias = [(m.inputs["L0_mlp_W0"], m.inputs["L0_mlp_b0"]), (m.inputs["L0_mlp_W1"], m.inputs["L0_mlp_b1"]), (m.inputs["L0_mlp_W2"], m.inputs["L0_mlp_b2"])][l]
                load(w_mlp[l][:, :, :], w.rearrange("(k p) n -> p k n", p=P))
                for f in range(2):
                    load(b_mlp[l][:, f:f + 1], column(bias[f * P:(f + 1) * P]))
            for name, of in (("ln_aggr_scale", m.inputs["L0_ln_aggr_scale"]), ("ln_aggr_bias", m.inputs["L0_ln_aggr_bias"]),
                             ("ln_out_scale", m.inputs["L0_ln_out_scale"]), ("ln_out_bias", m.inputs["L0_ln_out_bias"])):
                load(rows[name][:, :], row_everywhere(of))
            load(w_l[:, :, :], m.inputs["L1_W1l"].rearrange("(k p) n -> p k n", p=P))
            load(w_r[:, :, :], m.inputs["L1_W1r"].rearrange("(k p) n -> p k n", p=P))
            with sp.Fori(0, CHUNKS) as c:
                sp.wait_ge(pe_s.sem, pe_s.at("sums_t", c - 1))
                sp.dma_start(sums[:, :, :], agg[:, bass.ds(c * CW, CW), :]).then_inc(taken, 16)
                sp.wait_ge(act_s.sem, act_s.at(f"proj{CW - 1}_1", c))
                for table, t in ((source, stage[0]), (target, stage[1])):
                    sp.dma_start(chunk_rows(table, c), t[:, :, :]).then_inc(stored, 16)
            sp.wait_ge(stored, 32 * (CHUNKS + 1))

        @block.tensor
        def _(pe):
            pe.sem_inc(pe_s.sem, pe_s.start)
            pe.wait_ge(weights_in, 16 * n_weights)
            pe.wait_ge(lin_ready, 4 * H)
            with pe.Fori(0, CHUNKS) as c:
                pe.wait_ge(taken, 16 * (c + 1))
                pe.wait_ge(act_s.sem, act_s.at("lin", c - 1))
                for w in range(CW):
                    for kc in range(2):
                        nc.tensor.transpose(turn[:, kc * CW + w, :], sums[:, w, kc * P:(kc + 1) * P], m.ident[:, :])
                    mm = nc.tensor.transpose(turn[0:D_EA64, 2 * CW + w, :], sums[:, w, D:D + D_EA64], m.ident[:, :])
                mm.then_inc(pe_s.sem, 1)
                pe.wait_ge(act_s.sem, act_s.at("sums_t", c))
                pe.wait_ge(act_s.sem, act_s.at(f"proj{CW - 1}_1", c - 1))
                for w in range(CW):
                    nc.tensor.matmul(flat[:, w, :], sums_t[:, w, :], w_msg[:, 0, :], start=True, stop=False)
                    nc.tensor.matmul(flat[:, w, :], sums_t[:, CW + w, :], w_msg[:, 1, :], start=False, stop=False)
                    mm = nc.tensor.matmul(flat[:, w, :], sums_t[0:D_EA64, 2 * CW + w, :], w_edge[:, :], start=False, stop=True)
                mm.then_inc(pe_s.sem, 1)
                pe.wait_ge(dve_s.sem, dve_s.at("a_bias", c))
                for w in range(CW):
                    for kc in range(2):
                        mm = nc.tensor.transpose(turn[:, kc * CW + w, :], h[:, w, kc * P:(kc + 1) * P], m.ident[:, :])
                mm.then_inc(pe_s.sem, 1)
                for l in range(3):
                    pe.wait_ge(act_s.sem, act_s.at("h_t" if l == 0 else f"mlp{l - 1}", c))
                    if l:
                        pe.wait_ge(dve_s.sem, dve_s.at(f"skip{l - 1}", c))
                    for f in range(2):
                        for half in range(2):
                            for kc in range(2):
                                mm = nc.tensor.matmul(mlp_ps[:, 2 * f + half, :], w_mlp[l][:, kc, f * P:(f + 1) * P],
                                                      h_t[:, kc, half * CW * P // 2:(half + 1) * CW * P // 2], start=(kc == 0), stop=(kc == 1))
                    mm.then_inc(pe_s.sem, 1)
                pe.wait_ge(dve_s.sem, dve_s.at("skip2", c))
                for w in range(CW):
                    for kc in range(2):
                        mm = nc.tensor.transpose(flat[:, w, kc * P:(kc + 1) * P], h_t[:, kc, w * P:(w + 1) * P], m.ident[:, :])
                mm.then_inc(pe_s.sem, 1)
                pe.wait_ge(dve_s.sem, dve_s.at("c_normed", c))
                for w in range(CW):
                    for kc in range(2):
                        mm = nc.tensor.transpose(turn[:, kc * CW + w, :], h[:, w, kc * P:(kc + 1) * P], m.ident[:, :])
                mm.then_inc(pe_s.sem, 1)
                pe.wait_ge(act_s.sem, act_s.at("x_t", c))
                project_linear(pe, pe_s, lambda kc, w: x_t[:, kc * CW + w, :], w_lin, 2, H, turn)
                project(pe, pe_s, act_s, c, lambda kc, w: x_t[:, kc * CW + w, :], [pieces(w_l, 2, 0, 512), pieces(w_r, 2, 0, 512)], None, ring, None)

        @block.scalar
        def _(act):
            act.sem_inc(act_s.sem, act_s.start)
            act.sem_inc(stored, 32)
            act.wait_ge(weights_in, 16 * n_weights)
            with act.Fori(0, CHUNKS) as c:
                act.wait_ge(pe_s.sem, pe_s.at("sums_t", c))
                nc.scalar.copy(sums_t[:, 0:2 * CW, :], turn[:, 0:2 * CW, :])
                nc.scalar.copy(sums_t[0:D_EA64, 2 * CW:3 * CW, :], turn[0:D_EA64, 2 * CW:3 * CW, :]).then_inc(act_s.sem, 1)
                standard_deviation(act, dve_s, act_s, c, "a", nb)
                act.wait_ge(pe_s.sem, pe_s.at("h_t", c))
                nc.scalar.copy(h_t[:, :, :].rearrange("p k (w e) -> p (k w) e", e=P), turn[:, 0:2 * CW, :]).then_inc(act_s.sem, 1)
                for l in range(3):
                    act.wait_ge(pe_s.sem, pe_s.at(f"mlp{l}", c))
                    if l:
                        act.wait_ge(dve_s.sem, dve_s.at(f"skip{l - 1}", c))
                    for f in range(2):
                        ins = nc.scalar.activation(y[:, f, :].rearrange("p (b e) -> p b e", b=2), mlp_ps[:, 2 * f:2 * f + 2, :],
                                                   ACT.Relu if l < 2 else ACT.Identity, bias=b_mlp[l][:, f:f + 1])
                    ins.then_inc(act_s.sem, 1)
                standard_deviation(act, dve_s, act_s, c, "b", nb)
                standard_deviation(act, dve_s, act_s, c, "c", nb)
                act.wait_ge(pe_s.sem, pe_s.at("x_t", c))
                nc.scalar.copy(x_t[:, :, :], turn[:, 0:2 * CW, :]).then_inc(act_s.sem, 1)
                act.wait_ge(stored, 32 * (c + 1))
                keep_linear(act, pe_s, act_s, c, turn, stage, (512, 512), H)
                for w in range(CW):
                    act.wait_ge(pe_s.sem, pe_s.at(f"proj{w}_0", c))
                    nc.scalar.copy(stage[0][:, w, 0:512], ring[:, (2 * w) % 3, :]).then_inc(act_s.sem, 1)
                    act.wait_ge(pe_s.sem, pe_s.at(f"proj{w}_1", c))
                    nc.scalar.copy(stage[1][:, w, 0:512], ring[:, (2 * w + 1) % 3, :]).then_inc(act_s.sem, 1)

        @block.vector
        def _(dve):
            dve.sem_inc(dve_s.sem, dve_s.start)
            dve.wait_ge(weights_in, 16 * n_weights)
            linear_weights(dve, w_lin, (w_l, w_r), att, H, C, lin_ready)
            with dve.Fori(0, CHUNKS) as c:
                def link(name, ins):
                    ins.then_inc(dve_s.sem, 1)
                    dve.wait_ge(dve_s.sem, dve_s.at(name, c))

                x = m.xs[:, bass.ds(c * CW, CW), :]
                dve.wait_ge(pe_s.sem, pe_s.at("x_t", c - 1))
                dve.wait_ge(pe_s.sem, pe_s.at("msg", c))
                link("h", nc.vector.scalar_tensor_tensor(h[:, :, :], flat, 0.0, x, ALU.max, ALU.add))
                layer_norm(dve, link, act_s, c, "a", h, h, nb, 1e-6)
                link("a_scale", nc.vector.tensor_tensor(h[:, :, :], h[:, :, :], over_windows(rows["ln_aggr_scale"][:, :]), ALU.mult))
                link("a_bias", nc.vector.tensor_tensor(h[:, :, :], h[:, :, :], over_windows(rows["ln_aggr_bias"][:, :]), ALU.add))
                for l in range(3):
                    dve.wait_ge(act_s.sem, act_s.at(f"mlp{l}", c))
                    link(f"skip{l}", nc.vector.tensor_tensor(h_t[:, :, :], h_t[:, :, :], y[:, :, :], ALU.add))
                dve.wait_ge(pe_s.sem, pe_s.at("out", c))
                link("r", nc.vector.tensor_tensor(h[:, :, :], flat, x, ALU.add))
                layer_norm(dve, link, act_s, c, "b", h, h, nb, 1e-6)
                link("b_scale", nc.vector.tensor_tensor(h[:, :, :], h[:, :, :], over_windows(rows["ln_out_scale"][:, :]), ALU.mult))
                link("b_bias", nc.vector.tensor_tensor(h[:, :, :], h[:, :, :], over_windows(rows["ln_out_bias"][:, :]), ALU.add))
                link("xr", nc.vector.tensor_tensor(h[:, :, :], h[:, :, :], x, ALU.add))
                layer_norm(dve, link, act_s, c, "c", h, h, nb, 1e-5)
                settle(dve)
                link("kept", nc.vector.tensor_copy(x, h[:, :, :]))


def nodes_att(nc, m, tag, total, W, bias, outs, w_out=None, w_in=None, b_in=None, own=None, own_scale=1.0, residual=True,
              next_att=None):
    LH = next_att[1] if next_att else 0
    KI = W // P
    KX = KI if w_in else 4
    PX = P if w_in else C3
    widths = [v.shape[-1] for v in w_in] if w_in else [D, D]
    with ExitStack() as ctx:
        one = lambda n, s, d=F32: ctx.enter_context(nc.sbuf_tensor(f"{tag}_{n}", s, d))
        sem = lambda n: ctx.enter_context(nc.semaphore(f"{tag}_{n}"))
        y = one("y", [P, CW, W])
        x_t = one("x_t", [P, KX * CW, P])
        stage = [one("stage", [P, CW, widths[0] + LH])]
        if next_att:
            w_lin = LinearWeights(one, KI, LH, next_att[2])
        bias_row = one("bias", [P, bias.shape[-1]])
        ones_row = one("ones", [1, P])
        w_sb = [one(f"w{o}", [P, KI, n]) for o, n in enumerate(widths)] if w_in else [one("w3", [C3, 4, 2, C3])]
        b_sb = [one(f"b{o}", [1, n]) for o, n in enumerate(widths)] if b_in else []
        nb = NormBuffers(one)
        if w_out is not None:
            w_o, y_t = one("w_o", [P, KI, D]), one("y_t", [P, KI * CW, P])
        turn = ctx.enter_context(nc.psum_tensor(f"{tag}_turn", [P, 20, P], F32))
        ring = ctx.enter_context(nc.psum_tensor(f"{tag}_ring", [P, 3, 512], F32))
        flat = ring[:, :, :].rearrange("p b c -> p (b c)")[:, 0:CW * D].rearrange("p (w c) -> p w c", w=CW)
        weights_in, stored, ready, lin_ready = sem("weights"), sem("stored"), sem("ready"), sem("lin_ready")
        n_outs = 2 if w_in else 1
        first = ["y_t", "out"] if w_out is not None else []
        pe_s = Stages(sem("pe"), first + ["x_t"] + (["lin"] if next_att else []) + project_stages(n_outs))
        act_s = Stages(sem("act"), first[:1] + (["c_std"] if residual else []) + ["x_t"] + (["lin"] if next_att else []) + project_stages(n_outs))
        dve_s = Stages(sem("dve"), ["taken", "biased"]
                       + (["xr"] + norm_stages("c") + ["kept"] if residual else ["relu"]))
        block = ctx.enter_context(nc.Block())
        n_in = 1 + (2 if w_in else 8) + len(b_sb) + (w_out is not None)

        @block.sync
        def _(sp):
            load = lambda to, of: sp.dma_start(to, of).then_inc(weights_in, 16)
            load(bias_row[:, :], row_everywhere(bias))
            if w_in:
                for o in range(2):
                    load(w_sb[o][:, :, :], w_in[o].rearrange("(k p) n -> p k n", p=P))
            else:
                for i in range(4):
                    load(w_sb[0][:, i, 0, :], m.inputs["L3_W_up1"] if i else m.inputs["L3_W_up0"])
                    load(w_sb[0][:, i, 1, :], m.inputs["L3_Wsc1"] if i else m.inputs["L3_Wsc0"])
            for o, t in enumerate(b_sb):
                load(t[:, :], b_in[o].rearrange("(a n) -> a n", a=1))
            if w_out is not None:
                load(w_o[:, :, :], w_out.rearrange("(k p) n -> p k n", p=P))
            with sp.Fori(0, CHUNKS) as c:
                sp.wait_ge(act_s.sem, act_s.at(f"proj{CW - 1}_{n_outs - 1}", c))
                for table, product, low, high in outs:
                    sp.dma_start(chunk_rows(table, c), stage[product][:, :, low:high]).then_inc(stored, 16)
            sp.wait_ge(stored, 16 * len(outs) * (CHUNKS + 1))

        @block.gpsimd
        def _(pool):
            nc.gpsimd.memset(ones_row[:, :], 1.0).then_inc(ready, 1)

        @block.tensor
        def _(pe):
            pe.sem_inc(pe_s.sem, pe_s.start)
            pe.wait_ge(weights_in, 16 * n_in)
            pe.wait_ge(ready, 1)
            if next_att:
                pe.wait_ge(lin_ready, 2 * KI * LH)
            with pe.Fori(0, CHUNKS) as c:
                if w_out is not None:
                    pe.wait_ge(dve_s.sem, dve_s.at("taken", c))
                    pe.wait_ge(act_s.sem, act_s.at("x_t", c - 1))
                    for w in range(CW):
                        for kc in range(KI):
                            mm = nc.tensor.transpose(turn[:, kc * CW + w, :], y[:, w, kc * P:(kc + 1) * P], m.ident[:, :])
                    mm.then_inc(pe_s.sem, 1)
                    pe.wait_ge(act_s.sem, act_s.at("y_t", c))
                    pe.wait_ge(act_s.sem, act_s.at(f"proj{CW - 1}_{n_outs - 1}", c - 1))
                    for w in range(CW):
                        for kc in range(KI):
                            mm = nc.tensor.matmul(flat[:, w, :], y_t[:, kc * CW + w, :], w_o[:, kc, :], start=(kc == 0), stop=(kc == KI - 1))
                    mm.then_inc(pe_s.sem, 1)
                pe.wait_ge(dve_s.sem, dve_s.at("c_normed" if residual else "relu", c))
                pe.wait_ge(act_s.sem, act_s.at("lin" if next_att else "x_t", c - 1))
                settle(pe)
                for w in range(CW):
                    for kc in range(KX):
                        if w_in:
                            piece = y[:, w, kc * P:(kc + 1) * P]
                        else:
                            piece = y[:, w, 0:C3] if kc == 0 else y[:, w, C3 + kc - 1:D:3]
                        mm = nc.tensor.transpose(turn[0:PX, kc * CW + w, :], piece, m.ident[:, :])
                mm.then_inc(pe_s.sem, 1)
                pe.wait_ge(act_s.sem, act_s.at("x_t", c))
                pe.wait_ge(act_s.sem, act_s.at(f"proj{CW - 1}_{n_outs - 1}", c - 1))
                if next_att:
                    project_linear(pe, pe_s, lambda kc, w: x_t[:, kc * CW + w, :], w_lin, KI, LH, turn)
                if w_in:
                    project(pe, pe_s, act_s, c, lambda kc, w: x_t[:, kc * CW + w, :],
                            [pieces(w_sb[o], KI, 0, widths[o]) for o in range(2)], [b[:, :] for b in b_sb], ring, ones_row[:, :])
                else:
                    for w in range(CW):
                        if w >= 3:
                            pe.wait_ge(act_s.sem, act_s.at(f"proj{w - 3}_0", c))
                        for i in range(4):
                            mm = nc.tensor.matmul(ring[:, w % 3, i * P:(i + 1) * P], x_t[0:C3, i * CW + w, :],
                                                  w_sb[0][:, i, :, :].rearrange("p t c -> p (t c)"), start=True, stop=True)
                        mm.then_inc(pe_s.sem, 1)

        @block.scalar
        def _(act):
            act.sem_inc(act_s.sem, act_s.start)
            act.sem_inc(stored, 16 * len(outs))
            with act.Fori(0, CHUNKS) as c:
                if w_out is not None:
                    act.wait_ge(pe_s.sem, pe_s.at("y_t", c))
                    nc.scalar.copy(y_t[:, :, :], turn[:, 0:KI * CW, :]).then_inc(act_s.sem, 1)
                if residual:
                    standard_deviation(act, dve_s, act_s, c, "c", nb)
                act.wait_ge(pe_s.sem, pe_s.at("x_t", c))
                nc.scalar.copy(x_t[0:PX, :, :], turn[0:PX, 0:KX * CW, :]).then_inc(act_s.sem, 1)
                act.wait_ge(stored, 16 * len(outs) * (c + 1))
                if next_att:
                    keep_linear(act, pe_s, act_s, c, turn, (stage[0], own[:, bass.ds(c * CW, CW), :]), widths, LH)
                for w in range(CW):
                    act.wait_ge(pe_s.sem, pe_s.at(f"proj{w}_0", c))
                    if w_in:
                        nc.scalar.copy(stage[0][:, w, 0:widths[0]], ring[:, (2 * w) % 3, 0:widths[0]]).then_inc(act_s.sem, 1)
                        act.wait_ge(pe_s.sem, pe_s.at(f"proj{w}_1", c))
                        nc.scalar.mul(own[:, bass.ds(c * CW + w, 1), 0:widths[1]].rearrange("p a n -> p (a n)"), ring[:, (2 * w + 1) % 3, 0:widths[1]], own_scale).then_inc(act_s.sem, 1)
                    else:
                        both = ring[:, w % 3, :].rearrange("p (i t c) -> p i t c", i=4, t=2)
                        nc.scalar.copy(stage[0][:, w, :].rearrange("p (i c) -> p i c", i=4), both[:, :, 0, :])
                        to_own = own[:, bass.ds(c * CW + w, 1), :].rearrange("p a n -> p (a n)")
                        nc.scalar.copy(to_own.rearrange("p (i c) -> p i c", i=4), both[:, :, 1, :]).then_inc(act_s.sem, 1)

        @block.vector
        def _(dve):
            dve.sem_inc(dve_s.sem, dve_s.start)
            dve.wait_ge(weights_in, 16 * n_in)
            if next_att:
                linear_weights(dve, w_lin, w_sb, *next_att, lin_ready)
            with dve.Fori(0, CHUNKS) as c:
                def link(name, ins):
                    ins.then_inc(dve_s.sem, 1)
                    dve.wait_ge(dve_s.sem, dve_s.at(name, c))

                dve.wait_ge(pe_s.sem, pe_s.at("x_t", c - 1))
                chunk = total[:, bass.ds(c * CW, CW), :]
                if w_out is not None:
                    settle(dve)
                    link("taken", nc.vector.tensor_copy(y[:, :, :], chunk))
                else:
                    dve.sem_inc(dve_s.sem, 1)
                if w_out is not None:
                    dve.wait_ge(pe_s.sem, pe_s.at("out", c))
                    link("biased", nc.vector.tensor_tensor(y[:, :, :], flat, over_windows(bias_row[:, :]), ALU.add))
                else:
                    link("biased", nc.vector.tensor_tensor(y[:, :, :], chunk, over_windows(bias_row[:, :]), ALU.add))
                if residual:
                    x = m.xs[:, bass.ds(c * CW, CW), :]
                    link("xr", nc.vector.tensor_tensor(y[:, :, :], y[:, :, :], x, ALU.add))
                    layer_norm(dve, link, act_s, c, "c", y, y, nb, 1e-5)
                    settle(dve)
                    link("kept", nc.vector.tensor_copy(x, y[:, :, :]))
                else:
                    link("relu", nc.vector.tensor_scalar(y[:, :, :], y[:, :, :], 0.0, None, ALU.max))


def reload_steps(nc, o):
    with ExitStack() as ctx:
        listed = ctx.enter_context(nc.semaphore("relisted"))
        block = ctx.enter_context(nc.Block())

        @block.sync
        def _(sp):
            sp.dma_start(o.gk[:, :], o.gk_d.rearrange("(a k) -> a k", a=1)).then_inc(listed, 16)
            sp.dma_start(o.wk[:, :], o.wk_d.rearrange("(a k) -> a k", a=1)).then_inc(listed, 16)
            sp.wait_ge(listed, 32)


def edge_messages(nc, m, o, table, total):
    with ExitStack() as ctx:
        one = lambda n, s, d=F32: ctx.enter_context(nc.sbuf_tensor(f"e3_{n}", s, d))
        two = lambda n, s, d=F32: [one(f"{n}{b}", s, d) for b in range(2)]
        bank = lambda n, w=512: ctx.enter_context(nc.psum_tensor(f"e3_{n}", [P, w], F32))
        sem = lambda n: ctx.enter_context(nc.semaphore(f"e3_{n}"))
        many = lambda n, s, d=F32: [one(f"{n}{b}", s, d) for b in range(NB)]
        idx, dst_c = many("idx", [P, J], I32), many("dst_c", [P, J])
        sh, rbf = many("sh", [P, J, 4]), many("rbf", [2 * D_EA16, GE // 2])
        rows = many("rows", [P, J, D])
        rel, hot = many("rel", [P, J]), many("hot", [P, J, P])
        by_sh = two("by_sh", [P, J, 3, C3])
        dot = two("dot", [P, J, C3])
        by_sh0 = two("by_sh0", [P, J, 4, C3])
        scalar_part, x0_part = one("scalar_part", [P, J, C3]), one("x0_part", [P, J, C3])
        vector_part = one("vector_part", [P, J, 3, C3])
        message = many("message", [P, J, 4, C3])
        weights = [one(f"m{l}", [2 * k, 2 * n]) for l, (k, n) in enumerate(((D_EA16, C3), (C3, C3), (C3, C3), (C3, D)))]
        r = [one(f"r{l}", [P, GE // 2]) for l in range(3)]
        z = [bank(f"z{l}") for l in range(2)]
        tp = [bank(f"tp{b}", J * D) for b in range(2)]
        sums = [bank(f"sums{b}") for b in range(2)]
        weights_in, zeroed = sem("weights"), sem("zeroed")
        loaded = [sem(f"loaded{b}") for b in range(NB)]
        gathered = [m.dma_sem(f"e3_gathered{b}") for b in range(NB)]
        pe_f, act_f = Stages(sem("mlp"), ["z0", "z1", "z2", "tp"]), Stages(sem("act"), ["r0", "r1", "r2", "by_sh0"])
        pe_b = Stages(sem("sums"), ["sum"])
        dve_f = Stages(sem("dve_front"), ["rel", "hot", "by_sh", "dot2", "dot"])
        dve_b = Stages(sem("dve_back"), ["tp0", "tp3", "m0", "x0_part", "tp2", "tp1", "m1"])
        merges = Stages(sem("merges"), ["merged"])
        block = ctx.enter_context(nc.Block())

        @block.sync
        def _(sp):
            sp.wait_ge(zeroed, 5)
            for l, to in enumerate(weights):
                of = m.inputs[f"L3_M{l + 1}"]
                rows_of, cols_of = of.shape
                for half in range(2):
                    sp.dma_start(to[half * rows_of:(half + 1) * rows_of, half * cols_of:(half + 1) * cols_of], of).then_inc(weights_in, 16)

            def front(k, i, b):
                g = group_of(sp, o, k)
                part = bass.ds(g * GE, GE)
                sp.wait_ge(dve_b.sem, dve_b.at("m1", k - NB))
                settle(sp)
                sp.wait_ge(pe_f.sem, pe_f.at("z0", k - NB))
                settle(sp)
                sp.dma_start(idx[b][:, :], o.other[part].rearrange("(p j) -> p j", j=J)).then_inc(loaded[b], 16)
                sp.dma_start(dst_c[b][:, :], o.key_f[part].rearrange("(p j) -> p j", j=J)).then_inc(loaded[b], 16)
                sp.dma_start(sh[b][:, :, :], m.inputs["ea4"][part, :].rearrange("(p j) c -> p j c", j=J)).then_inc(loaded[b], 16)
                sp.dma_start(rbf[b][:, :], m.inputs["rbf_t"][bass.ds(g * 2 * D_EA16, 2 * D_EA16), :]).then_inc(loaded[b], 16)
            drive(sp, o, front)

        @block.gpsimd
        def _(pool):
            for t in weights:
                nc.gpsimd.memset(t[:, :], 0.0).then_inc(zeroed, 1)
            nc.gpsimd.memset(total[:, :, :], 0.0).then_inc(zeroed, 1)

            def front(k, i, b):
                pool.wait_ge(loaded[b], 64 * (i + 1))
                settle(pool)
                for j in range(J):
                    pool.indirect_dma_start(
                        out=rows[b][:, j, :], out_offset=None, in_=table,
                        in_offset=bass.IndirectOffsetOnAxis(ap=idx[b][:, j:j + 1], axis=0)).then_inc(gathered[b], 16)
            drive(pool, o, front)

        @block.tensor
        def _(pe):
            for s in (pe_f, pe_b):
                pe.sem_inc(s.sem, s.start)
            pe.wait_ge(weights_in, 8 * 16)

            def sums_of(k, b, tiles):
                if tiles[0] == 0:
                    pe.wait_ge(merges.sem, merges.at("merged", k - 2))
                    pe.wait_ge(dve_b.sem, dve_b.at("m1", k))
                for j in tiles:
                    mm = nc.tensor.matmul(sums[b % 2][:, 0:D], hot[b][:, j, :], message[b][:, j, :, :].rearrange("p t c -> p (t c)"),
                                          start=(j == 0), stop=(j == J - 1))
                if tiles[-1] == J - 1:
                    mm.then_inc(pe_b.sem, 1)

            def front(k, i, b, late=None):
                pe.wait_ge(loaded[b], 64 * (i + 1))
                for l in range(3):
                    pe.wait_ge(act_f.sem, act_f.at(f"r{l - 1}", k) if l else act_f.at("r2", k - 1))
                    settle(pe)
                    nc.tensor.matmul(z[l % 2][:, 0:GE // 2], weights[l][:, :], r[l - 1][:, :] if l else rbf[b][:, :], start=True, stop=True).then_inc(pe_f.sem, 1)
                    if late is not None:
                        sums_of(*late, ((0, 1), (2,), (3,))[l])
                pe.wait_ge(act_f.sem, act_f.at("r2", k))
                pe.wait_ge(dve_b.sem, dve_b.at("tp1", k - 2))
                for c in range(J // 2):
                    mm = nc.tensor.matmul(tp[b % 2][:, c * 2 * D:(c + 1) * 2 * D], r[2][:, c * P:(c + 1) * P], weights[3][:, :], start=True, stop=True)
                mm.then_inc(pe_f.sem, 1)

            rounds = rounds_of(pe, o)
            front(0, 0, 0)
            with pe.Fori(0, rounds) as i:
                for b in range(NB):
                    front(NB * i + b + 1, i + (b + 1) // NB, (b + 1) % NB, (NB * i + b - 1, b - 1) if b else None)
                sums_of(NB * i + NB - 1, NB - 1, range(J))

        @block.scalar
        def _(act):
            act.sem_inc(act_f.sem, act_f.start)

            def front(k, i, b):
                for l in range(3):
                    if l == 0:
                        act.wait_ge(pe_f.sem, pe_f.at("tp", k - 1))
                    act.wait_ge(pe_f.sem, pe_f.at(f"z{l}", k))
                    nc.scalar.activation(r[l][:, :], z[l % 2][:, 0:GE // 2], ACT.Silu).then_inc(act_f.sem, 1)
                act.wait_ge(gathered[b], 16 * J * (i + 1))
                act.wait_ge(loaded[b], 64 * (i + 1))
                act.wait_ge(dve_b.sem, dve_b.at("m1", k - 2))
                settle(act)
                for j in range(J):
                    ins = nc.scalar.activation(by_sh0[b % 2][:, j, :, :].rearrange("p t c -> p (t c)"), rows[b][:, j, :], ACT.Copy, scale=sh[b][:, j, 0:1])
                ins.then_inc(act_f.sem, 1)
            drive(act, o, front, None)

        @block.vector
        def _(dve):
            for s in (dve_f, dve_b, merges):
                dve.sem_inc(s.sem, s.start)
            dve.wait_ge(zeroed, 5)

            def front(k, i, b):
                def link(name, ins):
                    ins.then_inc(dve_f.sem, 1)
                    dve.wait_ge(dve_f.sem, dve_f.at(name, k))

                w = window_of(dve, o, k)
                dve.wait_ge(loaded[b], 64 * (i + 1))
                link("rel", nc.vector.tensor_scalar(rel[b][:, :], dst_c[b][:, :], m.base[:, bass.ds(w, 1)], None, ALU.subtract))
                dve.wait_ge(pe_b.sem, pe_b.at("sum", k - NB))
                for j in range(J):
                    ins = nc.vector.tensor_scalar(hot[b][:, j, :], m.iota[:, :], rel[b][:, j:j + 1], None, ALU.is_equal)
                ins.then_inc(dve_f.sem, 1)
                dve.wait_ge(gathered[b], 16 * J * (i + 1))
                x = rows[b][:, :, :].rearrange("p j (t c) -> p j t c", t=4)
                link("by_sh", nc.vector.tensor_tensor(by_sh[b % 2][:, :, :, :], x[:, :, 1:4, :], sh[b][:, :, 1:4].unsqueeze(3).broadcast_to([P, J, 3, C3]), ALU.mult))
                link("dot2", nc.vector.tensor_tensor(dot[b % 2][:, :, :], by_sh[b % 2][:, :, 0, :], by_sh[b % 2][:, :, 1, :], ALU.add))
                nc.vector.tensor_tensor(dot[b % 2][:, :, :], dot[b % 2][:, :, :], by_sh[b % 2][:, :, 2, :], ALU.add).then_inc(dve_f.sem, 1)

            def products(k, i, b):
                def link(name, ins):
                    ins.then_inc(dve_b.sem, 1)
                    dve.wait_ge(dve_b.sem, dve_b.at(name, k))

                x = rows[b][:, :, :].rearrange("p j (t c) -> p j t c", t=4)
                t = tp[b % 2][:, :].rearrange("p (j t c) -> p j t c", j=J, t=4)
                dve.wait_ge(dve_f.sem, dve_f.at("dot", k))
                dve.wait_ge(act_f.sem, act_f.at("by_sh0", k))
                dve.wait_ge(pe_f.sem, pe_f.at("tp", k))
                dve.wait_ge(pe_b.sem, pe_b.at("sum", k - NB))
                nc.vector.tensor_tensor(message[b][:, :, 0, :], t[:, :, 0, :], by_sh0[b % 2][:, :, 0, :], ALU.mult).then_inc(dve_b.sem, 1)
                link("tp3", nc.vector.scalar_tensor_tensor(scalar_part[:, :, :], t[:, :, 3, :], float(3 ** -0.5), dot[b % 2][:, :, :], ALU.mult, ALU.mult))
                nc.vector.tensor_tensor(message[b][:, :, 0, :], message[b][:, :, 0, :], scalar_part[:, :, :], ALU.add).then_inc(dve_b.sem, 1)
                link("x0_part", nc.vector.tensor_tensor(x0_part[:, :, :], t[:, :, 1, :], x[:, :, 0, :], ALU.mult))
                nc.vector.tensor_tensor(message[b][:, :, 1:4, :], by_sh0[b % 2][:, :, 1:4, :],
                                        t[:, :, 2:3, :].broadcast_to([P, J, 3, C3]), ALU.mult).then_inc(dve_b.sem, 1)
                link("tp1", nc.vector.tensor_tensor(vector_part[:, :, :, :], x0_part[:, :, :].unsqueeze(2).broadcast_to([P, J, 3, C3]),
                                                    sh[b][:, :, 1:4].unsqueeze(3).broadcast_to([P, J, 3, C3]), ALU.mult))
                nc.vector.tensor_tensor(message[b][:, :, 1:4, :], message[b][:, :, 1:4, :], vector_part[:, :, :, :], ALU.add).then_inc(dve_b.sem, 1)

            def merge(k, i, b):
                w = window_of(dve, o, k)
                dve.wait_ge(pe_b.sem, pe_b.at("sum", k))
                dve.wait_ge(merges.sem, merges.at("merged", k - 1))
                a = total[:, bass.ds(w, 1), :].rearrange("p a c -> p (a c)")
                nc.vector.tensor_tensor(a, a, sums[b % 2][:, 0:D], ALU.add).then_inc(merges.sem, 1)
            drive_late(dve, o, front, products, merge)


def nodes_3(nc, m, total, own, out):
    with ExitStack() as ctx:
        one = lambda n, s, d=F32: ctx.enter_context(nc.sbuf_tensor(f"n4_{n}", s, d))
        sem = lambda n: ctx.enter_context(nc.semaphore(f"n4_{n}"))
        rows = {n: one(n, [P, C3]) for n in ("gamma0", "beta0", "gamma1")}
        coef = one("coef", [P, 9, C3])
        w_lin, w_b = one("w_lin", [C3, 4, C3]), one("w_b", [C3, 4, C3])
        weights_in = sem("weights")

        with ExitStack() as first:
            tmp = lambda n, s: first.enter_context(nc.sbuf_tensor(f"n4_{n}", s, F32))
            turned = tmp("turned", [C3, 4 * CW, P])
            a, b = tmp("a", [P, CW, 4, C3]), tmp("b", [P, CW, 4, C3])
            squares = tmp("squares", [P, CW, 3, C3])
            vv, aa, part, poly0, poly1 = (tmp(n, [P, CW, C3]) for n in ("vv", "aa", "part", "poly0", "poly1"))
            turn = first.enter_context(nc.psum_tensor("n4_turn", [P, 20, P], F32))
            ring = first.enter_context(nc.psum_tensor("n4_ring", [P, 1536], F32))
            flat = ring[:, 0:CW * D].rearrange("p (w i c) -> p w i c", w=CW, i=4)
            pe_s = Stages(sem("pe"), ["msg_t", "a", "b_t", "o"])
            act_s = Stages(sem("act"), ["msg", "msg_t", "a", "b_t"])
            steps = ["aa", "sq", "vv2", "vv", "w1", "w0", "w3", "+w3", "w4", "+w4", "poly0", "w2", "b0",
                     "w6", "w5", "w7", "+w7", "w8", "+w8", "b1", "o"]
            dve_s = Stages(sem("dve"), steps)
            block = first.enter_context(nc.Block())

            @block.sync
            def _(sp):
                load = lambda to, of: sp.dma_start(to, of).then_inc(weights_in, 16)
                for n, of in (("gamma0", m.inputs["L3_gamma0"]), ("beta0", m.inputs["L3_beta0"]), ("gamma1", m.inputs["L3_gamma1"])):
                    load(rows[n][:, :], row_everywhere(of))
                load(coef[:, :, :].rearrange("p t c -> p (t c)"), row_everywhere(m.inputs["L3_Wc"]))
                for i in range(4):
                    load(w_lin[:, i, :], m.inputs["L3_W_lin1"] if i else m.inputs["L3_W_lin0"])
                    load(w_b[:, i, :], m.inputs["L3_WB1"] if i else m.inputs["L3_WB0"])
                sp.wait_ge(weights_in, 12 * 16)

            @block.tensor
            def _(pe):
                pe.sem_inc(pe_s.sem, pe_s.start)
                pe.wait_ge(weights_in, 12 * 16)
                with pe.Fori(0, CHUNKS) as c:
                    for phase in range(2):
                        if phase:
                            pe.wait_ge(dve_s.sem, dve_s.at("b1", c))
                        else:
                            pe.wait_ge(act_s.sem, act_s.at("msg", c))
                        settle(pe)
                        for i in range(4):
                            for w in range(CW):
                                mm = nc.tensor.transpose(turn[0:C3, i * CW + w, :], (b if phase else a)[:, w, i, :], m.ident[:, :])
                        mm.then_inc(pe_s.sem, 1)
                        pe.wait_ge(act_s.sem, act_s.at("b_t" if phase else "msg_t", c))
                        if phase == 0:
                            pe.wait_ge(dve_s.sem, dve_s.at("o", c - 1))
                        for w in range(CW):
                            for i in range(4):
                                mm = nc.tensor.matmul(flat[:, w, i, :], turned[:, i * CW + w, :], (w_b if phase else w_lin)[:, i, :], start=True, stop=True)
                        mm.then_inc(pe_s.sem, 1)

            @block.scalar
            def _(act):
                act.sem_inc(act_s.sem, act_s.start)
                with act.Fori(0, CHUNKS) as c:
                    act.wait_ge(dve_s.sem, dve_s.at("b1", c - 1))
                    nc.scalar.copy(a[:, :, :, :].rearrange("p w i c -> p w (i c)"), total[:, bass.ds(c * CW, CW), :]).then_inc(act_s.sem, 1)
                    act.wait_ge(pe_s.sem, pe_s.at("msg_t", c))
                    nc.scalar.copy(turned[:, :, :], turn[0:C3, :, :]).then_inc(act_s.sem, 1)
                    act.wait_ge(pe_s.sem, pe_s.at("a", c))
                    nc.scalar.copy(a[:, :, :, :], flat).then_inc(act_s.sem, 1)
                    act.wait_ge(pe_s.sem, pe_s.at("b_t", c))
                    nc.scalar.copy(turned[:, :, :], turn[0:C3, :, :]).then_inc(act_s.sem, 1)

            @block.vector
            def _(dve):
                dve.sem_inc(dve_s.sem, dve_s.start)
                dve.wait_ge(weights_in, 12 * 16)
                with dve.Fori(0, CHUNKS) as c:
                    def link(name, ins):
                        ins.then_inc(dve_s.sem, 1)
                        dve.wait_ge(dve_s.sem, dve_s.at(name, c))

                    tt = nc.vector.tensor_tensor
                    row = lambda t: over_windows(coef[:, t, :])
                    a0 = a[:, :, 0, :]
                    dve.wait_ge(act_s.sem, act_s.at("a", c))
                    link("aa", tt(aa[:, :, :], a0, a0, ALU.mult))
                    link("sq", tt(squares[:, :, :, :], a[:, :, 1:4, :], a[:, :, 1:4, :], ALU.mult))
                    link("vv2", tt(vv[:, :, :], squares[:, :, 0, :], squares[:, :, 1, :], ALU.add))
                    link("vv", tt(vv[:, :, :], vv[:, :, :], squares[:, :, 2, :], ALU.add))
                    link("w1", tt(poly0[:, :, :], a0, row(1), ALU.mult))
                    link("w0", tt(poly0[:, :, :], poly0[:, :, :], row(0), ALU.add))
                    for name, t, factor in (("w3", 3, aa), ("w4", 4, vv)):
                        link(name, tt(part[:, :, :], factor[:, :, :], row(t), ALU.mult))
                        link("+" + name, tt(poly0[:, :, :], poly0[:, :, :], part[:, :, :], ALU.add))
                    link("poly0", tt(poly0[:, :, :], poly0[:, :, :], a0, ALU.mult))
                    link("w2", tt(part[:, :, :], vv[:, :, :], row(2), ALU.mult))
                    link("b0", tt(b[:, :, 0, :], poly0[:, :, :], part[:, :, :], ALU.add))
                    link("w6", tt(poly1[:, :, :], a0, row(6), ALU.mult))
                    link("w5", tt(poly1[:, :, :], poly1[:, :, :], row(5), ALU.add))
                    for name, t, factor in (("w7", 7, aa), ("w8", 8, vv)):
                        link(name, tt(part[:, :, :], factor[:, :, :], row(t), ALU.mult))
                        link("+" + name, tt(poly1[:, :, :], poly1[:, :, :], part[:, :, :], ALU.add))
                    link("b1", tt(b[:, :, 1:4, :], a[:, :, 1:4, :], poly1[:, :, :].unsqueeze(2).broadcast_to([P, CW, 3, C3]), ALU.mult))
                    dve.wait_ge(pe_s.sem, pe_s.at("o", c))
                    chunk = bass.ds(c * CW, CW)
                    tt(total[:, chunk, :].rearrange("p w (i n) -> p w i n", i=4), flat, own[:, chunk, :].rearrange("p w (i n) -> p w i n", i=4),
                       ALU.add).then_inc(dve_s.sem, 1)

        with ExitStack() as second:
            tmp = lambda n, s: second.enter_context(nc.sbuf_tensor(f"n4_{n}", s, F32))
            ones, real = tmp("ones", [P, P]), tmp("real", [P, P])
            mean, moment = tmp("mean", [P, C3]), tmp("moment", [P, 2, C3])
            root, scale = tmp("root", [P, 2, C3]), tmp("scale", [P, 2, C3])
            squares = tmp("squares_o", [P, CW, D])
            y = [tmp(f"y{i}", [P, CW, D]) for i in range(2)]
            nb = NormBuffers(tmp)
            mean_ps = second.enter_context(nc.psum_tensor("n4_mean_ps", [P, 512], F32))
            square_ps = second.enter_context(nc.psum_tensor("n4_square_ps", [P, 512], F32))
            ready, stat, pe_done, act_done = sem("ready"), sem("stat"), sem("stat_pe"), sem("stat_act")
            squared, used = Stages(sem("squared"), ["centred", "square"]), sem("used")
            stored = sem("stored")
            act_s = Stages(sem("norm_act"), ["c_std"])
            dve_s = Stages(sem("norm_dve"), ["scaled0", "scaled1", "shifted", "xr"] + norm_stages("c"))
            block = second.enter_context(nc.Block())

            @block.sync
            def _(sp):
                def store(c, i):
                    sp.wait_ge(dve_s.sem, dve_s.at("c_normed", c))
                    settle(sp)
                    sp.dma_start(out[bass.ds(c * CW * P, CW * P), :].rearrange("(w p) d -> p w d", p=P), y[i][:, :, :]).then_inc(stored, 16)

                with sp.Fori(0, CHUNKS // 2) as h:
                    for i in range(2):
                        store(2 * h + i, i)
                store(CHUNKS - 1, 0)
                sp.wait_ge(stored, 16 * (CHUNKS + 1))

            @block.gpsimd
            def _(pool):
                nc.gpsimd.memset(ones[:, :], 1.0).then_inc(ready, 1)

            @block.tensor
            def _(pe):
                pe.wait_ge(stat, 1)
                nc.tensor.matmul(mean_ps[:, 0:C3], real[:, :], total[:, WN - 1, 0:C3], start=True, stop=True)
                with pe.Fori(0, WN - 2) as w:
                    nc.tensor.matmul(mean_ps[:, 0:C3], ones[:, :], total[:, bass.ds(w, 1), 0:C3].rearrange("p a c -> p (a c)"),
                                     start=False, stop=True, skip_group_check=True)
                nc.tensor.matmul(mean_ps[:, 0:C3], ones[:, :], total[:, WN - 2, 0:C3], start=False, stop=True, skip_group_check=True).then_inc(pe_done, 1)

                def squares_of(c, first=False, last=False):
                    pe.wait_ge(squared.sem, squared.at("square", c))
                    for w in range(CW):
                        mm = nc.tensor.matmul(square_ps[:, 0:D], (real if last and w == CW - 1 else ones)[:, :], squares[:, w, :],
                                              start=first and w == 0, stop=True, skip_group_check=True)
                    mm.then_inc(used, 1)

                squares_of(0, first=True)
                with pe.Fori(1, CHUNKS - 1) as c:
                    squares_of(c)
                squares_of(CHUNKS - 1, last=True)

            @block.scalar
            def _(act):
                act.sem_inc(act_s.sem, act_s.start)
                act.wait_ge(stat, 5)
                nc.scalar.activation(root[:, :, :], moment[:, :, :], ACT.Sqrt).then_inc(act_done, 1)
                with act.Fori(0, CHUNKS) as c:
                    standard_deviation(act, dve_s, act_s, c, "c", nb)

            @block.vector
            def _(dve):
                n = [0]

                def stage(ins):
                    n[0] += 1
                    ins.then_inc(stat, 1)
                    dve.wait_ge(stat, n[0])

                dve.sem_inc(squared.sem, squared.start)
                dve.sem_inc(dve_s.sem, dve_s.start)
                dve.sem_inc(used, 1)
                dve.sem_inc(stored, 16)
                dve.wait_ge(ready, 1)
                stage(nc.vector.tensor_scalar(real[:, :], m.node[:, 0:1].broadcast_to([P, P]), float(N_NODES - (WN - 1) * P), None, ALU.is_lt))
                dve.wait_ge(pe_done, 1)
                stage(nc.vector.tensor_scalar(mean[:, :], mean_ps[:, 0:C3], 1.0 / N_NODES, None, ALU.mult))
                with dve.Fori(0, CHUNKS) as c:
                    centred = total[:, bass.ds(c * CW, CW), 0:C3]
                    nc.vector.tensor_tensor(centred, centred, over_windows(mean[:, :]), ALU.subtract).then_inc(squared.sem, 1)
                    dve.wait_ge(squared.sem, squared.at("centred", c))
                    dve.wait_ge(used, c + 1)
                    chunk = total[:, bass.ds(c * CW, CW), :]
                    nc.vector.tensor_tensor(squares[:, :, :], chunk, chunk, ALU.mult).then_inc(squared.sem, 1)
                dve.wait_ge(used, CHUNKS + 1)
                eps = 1e-5
                stage(nc.vector.tensor_scalar(moment[:, 0, :], square_ps[:, 0:C3], 1.0 / N_NODES, eps, ALU.mult, ALU.add))
                stage(nc.vector.tensor_reduce(moment[:, 1, :], square_ps[:, C3:D].rearrange("p (x c) -> p c x", x=3), AX.X, ALU.add))
                stage(nc.vector.tensor_scalar(moment[:, 1, :], moment[:, 1, :], 1.0 / (3.0 * N_NODES), eps, ALU.mult, ALU.add))
                dve.wait_ge(act_done, 1)
                stage(nc.vector.reciprocal(scale[:, :, :], root[:, :, :]))
                stage(nc.vector.tensor_tensor(scale[:, 0, :], scale[:, 0, :], rows["gamma0"][:, :], ALU.mult))
                stage(nc.vector.tensor_tensor(scale[:, 1, :], scale[:, 1, :], rows["gamma1"][:, :], ALU.mult))

                def finish(c, i, before):
                    def link(name, ins):
                        ins.then_inc(dve_s.sem, 1)
                        dve.wait_ge(dve_s.sem, dve_s.at(name, c))

                    chunk = bass.ds(c * CW, CW)
                    dve.wait_ge(stored, before)
                    nc.vector.tensor_tensor(y[i][:, :, 0:C3], total[:, chunk, 0:C3], over_windows(scale[:, 0, :]), ALU.mult).then_inc(dve_s.sem, 1)
                    link("scaled1", nc.vector.tensor_tensor(y[i][:, :, C3:D].rearrange("p w (c x) -> p w x c", x=3),
                                                            total[:, chunk, C3:D].rearrange("p w (x c) -> p w x c", x=3),
                                                            scale[:, 1:2, :].unsqueeze(1).broadcast_to([P, CW, 3, C3]), ALU.mult))
                    link("shifted", nc.vector.tensor_tensor(y[i][:, :, 0:C3], y[i][:, :, 0:C3], over_windows(rows["beta0"][:, :]), ALU.add))
                    link("xr", nc.vector.tensor_tensor(y[i][:, :, :], y[i][:, :, :], m.xs[:, chunk, :], ALU.add))
                    layer_norm(dve, link, act_s, c, "c", y[i], y[i], nb, 1e-5)

                with dve.Fori(0, CHUNKS // 2) as h:
                    for i in range(2):
                        finish(2 * h + i, i, 16 * 2 * h + 16)
                finish(CHUNKS - 1, 0, 16 * CHUNKS)
def build(nc, a, out):
    m = Model(a)
    dram = lambda n, s, d=F32: nc.dram_tensor(n, s, d, kind="Internal").ap()
    as_given = Order(dram, "as_given", NG, a["dst"], a["src"])
    by_dst, by_row = Sorted(dram, "by_dst", NGS, a["pairs_by_dst"]), Sorted(dram, "by_row", NG, a["pairs_by_row"])
    source_1, target_1 = dram("source_1", (NP, 512 + 4)), dram("target_1", (NP + P, 512 + 4))
    source_2 = dram("source_2", (NP, 256 + 1))
    table_k, table_v = dram("table_k", (NP, 256)), dram("table_v", (NP, 256))
    table_up = dram("table_up", (NP, 256))
    prob_1, prob_2, prob_3 = dram("prob_1", (EPS, 4)), dram("prob_2", (EPS, 1)), dram("prob_3", (EP, 8))
    with ExitStack() as ctx:
        sb = lambda n, s, d=F32: ctx.enter_context(nc.sbuf_tensor(n, s, d))
        m.dma_sem = lambda n: ctx.enter_context(nc.semaphore(n))
        m.ident, m.iota = sb("ident", [P, P]), sb("iota", [P, P])
        m.node, m.base, m.end = sb("node", [P, WX]), sb("base", [P, WX]), sb("end", [P, WX])
        gk, wk = sb("gk", [1, KMAX], I32), sb("wk", [1, KMAX], I32)
        for n, o in (("as_given", as_given), ("by_dst", by_dst), ("by_row", by_row)):
            o.gk, o.wk, o.rounds = gk, wk, sb(f"{n}_rounds", [1, 1], I32)
        att = {"a1": sb("att1", [P, 512]), "a2": sb("att2", [P, 256])}
        build_steps(nc, m, as_given, "d_")
        m.xs = sb("xs", [P, WN, D])
        load_nodes(nc, m, att, (target_1,))
        own_wide = sb("own", [P, WX, D + 1])
        own = own_wide[:, :, 0:D]
        with ExitStack() as life:
            agg = life.enter_context(nc.sbuf_tensor("agg", [P, WX, D + D_EA64], F32))
            edge_sums(nc, m, as_given, "e0", a["x"], D, agg, attr=a["ea64"])
            nodes_0(nc, m, agg, source_1, target_1, att["a1"], 4, 128)
        sort_edges(nc, m, by_dst, "sd")
        build_steps(nc, m, by_dst, "s_")
        attention_probs(nc, m, by_dst, "a1", 4, 128, source_1, target_1, prob_1, att["a1"])
        with ExitStack() as life:
            total = life.enter_context(nc.sbuf_tensor("total_1", [P, WX, 512], F32))
            edge_sums(nc, m, by_dst, "a1v", source_1, 512, total, prob=prob_1, H=4)
            nodes_att(nc, m, "n1", total, 512, a["L1_b1"], [(source_2, 0, 0, 257)], own=own_wide,
                      w_in=(a["L1_W2l"], a["L1_W2r"]), residual=False, next_att=(att["a2"], 1, 256))
        total = sb("total", [P, WX, D])
        attention_probs(nc, m, by_dst, "a2", 1, 256, source_2, own_wide, prob_2, att["a2"])
        edge_sums(nc, m, by_dst, "a2v", source_2, 256, total, prob=prob_2)
        nodes_att(nc, m, "n2", total, 256, a["L1_b2"], [(table_k, 0, 0, 256), (table_v, 0, 256, 512)], own=own,
                  w_in=(a["L2_Wkv"], a["L2_Wq"]), b_in=(a["L2_bkv"], a["L2_bq"]), own_scale=float(32 ** -0.5))
        clear_semaphores(nc)
        sort_edges(nc, m, by_row, "sr")
        build_steps(nc, m, by_row, "r_")
        attention_probs(nc, m, by_row, "a3", 8, 32, table_k, own, prob_3)
        edge_sums(nc, m, by_row, "a3v", table_v, 256, total, prob=prob_3, H=8)
        nodes_att(nc, m, "n3", total, 256, a["L2_bo"], [(table_up, 0, 0, 256)], w_out=a["L2_Wo"], own=own)
        reload_steps(nc, as_given)
        edge_messages(nc, m, as_given, table_up, total)
        nodes_3(nc, m, total, own, out)


def clear_semaphores(nc):
    done = sorted(nc.released_uncleared_semaphores)
    nc.gpsimd.sem_clear(range(done[0], done[-1] + 1))
    nc.all_engine_barrier()


def load_nodes(nc, m, att, targets):
    with ExitStack() as ctx:
        loaded, zeroed = ctx.enter_context(nc.semaphore("x_loaded")), ctx.enter_context(nc.semaphore("x_zeroed"))
        zeros = ctx.enter_context(nc.sbuf_tensor("x_zeros", [P, 516], F32))
        block = ctx.enter_context(nc.Block())

        @block.sync
        def _(sp):
            sp.dma_start(m.xs[:, :, :], m.inputs["x"].rearrange("(w p) d -> p w d", p=P)).then_inc(loaded, 16)
            sp.dma_start(att["a1"][:, :], row_everywhere(m.inputs["L1_a1"])).then_inc(loaded, 16)
            sp.dma_start(att["a2"][:, :], row_everywhere(m.inputs["L1_a2"])).then_inc(loaded, 16)
            sp.wait_ge(zeroed, 1)
            for t in targets:
                sp.dma_start(t[NP:NP + P, :], zeros[:, 0:t.shape[-1]]).then_inc(loaded, 16)
            sp.wait_ge(loaded, 16 * (3 + len(targets)))

        @block.gpsimd
        def _(pool):
            nc.gpsimd.memset(zeros[:, :], 0.0).then_inc(zeroed, 1)


def kernel(**inputs):
    import numpy as _np
    import concourse.bacc as _bacc
    from concourse.bass_utils import run_bass_kernel_spmd as _run

    raw = {k: _np.asarray(v) for k, v in inputs.items()}
    edges = EP - N_EDGES
    loop = _np.arange(N_NODES, dtype=raw["src"].dtype)
    rbf = _np.pad(raw["edge_attr_16"], ((0, edges), (0, 0)))
    arrays = {
        "x": _np.pad(raw["x"], ((0, NP - N_NODES), (0, 0))),
        "src": _np.pad(raw["src"], (0, edges)),
        "dst": _np.pad(raw["dst"], (0, edges), constant_values=NP),
        "pairs_by_row": _np.stack([_np.pad(raw["src"], (0, edges), constant_values=NP), _np.pad(raw["dst"], (0, edges))], axis=1),
        "pairs_by_dst": _np.stack([_np.concatenate([raw["dst"], loop, _np.full(EPS - ES, NP, loop.dtype)]),
                                   _np.concatenate([raw["src"], loop, _np.zeros(EPS - ES, loop.dtype)])], axis=1),
        "ea64": _np.pad(raw["edge_attr_64"], ((0, edges), (0, 0))),
        "ea4": _np.pad(raw["edge_attr_4"], ((0, edges), (0, 0))),
        "rbf_t": _np.ascontiguousarray(rbf.reshape(NG, P, J // 2, 2, D_EA16).transpose(0, 3, 4, 2, 1)).reshape(NG * 2 * D_EA16, GE // 2),
        "L1_a1": raw["L1_gnn_a1"].reshape(-1), "L1_a2": raw["L1_gnn_a2"].reshape(-1),
        "L2_Wkv": _np.concatenate([raw["L2_gnn_Wk"], raw["L2_gnn_Wv"]], axis=1),
        "L2_bkv": _np.concatenate([raw["L2_gnn_bk"], raw["L2_gnn_bv"]]),
        "L3_Wc": _np.ascontiguousarray(_np.concatenate([raw["L3_gnn_Wc0"], raw["L3_gnn_Wc1"]], axis=1).T).reshape(-1),
    }
    taken = {"L1_gnn_a1", "L1_gnn_a2", "L2_gnn_Wk", "L2_gnn_Wv", "L2_gnn_bk", "L2_gnn_bv", "L3_gnn_Wc0", "L3_gnn_Wc1"}
    arrays.update({k.replace("_gnn", ""): _np.ascontiguousarray(v) for k, v in raw.items() if "_gnn_" in k and k not in taken})
    nc = _bacc.Bacc("TRN2", target_bir_lowering=False, num_devices=1)
    args = {n: nc.dram_tensor(f"in_{n}", v.shape, mybir.dt.from_np(v.dtype), kind="ExternalInput").ap() for n, v in arrays.items()}
    out = nc.dram_tensor("out_0", (NP, D), F32, kind="ExternalOutput").ap()
    build(nc, args, out)
    r = _run(nc, [{f"in_{n}": v for n, v in arrays.items()}], core_ids=[0])
    return r.results[0]["out_0"][:N_NODES]
```
